# Optimizing a Trainium2 kernel written in Bass

```python
import numpy as np
import jax
import jax.numpy as jnp

def _softmax(x, axis=-1):
    return jax.nn.softmax(x, axis=axis)

def _gelu(x):
    return jax.nn.gelu(x, approximate=True)

def _silu(x):
    return jax.nn.silu(x)

def _sigmoid(x):
    return jax.nn.sigmoid(x)

def _layernorm(x, axis=-1, eps=1e-05):
    m = jnp.mean(x, axis=axis, keepdims=True)
    v = jnp.var(x, axis=axis, keepdims=True)
    return (x - m) / jnp.sqrt(v + eps)

def _scatter_add(tgt, idx, src, axis=0):
    return tgt.at[idx].add(src)

def _segment_sum(src, seg, n):
    return jax.ops.segment_sum(src, seg, n)
kernel_name = 'mk_audio_tower_d2_tok_audfeat768_r4_95d6b6'

def setup_inputs(seed: int=0):
    np.random.seed(seed)
    _w = jnp.asarray

    def _rec_inputs():
        import jax
        import jax.numpy as jnp
        _rk = jax.random.key(seed)
        x = -0.000222058 + 0.999998 * jax.random.normal(jax.random.fold_in(_rk, 1), (128, 125, 192), jnp.float32)
        return x
    x = _rec_inputs()

    def _L0_tok_setup():
        import jax, jax.numpy as jnp
        import numpy as np
        B, S, D, K = (8, 1024, 192, 7)
        EPS = 1e-05
        key = jax.random.key(seed)
        k0, k1, k2, k3, k4 = jax.random.split(key, 5)
        return {'x': jax.random.normal(k0, (B, S, D), jnp.float32), 'w_dw': jax.random.normal(k1, (D, 1, K), jnp.float32) * 0.2, 'b_dw': jax.random.normal(k2, (D,), jnp.float32) * 0.02, 'w_pw': jax.random.normal(k3, (D, D, 1), jnp.float32) * 0.03, 'b_pw': jax.random.normal(k4, (D,), jnp.float32) * 0.02, 'gamma': jnp.ones((D,), jnp.float32), 'beta': jnp.zeros((D,), jnp.float32)}
    _L0_tok_all = _L0_tok_setup()
    _L0_tok_in = {k: v for k, v in _L0_tok_all.items() if k in ('w_dw', 'b_dw', 'w_pw', 'b_pw', 'gamma', 'beta')}
    del _L0_tok_all

    def _L0_attn_setup():
        import jax, jax.numpy as jnp
        import numpy as np
        N_HEAD = 12
        key = jax.random.key(seed)
        ks = jax.random.split(key, 5)
        B, T, C = (8, 256, 192)
        s = 0.02
        return {'x': jax.random.normal(ks[0], (B, T, C), dtype=jnp.float32), 'w_attn': jax.random.normal(ks[1], (C, 3 * C), dtype=jnp.float32) * s, 'b_attn': jax.random.normal(ks[2], (3 * C,), dtype=jnp.float32) * s, 'w_proj': jax.random.normal(ks[3], (C, C), dtype=jnp.float32) * s, 'b_proj': jax.random.normal(ks[4], (C,), dtype=jnp.float32) * s}
    _L0_attn_all = _L0_attn_setup()
    _L0_attn_in = {k: v for k, v in _L0_attn_all.items() if k in ('w_attn', 'b_attn', 'w_proj', 'b_proj')}
    del _L0_attn_all

    def _L0_ffn_setup():
        import jax, jax.numpy as jnp
        import numpy as np
        B, S, H = (2, 256, 192)
        E, K, I = (16, 4, 192)
        ALPHA, LIMIT, EPS = (1.702, 7.0, 1e-05)

        def _swiglu(h):
            x_glu, x_lin = jnp.split(h, 2, axis=-1)
            x_glu = jnp.minimum(x_glu, LIMIT)
            x_lin = jnp.clip(x_lin, -LIMIT, LIMIT)
            return x_glu * jax.nn.sigmoid(ALPHA * x_glu) * (x_lin + 1.0)
        key = jax.random.key(seed)
        ks = jax.random.split(key, 7)
        x = jax.random.normal(ks[0], (B, S, H), dtype=jnp.float32)
        scale = jnp.ones((H,), jnp.float32)
        gate_w = jax.random.normal(ks[1], (E, H), jnp.float32) * 0.02
        gate_b = jnp.zeros((E,), jnp.float32)
        w1 = jax.random.normal(ks[2], (E, H, 2 * I), jnp.float32) * 0.02
        b1 = jax.random.normal(ks[3], (E, 2 * I), jnp.float32) * 0.02
        w2 = jax.random.normal(ks[4], (E, I, H), jnp.float32) * 0.02
        b2 = jax.random.normal(ks[5], (E, H), jnp.float32) * 0.02
        return {'x': x, 'scale': scale, 'gate_w': gate_w, 'gate_b': gate_b, 'w1': w1, 'b1': b1, 'w2': w2, 'b2': b2}
    _L0_ffn_all = _L0_ffn_setup()
    _L0_ffn_in = {k: v for k, v in _L0_ffn_all.items() if k in ('scale', 'gate_w', 'gate_b', 'w1', 'b1', 'w2', 'b2')}
    del _L0_ffn_all

    def _L1_attn_setup():
        import jax, jax.numpy as jnp
        import numpy as np
        EPS = 1e-05
        B, T, C = (8, 512, 192)
        H = 4 * C
        LAYER_ID, N_LAYER = (4, 12)

        def _ln(x, w, b):
            mu = x.mean(-1, keepdims=True)
            var = ((x - mu) ** 2).mean(-1, keepdims=True)
            return (x - mu) / jnp.sqrt(var + EPS) * w + b

        def _wkv_scan(w, k, v):
            a0 = jnp.zeros(k.shape[1:], k.dtype)
            b0 = jnp.zeros_like(a0)
            m0 = jnp.full_like(a0, -1e+38)

            def step(carry, kv):
                a, b, m = carry
                kt, vt = kv
                mm = jnp.maximum(m + w, kt)
                e1 = jnp.exp(m + w - mm)
                e2 = jnp.exp(kt - mm)
                return ((e1 * a + e2 * vt, e1 * b + e2, mm), (a, b, m))
            _, (A, Bd, M) = jax.lax.scan(step, (a0, b0, m0), (k, v))
            return (A, Bd, M)

        def bi_wkv(w, u, k, v):
            kt = jnp.swapaxes(k, 0, 1)
            vt = jnp.swapaxes(v, 0, 1)
            af, bf, mf = _wkv_scan(w, kt, vt)
            ab, bb, mb = _wkv_scan(w, kt[::-1], vt[::-1])
            ab, bb, mb = (ab[::-1], bb[::-1], mb[::-1])
            kk = kt + u
            M = jnp.maximum(jnp.maximum(mf, mb), kk)
            ef = jnp.exp(mf - M)
            eb = jnp.exp(mb - M)
            ec = jnp.exp(kk - M)
            y = (ef * af + eb * ab + ec * vt) / (ef * bf + eb * bb + ec)
            return jnp.swapaxes(y, 0, 1)
        key = jax.random.key(seed)
        ks = jax.random.split(key, 9)
        x = jax.random.normal(ks[0], (B, T, C), jnp.float32)
        r01 = LAYER_ID / (N_LAYER - 1)
        h = np.arange(C, dtype=np.float64)
        decay = (-5.0 + 8.0 * (h / (C - 1)) ** (0.7 + 1.3 * r01)).astype(np.float32)
        zigzag = ((np.arange(C) + 1) % 3 - 1).astype(np.float32) * 0.5
        first = (np.float32(np.log(0.3)) + zigzag).astype(np.float32)
        s = 0.02
        return {'x': x, 'ln1_w': jnp.ones((C,), jnp.float32), 'ln1_b': jnp.zeros((C,), jnp.float32), 'ln2_w': jnp.ones((C,), jnp.float32), 'ln2_b': jnp.zeros((C,), jnp.float32), 'decay': jnp.asarray(decay), 'first': jnp.asarray(first), 'Wk_a': s * jax.random.normal(ks[1], (C, C), jnp.float32), 'Wv_a': s * jax.random.normal(ks[2], (C, C), jnp.float32), 'Wr_a': s * jax.random.normal(ks[3], (C, C), jnp.float32), 'Wo_a': s * jax.random.normal(ks[4], (C, C), jnp.float32), 'Wk_f': s * jax.random.normal(ks[5], (H, C), jnp.float32), 'Wv_f': s * jax.random.normal(ks[6], (C, H), jnp.float32), 'Wr_f': s * jax.random.normal(ks[7], (C, C), jnp.float32)}
    _L1_attn_all = _L1_attn_setup()
    _L1_attn_in = {k: v for k, v in _L1_attn_all.items() if k in ('ln1_w', 'ln1_b', 'ln2_w', 'ln2_b', 'decay', 'first', 'Wk_a', 'Wv_a', 'Wr_a', 'Wo_a', 'Wk_f', 'Wv_f', 'Wr_f')}
    del _L1_attn_all

    def _L1_ffn_setup():
        import jax, jax.numpy as jnp
        import numpy as np
        B, T, E = (2, 256, 192)
        H = 768
        N_EXP = 4
        key = jax.random.key(seed)
        ks = jax.random.split(key, 8)
        s_e = 1.0 / np.sqrt(E)
        s_h = 1.0 / np.sqrt(H)
        return {'x': jax.random.normal(ks[0], (B, T, E), dtype=jnp.float32), 'Wg': jax.random.uniform(ks[1], (E, N_EXP), minval=-s_e, maxval=s_e, dtype=jnp.float32), 'bg': jax.random.uniform(ks[2], (N_EXP,), minval=-s_e, maxval=s_e, dtype=jnp.float32), 'W1': jax.random.uniform(ks[3], (N_EXP, E, H), minval=-s_e, maxval=s_e, dtype=jnp.float32), 'b1': jax.random.uniform(ks[4], (N_EXP, H), minval=-s_e, maxval=s_e, dtype=jnp.float32), 'W2': jax.random.uniform(ks[5], (N_EXP, H, E), minval=-s_h, maxval=s_h, dtype=jnp.float32), 'b2': jax.random.uniform(ks[6], (N_EXP, E), minval=-s_h, maxval=s_h, dtype=jnp.float32)}
    _L1_ffn_all = _L1_ffn_setup()
    _L1_ffn_in = {k: v for k, v in _L1_ffn_all.items() if k in ('Wg', 'bg', 'W1', 'b1', 'W2', 'b2')}
    del _L1_ffn_all
    return {'x': x, 'L0_tok_w_dw': _L0_tok_in['w_dw'], 'L0_tok_b_dw': _L0_tok_in['b_dw'], 'L0_tok_w_pw': _L0_tok_in['w_pw'], 'L0_tok_b_pw': _L0_tok_in['b_pw'], 'L0_tok_gamma': _L0_tok_in['gamma'], 'L0_tok_beta': _L0_tok_in['beta'], 'L0_attn_w_attn': _L0_attn_in['w_attn'], 'L0_attn_b_attn': _L0_attn_in['b_attn'], 'L0_attn_w_proj': _L0_attn_in['w_proj'], 'L0_attn_b_proj': _L0_attn_in['b_proj'], 'L0_ffn_scale': _L0_ffn_in['scale'], 'L0_ffn_gate_w': _L0_ffn_in['gate_w'], 'L0_ffn_gate_b': _L0_ffn_in['gate_b'], 'L0_ffn_w1': _L0_ffn_in['w1'], 'L0_ffn_b1': _L0_ffn_in['b1'], 'L0_ffn_w2': _L0_ffn_in['w2'], 'L0_ffn_b2': _L0_ffn_in['b2'], 'L1_attn_ln1_w': _L1_attn_in['ln1_w'], 'L1_attn_ln1_b': _L1_attn_in['ln1_b'], 'L1_attn_ln2_w': _L1_attn_in['ln2_w'], 'L1_attn_ln2_b': _L1_attn_in['ln2_b'], 'L1_attn_decay': _L1_attn_in['decay'], 'L1_attn_first': _L1_attn_in['first'], 'L1_attn_Wk_a': _L1_attn_in['Wk_a'], 'L1_attn_Wv_a': _L1_attn_in['Wv_a'], 'L1_attn_Wr_a': _L1_attn_in['Wr_a'], 'L1_attn_Wo_a': _L1_attn_in['Wo_a'], 'L1_attn_Wk_f': _L1_attn_in['Wk_f'], 'L1_attn_Wv_f': _L1_attn_in['Wv_f'], 'L1_attn_Wr_f': _L1_attn_in['Wr_f'], 'L1_ffn_Wg': _L1_ffn_in['Wg'], 'L1_ffn_bg': _L1_ffn_in['bg'], 'L1_ffn_W1': _L1_ffn_in['W1'], 'L1_ffn_b1': _L1_ffn_in['b1'], 'L1_ffn_W2': _L1_ffn_in['W2'], 'L1_ffn_b2': _L1_ffn_in['b2']}

def reference(x, L0_tok_w_dw, L0_tok_b_dw, L0_tok_w_pw, L0_tok_b_pw, L0_tok_gamma, L0_tok_beta, L0_attn_w_attn, L0_attn_b_attn, L0_attn_w_proj, L0_attn_b_proj, L0_ffn_scale, L0_ffn_gate_w, L0_ffn_gate_b, L0_ffn_w1, L0_ffn_b1, L0_ffn_w2, L0_ffn_b2, L1_attn_ln1_w, L1_attn_ln1_b, L1_attn_ln2_w, L1_attn_ln2_b, L1_attn_decay, L1_attn_first, L1_attn_Wk_a, L1_attn_Wv_a, L1_attn_Wr_a, L1_attn_Wo_a, L1_attn_Wk_f, L1_attn_Wv_f, L1_attn_Wr_f, L1_ffn_Wg, L1_ffn_bg, L1_ffn_W1, L1_ffn_b1, L1_ffn_W2, L1_ffn_b2):
    import jax
    import jax.numpy as jnp

    def _L0_tok_ref(x, w_dw, b_dw, w_pw, b_pw, gamma, beta):
        import jax, jax.numpy as jnp
        import numpy as np
        B, S, D, K = (8, 1024, 192, 7)
        EPS = 1e-05
        d = w_dw.shape[0]
        h = jnp.transpose(x, (0, 2, 1))
        h = jax.lax.conv_general_dilated(h, w_dw, window_strides=(1,), padding='SAME', dimension_numbers=('NCH', 'OIH', 'NCH'), feature_group_count=d) + b_dw[None, :, None]
        h = jnp.einsum('od,bds->bos', w_pw[:, :, 0], h) + b_pw[None, :, None]
        h = jax.nn.relu(h)
        h = jax.lax.reduce_window(h, -jnp.inf, jax.lax.max, (1, 1, 2), (1, 1, 2), 'VALID')
        h = jnp.transpose(h, (0, 2, 1))
        y = jnp.real(jnp.fft.fft2(h))
        mu = jnp.mean(y, axis=-1, keepdims=True)
        var = jnp.var(y, axis=-1, keepdims=True)
        return (y - mu) * jax.lax.rsqrt(var + EPS) * gamma + beta

    def _L0_attn_ref(x, w_attn, b_attn, w_proj, b_proj):
        import jax, jax.numpy as jnp
        import numpy as np
        N_HEAD = 12
        B, T, C = x.shape
        H, D = (N_HEAD, C // N_HEAD)
        qkv = x @ w_attn + b_attn
        q, k, v = jnp.split(qkv, 3, axis=-1)
        q = q.reshape(B, T, H, D)
        k = k.reshape(B, T, H, D)
        v = v.reshape(B, T, H, D)
        wei = jnp.einsum('bthd,bshd->bhts', q, k)
        causal = jnp.tril(jnp.ones((T, T), dtype=bool))
        wei = jnp.where(causal[None, None], wei, -jnp.inf)
        wei = jax.nn.softmax(wei, axis=-1)
        out = jnp.einsum('bhts,bshd->bthd', wei, v)
        out = out.reshape(B, T, C)
        return out @ w_proj + b_proj

    def _L0_ffn_ref(x, scale, gate_w, gate_b, w1, b1, w2, b2):
        import jax, jax.numpy as jnp
        import numpy as np
        B, S, H = (2, 256, 192)
        E, K, I = (16, 4, 192)
        ALPHA, LIMIT, EPS = (1.702, 7.0, 1e-05)

        def _swiglu(h):
            x_glu, x_lin = jnp.split(h, 2, axis=-1)
            x_glu = jnp.minimum(x_glu, LIMIT)
            x_lin = jnp.clip(x_lin, -LIMIT, LIMIT)
            return x_glu * jax.nn.sigmoid(ALPHA * x_glu) * (x_lin + 1.0)
        Bx, Sx, Hx = x.shape
        xf = x.astype(jnp.float32)
        t = xf * jax.lax.rsqrt(jnp.mean(xf * xf, axis=-1, keepdims=True) + EPS) * scale
        t = t.reshape(-1, Hx)
        T = t.shape[0]
        g = t @ gate_w.T + gate_b
        vals, idx = jax.lax.top_k(g, K)
        w = jax.nn.softmax(vals, axis=-1) / K
        full_w = jnp.zeros((T, E), jnp.float32).at[jnp.arange(T)[:, None], idx].set(w)
        h = jnp.einsum('th,ehf->tef', t, w1) + b1
        h = _swiglu(h)
        y = jnp.einsum('tei,eih->teh', h, w2) + b2
        out = jnp.einsum('teh,te->th', y, full_w) * K
        return x + out.astype(x.dtype).reshape(Bx, Sx, Hx)

    def _L1_attn_ref(x, ln1_w, ln1_b, ln2_w, ln2_b, decay, first, Wk_a, Wv_a, Wr_a, Wo_a, Wk_f, Wv_f, Wr_f):
        import jax, jax.numpy as jnp
        import numpy as np
        EPS = 1e-05
        B, T, C = (8, 512, 192)
        H = 4 * C
        LAYER_ID, N_LAYER = (4, 12)

        def _ln(x, w, b):
            mu = x.mean(-1, keepdims=True)
            var = ((x - mu) ** 2).mean(-1, keepdims=True)
            return (x - mu) / jnp.sqrt(var + EPS) * w + b

        def _wkv_scan(w, k, v):
            a0 = jnp.zeros(k.shape[1:], k.dtype)
            b0 = jnp.zeros_like(a0)
            m0 = jnp.full_like(a0, -1e+38)

            def step(carry, kv):
                a, b, m = carry
                kt, vt = kv
                mm = jnp.maximum(m + w, kt)
                e1 = jnp.exp(m + w - mm)
                e2 = jnp.exp(kt - mm)
                return ((e1 * a + e2 * vt, e1 * b + e2, mm), (a, b, m))
            _, (A, Bd, M) = jax.lax.scan(step, (a0, b0, m0), (k, v))
            return (A, Bd, M)

        def bi_wkv(w, u, k, v):
            kt = jnp.swapaxes(k, 0, 1)
            vt = jnp.swapaxes(v, 0, 1)
            af, bf, mf = _wkv_scan(w, kt, vt)
            ab, bb, mb = _wkv_scan(w, kt[::-1], vt[::-1])
            ab, bb, mb = (ab[::-1], bb[::-1], mb[::-1])
            kk = kt + u
            M = jnp.maximum(jnp.maximum(mf, mb), kk)
            ef = jnp.exp(mf - M)
            eb = jnp.exp(mb - M)
            ec = jnp.exp(kk - M)
            y = (ef * af + eb * ab + ec * vt) / (ef * bf + eb * bb + ec)
            return jnp.swapaxes(y, 0, 1)
        Bn, Tn, Cn = x.shape
        h = _ln(x, ln1_w, ln1_b)
        k = h @ Wk_a.T
        v = h @ Wv_a.T
        sr = jax.nn.sigmoid(h @ Wr_a.T)
        y = bi_wkv(decay / Tn, first / Tn, k, v)
        x = x + sr * y @ Wo_a.T
        h = _ln(x, ln2_w, ln2_b)
        kf = jnp.square(jax.nn.relu(h @ Wk_f.T))
        x = x + jax.nn.sigmoid(h @ Wr_f.T) * (kf @ Wv_f.T)
        return x

    def _L1_ffn_ref(x, Wg, bg, W1, b1, W2, b2):
        import jax, jax.numpy as jnp
        import numpy as np
        B, T, E = (2, 256, 192)
        H = 768
        N_EXP = 4
        gate_logits = jnp.einsum('bte,en->btn', x, Wg) + bg
        top = jnp.argmax(gate_logits, axis=-1)
        h = jax.nn.gelu(jnp.einsum('bte,neh->nbth', x, W1) + b1[:, None, None, :], approximate=False)
        y = jnp.einsum('nbth,nhe->nbte', h, W2) + b2[:, None, None, :]
        onehot = jax.nn.one_hot(top, N_EXP, dtype=x.dtype)
        out = jnp.einsum('nbte,btn->bte', y, onehot)
        return out
    h = _L0_tok_ref(x, L0_tok_w_dw, L0_tok_b_dw, L0_tok_w_pw, L0_tok_b_pw, L0_tok_gamma, L0_tok_beta)
    h = h + _L0_attn_ref(_layernorm(h, axis=-1), L0_attn_w_attn, L0_attn_b_attn, L0_attn_w_proj, L0_attn_b_proj)
    h = h + _L0_ffn_ref(_layernorm(h, axis=-1), L0_ffn_scale, L0_ffn_gate_w, L0_ffn_gate_b, L0_ffn_w1, L0_ffn_b1, L0_ffn_w2, L0_ffn_b2)
    h = h + _L1_attn_ref(_layernorm(h, axis=-1), L1_attn_ln1_w, L1_attn_ln1_b, L1_attn_ln2_w, L1_attn_ln2_b, L1_attn_decay, L1_attn_first, L1_attn_Wk_a, L1_attn_Wv_a, L1_attn_Wr_a, L1_attn_Wo_a, L1_attn_Wk_f, L1_attn_Wv_f, L1_attn_Wr_f)
    h = h + _L1_ffn_ref(_layernorm(h, axis=-1), L1_ffn_Wg, L1_ffn_bg, L1_ffn_W1, L1_ffn_b1, L1_ffn_W2, L1_ffn_b2)
    return h

_drawn_inputs = setup_inputs


def setup_inputs(seed=0):
    import zlib

    import numpy as np

    out = dict(_drawn_inputs(seed))
    spreads = {'L0_tok_gamma': (1.0, 0.2),
     'L0_tok_beta': (0.0, 0.1),
     'L0_ffn_scale': (1.0, 0.6),
     'L0_ffn_gate_b': (0.0, 0.8),
     'L1_attn_ln1_w': (1.0, 0.6),
     'L1_attn_ln1_b': (0.0, 0.8),
     'L1_attn_ln2_w': (1.0, 0.6),
     'L1_attn_ln2_b': (0.0, 0.8)}
    factors = {'L0_attn_b_attn': 7.959,
     'L0_attn_b_proj': 2.862,
     'L0_ffn_gate_w': 4.77,
     'L0_ffn_w1': 4.448,
     'L0_ffn_b1': 8.0,
     'L0_ffn_w2': 4.439,
     'L0_ffn_b2': 8.0,
     'L1_attn_decay': 8.0,
     'L1_attn_first': 64.0,
     'L1_attn_Wk_a': 8.0,
     'L1_attn_Wv_a': 8.0,
     'L1_attn_Wr_a': 8.0,
     'L1_attn_Wo_a': 8.0,
     'L1_attn_Wk_f': 5.55,
     'L1_attn_Wv_f': 5.181,
     'L1_attn_Wr_f': 8.0,
     'L1_ffn_bg': 13.385,
     'L1_ffn_b1': 60.099,
     'L1_ffn_b2': 41.39,
     'L1_ffn_Wg': 3.63,
     'L1_ffn_W1': 4.459,
     'L1_ffn_W2': 3.761}
    for name, (base, spread) in spreads.items():
        noise = np.random.default_rng([zlib.crc32(name.encode()), seed]).standard_normal(out[name].shape)
        drawn = base * np.exp(spread * noise) if base else spread * noise
        out[name] = jnp.asarray(drawn.astype(out[name].dtype))
    for name, factor in factors.items():
        out[name] = (out[name] * factor).astype(out[name].dtype)
    return out
```

```python
from contextlib import ExitStack

import numpy as np

import concourse.bass as bass
from concourse import mybir

F32 = mybir.dt.float32
F32R = mybir.dt.float32r
ALU = mybir.AluOpType
ACT = mybir.ActivationFunctionType
AXX = mybir.AxisListType.X

P = 128
B, S, D = 128, 125, 192
T = S // 2
TP = 64
TAPS = 7
HALO = TAPS // 2
NB = 8
NT = B // NB
NG = NB // 2
N = NB * TP
D2 = D - P
HEADS, HD = 12, 16
PAIRS = HEADS // 2
CONV_T = 2 * T
KC = D // 2 + 1
KP = KC + 1
EPS = 1e-5
NEG = -1.0e38
MASKED = -1.0e30
FREE = 3.0e38

A_COLS = {"pw": 256, "fft": 2 * KP, "q": 256, "k": 256, "v": 192, "proj": 192, "gate": 16}
C_COLS = {"wk": 256, "wv": 256, "wr": 256, "wo": 192, "rf": 192, "kf": 768, "gate": 16}


def offsets(cols):
    at, out = 0, {}
    for name, n in cols.items():
        out[name] = (at, n)
        at += n
    return out, at


A_AT, A_TOT = offsets(A_COLS)
C_AT, C_TOT = offsets(C_COLS)

A_COL = {n: k for k, n in enumerate(
    [f"tap{j}a" for j in range(TAPS)] + [f"tap{j}b" for j in range(TAPS)]
    + ["bdwa", "bdwb", "bpwa", "bpwb", "bqa", "bqb", "bkea", "bkoa", "bkeb", "bkob", "even", "odd"])}
A_ROW = {n: k for k, n in enumerate(["gamma", "beta", "bv", "bproj", "scale", "gateb"])}
C_ROW = {n: k for k, n in enumerate(["ln1w", "ln1b", "ln2w", "ln2b", "gateb"])}


class Semaphores:

    def __init__(self, nc, phase):
        self.nc, self.all = nc, []
        self.passed = self.new(f"passed{phase}")

    def new(self, name):
        self.all.append(self.nc.alloc_semaphore(name=name))
        return self.all[-1]

    def end(self):
        self.nc.all_engine_barrier()
        self.nc.clear_and_free_semaphores(self.all)
        self.nc.all_engine_barrier()


class Signal:

    def __init__(self, nc, stack, name, per=1, ways=2, step=1, credit=False):
        self.sem = stack.new(name)
        self.per, self.ways, self.step = per, ways, step
        self.primed = per * ways * step if credit else 0

    def credit(self, eng):
        eng.sem_inc(self.sem, self.primed)

    def now(self, it, u, n=None):
        n = self.per if n is None else n
        return it * (self.per * self.ways * self.step) + (u * self.per + n) * self.step + self.primed

    def last(self, it, u, n=None):
        n = self.per if n is None else n
        return it * (self.per * self.ways * self.step) + (u * self.per + n) * self.step

    def back(self, it, k):
        return self.now(it, k) if k >= 0 else self.last(it, self.ways + k)


def product5(nc, out, act, act_cols, w, w_cols, act_moves, start, stop):
    passes = ((0, 0, 0), (0, 1, 0), (1, 0, 0), (2, 0, 1), (2, 1, 1))
    last = None
    for k, (a, hl, part) in enumerate(passes):
        x = act[:, a, act_cols]
        y = w[:, hl, part, w_cols]
        lhs, rhs = (y, x) if act_moves else (x, y)
        last = nc.tensor.matmul(out, lhs, rhs, start=start and k == 0, stop=stop and k == 4,
                                skip_group_check=True)
    return last


def split_weights(nc, stack, prefix, jobs):
    CH = 1024
    pieces = []
    for src, hi, lo in jobs:
        p, n = src.shape
        for c in range(0, n, CH):
            m = min(CH, n - c)
            pieces.append((src[:, c:c + m], hi[:, c:c + m], lo[:, c:c + m], p, m))
    with ExitStack() as ctx:
        stage = ctx.enter_context(nc.sbuf_tensor(f"{prefix}_stage", [P, 4, CH], F32))
        loaded = [stack.new(f"{prefix}_loaded{j}") for j in range(4)]
        high = stack.new(f"{prefix}_high")
        low = stack.new(f"{prefix}_low")
        block = ctx.enter_context(nc.Block())

        @block.sync
        def _(sp):
            for k, (src, hi, lo, p, m) in enumerate(pieces):
                if k >= 4:
                    sp.wait_ge(low, k - 3)
                sp.dma_start(stage[0:p, k % 4, 0:m], src).then_inc(loaded[k % 4], 16)

        @block.scalar
        def _(act):
            for k, (src, hi, lo, p, m) in enumerate(pieces):
                act.wait_ge(loaded[k % 4], 16 * (k // 4 + 1))
                nc.scalar.copy(hi, stage[0:p, k % 4, 0:m]).then_inc(high, 1)

        @block.vector
        def _(dve):
            for k, (src, hi, lo, p, m) in enumerate(pieces):
                dve.wait_ge(high, k + 1)
                nc.vector.tensor_tensor(lo, stage[0:p, k % 4, 0:m], hi.bitcast(F32),
                                        ALU.subtract).then_inc(low, 1)


def fill_identity(nc, pool, ident, sem):
    pool.memset(ident[:, :], 0.0).then_inc(sem, 1)
    pool.wait_ge(sem, 1)
    pool.affine_select(out=ident[:, :], in_=ident[:, :], compare_op=ALU.not_equal, fill=1.0,
                       base=0, pattern=[[-1, P]], channel_multiplier=1).then_inc(sem, 1)


def norm_stats(nc, stack, dve, src, st, mv, stats_ready, moments_ready, it, u):
    for g in range(NG):
        nc.vector.bn_stats(st[:, g, :], src[:, g, :]).then_inc(stats_ready.sem, 1)
    dve.wait_ge(stats_ready.sem, stats_ready.now(it, u))
    dve.sem_inc(stack.passed, 1)
    for g in range(NG):
        nc.vector.bn_aggr(mv[:, g, :], st[:, g, :]).then_inc(moments_ready.sem, 1)


def norm_apply(nc, out, src, mv, rs, sig):
    for g in range(NG):
        nc.vector.tensor_scalar(out[:, g, :], src[:, g, :], mv[:, g, 0:1], rs[:, g:g + 1],
                                ALU.subtract, ALU.mult).then_inc(sig.sem, 1)


def transpose_tile(nc, ps, b0, src, ident, sig):
    for g in range(NG):
        nc.tensor.transpose(ps[:, b0, g * P:(g + 1) * P], src[:, g, 0:P], ident[:, :])
    for g in range(NG):
        last = nc.tensor.transpose(ps[0:D2, b0 + 1, g * P:(g + 1) * P], src[:, g, P:D], ident[:, :])
    last.then_inc(sig.sem, 1)


def pack_high(nc, ps, b0, pk, sig):
    nc.scalar.copy(pk[:, 0, :], ps[:, b0, :]).then_inc(sig.sem, 1)
    nc.scalar.copy(pk[0:D2, 2, :], ps[0:D2, b0 + 1, :]).then_inc(sig.sem, 1)


def pack_low(nc, dve, ps, b0, pk, high, sig, it, u):
    dve.wait_ge(high.sem, high.now(it, u, 1))
    nc.vector.tensor_tensor(pk[:, 1, :], ps[:, b0, :], pk[:, 0, :].bitcast(F32),
                            ALU.subtract).then_inc(sig.sem, 1)
    dve.wait_ge(high.sem, high.now(it, u, 2))
    nc.vector.tensor_tensor(pk[D2:P, 2, :], ps[0:D2, b0 + 1, :], pk[0:D2, 2, :].bitcast(F32),
                            ALU.subtract).then_inc(sig.sem, 1)


def bcast_groups(row, n=D):
    return row[:, 0:n].unsqueeze(1).to_broadcast([P, NG, n])


class Router:

    def __init__(self, nc, stack, ctx, prefix, experts, k):
        self.nc, self.e, self.k, self.stack = nc, experts, k, stack
        sb = lambda n, shape: ctx.enter_context(nc.sbuf_tensor(f"{prefix}_{n}", shape, F32))
        self.gb = [sb(f"gb{u}", [P, NG, 24]) for u in range(2)]
        self.rep = [sb(f"rep{u}", [P, NG, 24]) for u in range(2)]
        self.m8 = [sb(f"m8{u}", [P, NG, 8]) for u in range(2)]
        self.sh = [sb(f"sh{u}", [P, NG, 16]) for u in range(2)]
        self.ex = [sb(f"ex{u}", [P, NG, 16]) for u in range(2)]
        self.wm = [sb(f"wm{u}", [P, NG, 16]) for u in range(2)]
        self.den = [sb(f"den{u}", [P, NG]) for u in range(2)]
        self.fw = [sb(f"fw{u}", [P, NG, 16]) for u in range(2)]
        sig = lambda n, per=1: Signal(nc, stack, f"{prefix}_{n}", per)
        self.biased, self.found, self.cut = sig("biased"), sig("found", NG), sig("cut")
        self.replaced, self.masked = sig("replaced", NG), sig("masked")
        self.shifted, self.exped = sig("shifted"), sig("exped")
        self.weighed, self.summed, self.inverse = sig("weighed"), sig("summed"), sig("inverse")
        self.gates = sig("gates")
        self.init = stack.new(f"{prefix}_init")

    def start(self, dve):
        nc = self.nc
        for u in range(2):
            nc.vector.memset(self.gb[u][:, :, 0:16], -FREE)
            nc.vector.memset(self.gb[u][:, :, 16:24], FREE)
            nc.vector.memset(self.wm[u][:, :, :], 0.0)
            nc.vector.memset(self.fw[u][:, :, :], 0.0).then_inc(self.init, 1)
        dve.wait_ge(self.init, 2)

    def choose(self, dve, logits, bias_row, it, u):
        nc, e, k = self.nc, self.e, self.k
        gb, rep, m8 = self.gb[u], self.rep[u], self.m8[u]
        nc.vector.tensor_tensor(gb[:, :, 0:e], logits, bcast_groups(bias_row, e),
                                ALU.add).then_inc(self.biased.sem, 1)
        dve.wait_ge(self.biased.sem, self.biased.now(it, u))
        dve.sem_inc(self.stack.passed, 1)
        for g in range(NG):
            nc.vector.max(m8[:, g, :], gb[:, g, 0:16]).then_inc(self.found.sem, 1)
        dve.wait_ge(self.found.sem, self.found.now(it, u))
        nc.vector.memset(m8[:, :, k:8], FREE).then_inc(self.cut.sem, 1)
        if k > 1:
            nc.vector.tensor_tensor(self.sh[u][:, :, :], gb[:, :, 0:16],
                                    m8[:, :, 0:1].to_broadcast([P, NG, 16]),
                                    ALU.subtract).then_inc(self.shifted.sem, 1)
        dve.wait_ge(self.cut.sem, self.cut.now(it, u))
        dve.sem_inc(self.stack.passed, 1)
        for g in range(NG):
            nc.vector.match_replace(rep[:, g, :], m8[:, g, :], gb[:, g, :], -FREE / 2
                                    ).then_inc(self.replaced.sem, 1)
        dve.wait_ge(self.replaced.sem, self.replaced.now(it, u))
        if k == 1:
            nc.vector.tensor_tensor(self.fw[u][:, :, 0:e], rep[:, :, 0:e], gb[:, :, 0:e],
                                    ALU.not_equal).then_inc(self.gates.sem, 1)
            return
        nc.vector.tensor_tensor(self.wm[u][:, :, :], rep[:, :, 0:16], gb[:, :, 0:16],
                                ALU.not_equal).then_inc(self.masked.sem, 1)
        dve.wait_ge(self.masked.sem, self.masked.now(it, u))
        dve.wait_ge(self.exped.sem, self.exped.now(it, u))
        nc.vector.tensor_tensor(self.wm[u][:, :, :], self.wm[u][:, :, :], self.ex[u][:, :, :],
                                ALU.mult).then_inc(self.weighed.sem, 1)
        dve.wait_ge(self.weighed.sem, self.weighed.now(it, u))
        nc.vector.tensor_reduce(self.den[u][:, :], self.wm[u][:, :, :], AXX, ALU.add
                                ).then_inc(self.summed.sem, 1)
        dve.wait_ge(self.summed.sem, self.summed.now(it, u))
        nc.vector.reciprocal(self.den[u][:, :], self.den[u][:, :]).then_inc(self.inverse.sem, 1)
        dve.wait_ge(self.inverse.sem, self.inverse.now(it, u))
        nc.vector.tensor_tensor(self.fw[u][:, :, :], self.wm[u][:, :, :],
                                self.den[u][:, :].unsqueeze(2).to_broadcast([P, NG, 16]),
                                ALU.mult).then_inc(self.gates.sem, 1)

    def exponentials(self, act, it, u):
        act.wait_ge(self.shifted.sem, self.shifted.now(it, u))
        self.nc.scalar.activation(self.ex[u][:, :, :], self.sh[u][:, :, :], ACT.Exp
                                  ).then_inc(self.exped.sem, 1)

    def spread(self, pe, ps, bank, ident, sig, it, u):
        pe.wait_ge(self.gates.sem, self.gates.now(it, u))
        for g in range(NG):
            last = self.nc.tensor.transpose(ps[0:16, bank, g * P:(g + 1) * P],
                                            self.fw[u][:, g, :], ident[:, :])
        last.then_inc(sig.sem, 1)


def phase_a(nc, stack, io):
    with ExitStack() as ctx:
        sb = lambda n, shape, dt=F32: ctx.enter_context(nc.sbuf_tensor(f"a_sb_{n}", shape, dt))
        two = lambda n, shape, dt=F32: [sb(f"{n}{u}", shape, dt) for u in range(2)]
        sig = lambda n, per=1, step=1, ways=2, credit=False: Signal(nc, stack, f"a_{n}", per, ways, step, credit)
        sig4 = lambda n, per=1: sig(n, per, ways=4)
        ps = ctx.enter_context(nc.psum_tensor("a_ps", [P, 8, 512], F32))

        W = sb("W", [P, 2, 2, A_TOT], F32R)
        CS = sb("CS", [P, 2, 2, P], F32R)
        cols = sb("cols", [P, len(A_COL)])
        rows = sb("rows", [P, len(A_ROW), D])
        mask = sb("mask", [P, P])
        ident = sb("ident", [P, P])
        split_weights(nc, stack, "aw", [
            (io["a_w"].rearrange("p a n -> p (a n)"),
             W[:, 0].rearrange("p a n -> p (a n)"), W[:, 1].rearrange("p a n -> p (a n)")),
            (io["dft_t"], CS[:, 0].rearrange("p a n -> p (a n)"), CS[:, 1].rearrange("p a n -> p (a n)"))])

        xin = two("xin", [P, NB + NB // 2, CONV_T + 2 * HALO])
        acc = two("acc", [P, (NB + NB // 2) * CONV_T])
        cv = two("cv", [P, 2 * (NB + NB // 2) * CONV_T], F32R)
        mx = two("mx", [P, 2, NB, TP])
        pk = two("pk", [P, 3, N], F32R)
        bs = two("bs", [P, NG, KP])
        yb, hb, nb = two("yb", [P, NG, D]), two("hb", [P, NG, D]), two("nb", [P, NG, D])
        q = two("q", [P, 2, N])
        kx = two("kx", [P, 2, 2, N])
        vblk = two("vblk", [P, NG, 2, PAIRS, 2, HD + 1])
        pt = two("pt", [P, 2 * PAIRS, P])
        sm_mx = two("smmx", [P, 2 * HEADS])
        rden = two("rden", [P, 2 * HEADS])
        st, mv = two("st", [P, NG, 6]), two("mv", [P, NG, 2])
        rs = two("rs", [P, NG])
        ra, rb, rc = two("ra", [P, NG]), two("rb", [P, NG]), two("rc", [P, NG])
        half = sb("half", [P, NG])
        fwt = two("fwt", [64, N], F32R)
        router = Router(nc, stack, ctx, "ar", 16, 4)

        dma = lambda n: [sig(f"{n}{u}", 1, 16, 1) for u in range(2)]
        loaded, consts = dma("loaded"), stack.new("a_consts")
        setup = stack.new("a_setup")
        cleared = stack.new("a_cleared")
        identity = stack.new("a_identity")
        conv0, conv, conv_h, conv_l = sig("conv0", 2), sig("conv", 2 * (TAPS - 1), credit=True), sig("convh", 2), sig("convl", 2)
        pw_done, pooled, act_r = sig("pwdone"), sig("pooled", 2), sig("relu", 2)
        hp_h, hp_l = sig("hph", 2), sig("hpl", 2)
        ftd, pq_h, pq_l = sig("ftd"), sig("pqh"), sig("pql")
        fts, bs_up, y_ready = sig("fts"), sig("bsup"), sig("y", 2)
        s1, m1, v1, r1, a1, g1, h0 = sig("s1", 4), sig("m1", 4), sig("v1"), sig("r1"), sig("a1", 4), sig("g1"), sig("h0")
        s2, m2, v2, r2, n1 = sig("s2", 4), sig("m2", 4), sig("v2"), sig("r2"), sig("n1", 4)
        t1, p1h, p1l = sig("t1"), sig("p1h", 2), sig("p1l", 2)
        q_ps, q_up, k_ps, v_ps, v_up = sig("qps"), sig("qup", 2), sig("kps"), sig("vps"), sig("vup")
        ka_up, kv_up, vd_up, vo_up = sig("kaup", 2), sig("kvup", 2), sig("vdup", 2), sig("voup", 2)
        sc, sadd, smax, ssub, sexp = sig4("sc"), sig4("sadd", 4), sig4("smax"), sig4("ssub"), sig4("sexp")
        ptt, pta, ptv, pv, rd, at = sig4("ptt"), sig4("pta", 2), sig4("ptv"), sig4("pv"), sig4("rd"), sig4("at")
        t2, p2h, p2l = sig("t2"), sig("p2h", 2), sig("p2l", 2)
        hbias, pr, h1 = sig("hbias"), sig("pr"), sig("h1")
        s3, m3, pl3, n2, base, tt = sig("s3", 4), sig("m3", 4), sig("pl3", 6), sig("n2", 4), sig("base"), sig("tt", 4)
        t3, p3h, p3l = sig("t3"), sig("p3h", 2), sig("p3l", 2)
        gt, fwps, fwh, fwl = sig("gt"), sig("fwps"), sig("fwh"), sig("fwl")
        st_pk, st_fw, st_base = dma("stpk"), dma("stfw"), dma("stbase")
        block = ctx.enter_context(nc.Block())
        col = lambda n, p0=0, p1=P: cols[p0:p1, A_COL[n]:A_COL[n] + 1]
        row = lambda n: rows[:, A_ROW[n], :]
        w_at = lambda n, a=0, m=None: slice(A_AT[n][0] + a, A_AT[n][0] + a + (m or A_AT[n][1]))
        NC = NB * CONV_T
        acc0 = [a[:, 0:NC].rearrange("p (b s) -> p b s", b=NB) for a in acc]
        acc1 = [a[:, NC:NC + NC // 2].rearrange("p (b s) -> p b s", b=NB // 2) for a in acc]
        sm = [a[:, 0:2 * PAIRS * P].rearrange("p (g j c) -> p g j c", g=2, j=PAIRS) for a in [
            sb(f"sm{u}", [P, 2 * PAIRS * P]) for u in range(2)]]
        pqn = NG * 2 * KP
        pq = [[c[:, hl * pqn:(hl + 1) * pqn].rearrange("p (g n) -> p g n", g=NG) for hl in range(2)] for c in cv]

        def dft_out(u, b0):
            return ps[:, 4 * u + b0:4 * u + b0 + 2, :].rearrange("p b (h n) -> p b h n", h=2)[:, :, :, 0:2 * KP]

        def two_banks(u, b0, n):
            return ps[:, 4 * u + b0:4 * u + b0 + 2, :].rearrange("p b (h n) -> p b h n", h=2)[:, :, :, 0:n]

        def split4(ap):
            return ap.rearrange("p (b h) n -> p b h n", b=2)

        @block.sync
        def _(sp):
            sp.dma_start(cols[:, :], io["a_cols"]).then_inc(consts, 16)
            sp.dma_start(rows[:, :, :], io["a_rows"]).then_inc(consts, 16)
            sp.dma_start(mask[:, :], io["a_mask"]).then_inc(consts, 16)
            with sp.Fori(0, NT // 2) as it:
                for u in range(2):
                    sp.wait_ge(conv.sem, conv.last(it, u))
                    sp.sem_inc(stack.passed, 1)
                    sp.dma_start(xin[u][:, :, :], io["x"][it * 2 + u]).then_inc(loaded[u].sem, 16)
                for u in range(2):
                    sp.wait_ge(base.sem, base.now(it, u))
                    sp.sem_inc(stack.passed, 1)
                    sp.dma_start(io["base"][it * 2 + u], hb[u][:, :, :]).then_inc(st_base[u].sem, 16)
                for u in range(2):
                    sp.wait_ge(p3h.sem, p3h.now(it, u))
                    sp.sem_inc(stack.passed, 1)
                    sp.wait_ge(p3l.sem, p3l.now(it, u))
                    sp.sem_inc(stack.passed, 1)
                    sp.dma_start(io["tp"][it * 2 + u], pk[u][:, :, :].bitcast(F32)).then_inc(st_pk[u].sem, 16)
                for u in range(2):
                    sp.wait_ge(fwh.sem, fwh.now(it, u))
                    sp.sem_inc(stack.passed, 1)
                    sp.wait_ge(fwl.sem, fwl.now(it, u))
                    sp.sem_inc(stack.passed, 1)
                    sp.dma_start(io["fw"][it * 2 + u], fwt[u][:, :].bitcast(F32)).then_inc(st_fw[u].sem, 16)
                for u in range(2):
                    sp.wait_ge(st_base[u].sem, st_base[u].now(it, 0))
                    sp.sem_inc(stack.passed, 1)
                    sp.wait_ge(st_pk[u].sem, st_pk[u].now(it, 0))
                    sp.sem_inc(stack.passed, 1)
                    sp.wait_ge(st_fw[u].sem, st_fw[u].now(it, 0))
                    sp.sem_inc(stack.passed, 1)

        @block.gpsimd
        def _(pool):
            fill_identity(nc, pool, ident, identity)
            nc.gpsimd.memset(half[:, :], -0.5).then_inc(setup, 1)
            for u in range(2):
                nc.gpsimd.memset(vblk[u][:, :, :, :, :, :], 0.0).then_inc(setup, 1)
                nc.gpsimd.memset(mx[u][:, :, :, :], 0.0).then_inc(setup, 1)
            pool.wait_ge(setup, 5)
            for u in range(2):
                for par in range(2):
                    nc.gpsimd.memset(vblk[u][64 * par:64 * par + 64, :, :, :, par, HD:HD + 1], 1.0).then_inc(setup, 1)
            pool.wait_ge(setup, 9)
            with pool.Fori(0, NT // 2) as it:
                for (m, v, r) in ((m1, v1, r1), (m2, v2, r2)):
                    for u in range(2):
                        pool.wait_ge(m.sem, m.now(it, u))
                        pool.sem_inc(stack.passed, 1)
                        nc.gpsimd.tensor_scalar(ra[u][:, :], mv[u][:, :, 1], EPS, None, ALU.add).then_inc(v.sem, 1)
                        pool.wait_ge(v.sem, v.now(it, u))
                        nc.gpsimd.tensor_tensor(rs[u][:, :], ra[u][:, :], half[:, :], ALU.pow).then_inc(r.sem, 1)
                for u in range(2):
                    pool.wait_ge(v_up.sem, v_up.now(it, u))
                    pool.sem_inc(stack.passed, 1)
                    for b in range(2):
                        for par in range(2):
                            if b != par:
                                continue
                            nc.gpsimd.tensor_copy(
                                vblk[u][64 * par:64 * par + 64, :, b, :, par, 0:HD],
                                yb[u][64 * b:64 * b + 64, :, :].rearrange("p g (j a c) -> p g j a c", j=PAIRS, a=2)[:, :, :, par, :]
                            ).then_inc(vd_up.sem, 1)
                pool.wait_ge(vd_up.sem, vd_up.now(it, 1))
                for pg in range(2):
                    for u in range(2):
                        pool.wait_ge(smax.sem, smax.now(it, 2 * pg + u))
                        nc.gpsimd.tensor_tensor(
                            sm[u].rearrange("p g j (a c) -> p (g j a) c", a=2),
                            sm[u].rearrange("p g j (a c) -> p (g j a) c", a=2),
                            sm_mx[u][:, :].unsqueeze(2).to_broadcast([P, 2 * HEADS, TP]),
                            ALU.subtract).then_inc(ssub.sem, 1)
                for u in range(2):
                    pool.wait_ge(p1l.sem, p1l.now(it, u))
                    pool.wait_ge(h0.sem, h0.now(it, u))
                    nc.gpsimd.tensor_tensor(hb[u][:, :, :], hb[u][:, :, :], bcast_groups(row("bproj")), ALU.add).then_inc(hbias.sem, 1)
                for u in range(2):
                    pool.wait_ge(m3.sem, m3.now(it, u))
                    pool.sem_inc(stack.passed, 1)
                    nc.gpsimd.tensor_scalar(ra[u][:, :], mv[u][:, :, 1], EPS, None, ALU.add).then_inc(pl3.sem, 1)
                    pool.wait_ge(pl3.sem, pl3.now(it, u, 1))
                    nc.gpsimd.tensor_tensor(rs[u][:, :], ra[u][:, :], half[:, :], ALU.pow).then_inc(pl3.sem, 1)
                    pool.wait_ge(pl3.sem, pl3.now(it, u, 2))
                    nc.gpsimd.tensor_tensor(rb[u][:, :], rs[u][:, :], rs[u][:, :], ALU.mult).then_inc(pl3.sem, 1)
                    pool.wait_ge(pl3.sem, pl3.now(it, u, 3))
                    nc.gpsimd.tensor_tensor(rb[u][:, :], rb[u][:, :], mv[u][:, :, 1], ALU.mult).then_inc(pl3.sem, 1)
                    pool.wait_ge(pl3.sem, pl3.now(it, u, 4))
                    pool.sem_inc(stack.passed, 1)
                    nc.gpsimd.tensor_scalar(rb[u][:, :], rb[u][:, :], EPS, None, ALU.add).then_inc(pl3.sem, 1)
                    pool.wait_ge(pl3.sem, pl3.now(it, u, 5))
                    nc.gpsimd.tensor_tensor(rc[u][:, :], rb[u][:, :], half[:, :], ALU.pow).then_inc(pl3.sem, 1)

        @block.vector
        def _(dve):
            dve.wait_ge(consts, 48)
            router.start(dve)
            for u in range(2):
                nc.vector.memset(fwt[u][:, :].bitcast(F32), 0.0).then_inc(cleared, 1)
            dve.wait_ge(setup, 9)
            dve.wait_ge(cleared, 2)
            conv.credit(dve)
            with dve.Fori(0, NT // 2) as it:
                for u in range(2):
                    xa, xb = xin[u][:, 0:NB, :], xin[u][:, NB:NB + NB // 2, :]
                    dve.wait_ge(conv0.sem, conv0.now(it, u))
                    for j in range(1, TAPS):
                        for c, (x, a) in enumerate(((xa, acc0[u]), (xb, acc1[u]))):
                            if j > 1:
                                dve.wait_ge(conv.sem, conv.now(it, u, 2 * (j - 2) + c + 1))
                            nc.vector.scalar_tensor_tensor(
                                a, x[:, :, j:j + CONV_T], col(f"tap{j}{'ab'[c]}"), a,
                                ALU.mult, ALU.add).then_inc(conv.sem, 1)
                    for c, (c0, c1) in enumerate(((0, NC), (NC, NC + NC // 2))):
                        dve.wait_ge(conv_h.sem, conv_h.now(it, u, c + 1))
                        nc.vector.tensor_tensor(cv[u][:, NC * 3 // 2 + c0:NC * 3 // 2 + c1], acc[u][:, c0:c1],
                                                cv[u][:, c0:c1].bitcast(F32), ALU.subtract).then_inc(conv_l.sem, 1)
                for u in range(2):
                    dve.wait_ge(pw_done.sem, pw_done.now(it, u))
                    for c in range(2):
                        src = ps[:, 4 * u + 2 * c:4 * u + 2 * c + 2, 0:NC // 2].rearrange(
                            "p h (b s t) -> p h b s t", b=NB // 2, t=2)
                        nc.vector.tensor_reduce(
                            mx[u][:, c, :, 0:T].rearrange("p (h b) s -> p h b s", h=2), src, AXX, ALU.max
                        ).then_inc(pooled.sem, 1)
                for u in range(2):
                    dve.wait_ge(hp_h.sem, hp_h.now(it, u, 1))
                    nc.vector.tensor_tensor(pk[u][:, 1, :], mx[u][:, 0].rearrange("p b s -> p (b s)"),
                                            pk[u][:, 0, :].bitcast(F32), ALU.subtract).then_inc(hp_l.sem, 1)
                    dve.wait_ge(hp_h.sem, hp_h.now(it, u, 2))
                    nc.vector.tensor_tensor(pk[u][D2:P, 2, :], mx[u][0:D2, 1].rearrange("p b s -> p (b s)"),
                                            pk[u][0:D2, 2, :].bitcast(F32), ALU.subtract).then_inc(hp_l.sem, 1)
                for u in range(2):
                    dve.wait_ge(pq_h.sem, pq_h.now(it, u))
                    nc.vector.tensor_tensor(split4(pq[u][1]), dft_out(u, 0), split4(pq[u][0].bitcast(F32)),
                                            ALU.subtract).then_inc(pq_l.sem, 1)
                for u in range(2):
                    dve.wait_ge(bs_up.sem, bs_up.now(it, u))
                    a = two_banks(u, 2, KP)
                    nc.vector.tensor_tensor(split4(yb[u][:, :, 0:KC]), a[:, :, :, 0:KC], split4(bs[u][:, :, 0:KC]),
                                            ALU.subtract).then_inc(y_ready.sem, 1)
                    nc.vector.tensor_tensor(split4(yb[u][:, :, KC:D]), a[:, :, :, 1:KC - 1],
                                            split4(bs[u][:, :, 1:KC - 1]), ALU.add).then_inc(y_ready.sem, 1)
                for u in range(2):
                    dve.wait_ge(y_ready.sem, y_ready.now(it, u))
                    norm_stats(nc, stack, dve, yb[u], st[u], mv[u], s1, m1, it, u)
                for u in range(2):
                    dve.wait_ge(r1.sem, r1.now(it, u))
                    norm_apply(nc, nb[u], yb[u], mv[u], rs[u], a1)
                for u in range(2):
                    dve.wait_ge(a1.sem, a1.now(it, u))
                    nc.vector.tensor_tensor(nb[u][:, :, :], nb[u][:, :, :], bcast_groups(row("gamma")), ALU.mult).then_inc(g1.sem, 1)
                for u in range(2):
                    dve.wait_ge(g1.sem, g1.now(it, u))
                    nc.vector.tensor_tensor(hb[u][:, :, :], nb[u][:, :, :], bcast_groups(row("beta")), ALU.add).then_inc(h0.sem, 1)
                for u in range(2):
                    dve.wait_ge(h0.sem, h0.now(it, u))
                    norm_stats(nc, stack, dve, hb[u], st[u], mv[u], s2, m2, it, u)
                for u in range(2):
                    dve.wait_ge(r2.sem, r2.now(it, u))
                    norm_apply(nc, nb[u], hb[u], mv[u], rs[u], n1)
                for u in range(2):
                    dve.wait_ge(t1.sem, t1.now(it, u))
                    pack_low(nc, dve, ps, 4 * u, pk[u], p1h, p1l, it, u)
                for u in range(2):
                    dve.wait_ge(k_ps.sem, k_ps.now(it, u))
                    nc.vector.tensor_scalar(kx[u][0:D2, 1, 0, :], ps[0:D2, 4 * u + 1, :], col("even", 0, D2), col("bkeb", 0, D2),
                                            ALU.mult, ALU.add).then_inc(kv_up.sem, 1)
                    nc.vector.tensor_scalar(kx[u][0:D2, 1, 1, :], ps[0:D2, 4 * u + 1, :], col("odd", 0, D2), col("bkob", 0, D2),
                                            ALU.mult, ALU.add).then_inc(kv_up.sem, 1)
                for u in range(2):
                    dve.wait_ge(v_ps.sem, v_ps.now(it, u))
                    nc.vector.tensor_tensor(split4(yb[u][:, :, :]), two_banks(u, 2, D),
                                            row("bv").unsqueeze(1).unsqueeze(1).to_broadcast([P, 2, 2, D]), ALU.add).then_inc(v_up.sem, 1)
                for pg in range(2):
                    for u in range(2):
                        dve.wait_ge(sc.sem, sc.now(it, 2 * pg + u))
                        if pg == 1:
                            dve.wait_ge(ptt.sem, ptt.now(it, u))
                        s = ps[:, 4 * u:4 * u + 4, :].rearrange("p r (g s c) -> p g s r c", g=2, s=2)
                        for g in range(2):
                            nc.vector.tensor_tensor(sm[u][:, g, 0:4, :], s[:, g, 0, :, :],
                                                    mask[:, :].unsqueeze(1).to_broadcast([P, 4, P]), ALU.add).then_inc(sadd.sem, 1)
                            nc.vector.tensor_tensor(sm[u][:, g, 4:6, :], s[:, g, 1, 0:2, :],
                                                    mask[:, :].unsqueeze(1).to_broadcast([P, 2, P]), ALU.add).then_inc(sadd.sem, 1)
                        dve.wait_ge(sadd.sem, sadd.now(it, 2 * pg + u))
                        nc.vector.tensor_reduce(sm_mx[u][:, :], sm[u].rearrange("p g j (a c) -> p (g j a) c", a=2),
                                                AXX, ALU.max).then_inc(smax.sem, 1)
                    for u in range(2):
                        dve.wait_ge(ptt.sem, ptt.now(it, 2 * pg + u))
                        nc.vector.tensor_copy(pt[u][:, 0:4, :], ps[:, 4 * u, :].rearrange("p (j c) -> p j c", j=4)).then_inc(ptv.sem, 1)
                    for u in range(2):
                        dve.wait_ge(pv.sem, pv.now(it, 2 * pg + u))
                        o = ps[:, 4 * u + 3, 0:2 * HEADS * (HD + 1)].rearrange("p (h c) -> p h c", c=HD + 1)
                        nc.vector.reciprocal(rden[u][:, :], o[:, :, HD]).then_inc(rd.sem, 1)
                        dve.wait_ge(rd.sem, rd.now(it, 2 * pg + u))
                        nc.vector.tensor_tensor(
                            nb[u][:, 2 * pg:2 * pg + 2, :].rearrange("p g (h c) -> p (g h) c", c=HD), o[:, :, 0:HD],
                            rden[u][:, :].unsqueeze(2).to_broadcast([P, 2 * HEADS, HD]), ALU.mult).then_inc(at.sem, 1)
                for u in range(2):
                    dve.wait_ge(t2.sem, t2.now(it, u))
                    pack_low(nc, dve, ps, 4 * u, pk[u], p2h, p2l, it, u)
                for u in range(2):
                    dve.wait_ge(pr.sem, pr.now(it, u))
                    dve.wait_ge(hbias.sem, hbias.now(it, u))
                    nc.vector.tensor_tensor(split4(hb[u][:, :, :]), two_banks(u, 2, D), split4(hb[u][:, :, :]), ALU.add).then_inc(h1.sem, 1)
                for u in range(2):
                    dve.wait_ge(h1.sem, h1.now(it, u))
                    norm_stats(nc, stack, dve, hb[u], st[u], mv[u], s3, m3, it, u)
                for u in range(2):
                    dve.wait_ge(pl3.sem, pl3.now(it, u))
                    norm_apply(nc, yb[u], hb[u], mv[u], rs[u], n2)
                for u in range(2):
                    dve.wait_ge(n2.sem, n2.now(it, u))
                    nc.vector.tensor_tensor(hb[u][:, :, :], hb[u][:, :, :], yb[u][:, :, :], ALU.add).then_inc(base.sem, 1)
                    for g in range(NG):
                        nc.vector.scalar_tensor_tensor(nb[u][:, g, :], yb[u][:, g, :], rc[u][:, g:g + 1],
                                                       row("scale"), ALU.mult, ALU.mult).then_inc(tt.sem, 1)
                for u in range(2):
                    dve.wait_ge(t3.sem, t3.now(it, u))
                    pack_low(nc, dve, ps, 4 * u, pk[u], p3h, p3l, it, u)
                for u in range(2):
                    dve.wait_ge(gt.sem, gt.now(it, u))
                    router.choose(dve, ps[:, 4 * u + 2, 0:NG * 16].rearrange("p (g e) -> p g e", g=NG), row("gateb"), it, u)
                for u in range(2):
                    dve.wait_ge(fwh.sem, fwh.now(it, u))
                    nc.vector.tensor_tensor(fwt[u][32:48, :], ps[0:16, 4 * u + 3, :], fwt[u][0:16, :].bitcast(F32),
                                            ALU.subtract).then_inc(fwl.sem, 1)
                for u in range(2):
                    dve.wait_ge(st_base[u].sem, st_base[u].now(it, 0))
                    dve.wait_ge(st_pk[u].sem, st_pk[u].now(it, 0))
                    dve.wait_ge(st_fw[u].sem, st_fw[u].now(it, 0))

        @block.scalar
        def _(act):
            act.wait_ge(consts, 48)
            act.wait_ge(setup, 9)
            act.wait_ge(cleared, 2)
            with act.Fori(0, NT // 2) as it:
                for u in range(2):
                    act.wait_ge(loaded[u].sem, loaded[u].now(it, 0))
                    nc.scalar.activation(acc0[u], xin[u][:, 0:NB, 0:CONV_T], ACT.Identity,
                                         bias=col("bdwa"), scale=col("tap0a")).then_inc(conv0.sem, 1)
                    nc.scalar.activation(acc1[u], xin[u][:, NB:NB + NB // 2, 0:CONV_T], ACT.Identity,
                                         bias=col("bdwb"), scale=col("tap0b")).then_inc(conv0.sem, 1)
                for u in range(2):
                    for c, (c0, c1) in enumerate(((0, NC), (NC, NC + NC // 2))):
                        act.wait_ge(conv.sem, conv.now(it, u, 2 * (TAPS - 2) + c + 1))
                        nc.scalar.copy(cv[u][:, c0:c1], acc[u][:, c0:c1]).then_inc(conv_h.sem, 1)
                for u in range(2):
                    for c in range(2):
                        act.wait_ge(pooled.sem, pooled.now(it, u, c + 1))
                        nc.scalar.activation(mx[u][:, c, :, 0:T], mx[u][:, c, :, 0:T], ACT.Relu,
                                             bias=col(f"bpw{'ab'[c]}")).then_inc(act_r.sem, 1)
                    act.wait_ge(act_r.sem, act_r.now(it, u, 1))
                    nc.scalar.copy(pk[u][:, 0, :], mx[u][:, 0].rearrange("p b s -> p (b s)")).then_inc(hp_h.sem, 1)
                    act.wait_ge(act_r.sem, act_r.now(it, u, 2))
                    nc.scalar.copy(pk[u][0:D2, 2, :], mx[u][0:D2, 1].rearrange("p b s -> p (b s)")).then_inc(hp_h.sem, 1)
                for u in range(2):
                    act.wait_ge(ftd.sem, ftd.now(it, u))
                    nc.scalar.copy(split4(pq[u][0]), dft_out(u, 0)).then_inc(pq_h.sem, 1)
                for u in range(2):
                    act.wait_ge(fts.sem, fts.now(it, u))
                    nc.scalar.copy(split4(bs[u][:, :, :]), two_banks(u, 2, 2 * KP)[:, :, :, KP:2 * KP]).then_inc(bs_up.sem, 1)
                for u in range(2):
                    act.wait_ge(t1.sem, t1.now(it, u))
                    pack_high(nc, ps, 4 * u, pk[u], p1h)
                for u in range(2):
                    act.wait_ge(q_ps.sem, q_ps.now(it, u))
                    nc.scalar.activation(q[u][:, 0, :], ps[:, 4 * u + 2, :], ACT.Identity, bias=col("bqa")).then_inc(q_up.sem, 1)
                    nc.scalar.activation(q[u][0:D2, 1, :], ps[0:D2, 4 * u + 3, :], ACT.Identity, bias=col("bqb", 0, D2)).then_inc(q_up.sem, 1)
                for u in range(2):
                    act.wait_ge(k_ps.sem, k_ps.now(it, u))
                    nc.scalar.activation(kx[u][:, 0, 0, :], ps[:, 4 * u, :], ACT.Identity, bias=col("bkea"), scale=col("even")).then_inc(ka_up.sem, 1)
                    nc.scalar.activation(kx[u][:, 0, 1, :], ps[:, 4 * u, :], ACT.Identity, bias=col("bkoa"), scale=col("odd")).then_inc(ka_up.sem, 1)
                for u in range(2):
                    act.wait_ge(v_up.sem, v_up.now(it, u))
                    for b in range(2):
                        par = 1 - b
                        nc.scalar.copy(
                            vblk[u][64 * par:64 * par + 64, :, b, :, par, 0:HD],
                            yb[u][64 * b:64 * b + 64, :, :].rearrange("p g (j a c) -> p g j a c", j=PAIRS, a=2)[:, :, :, par, :]
                        ).then_inc(vo_up.sem, 1)
                for pg in range(2):
                    for u in range(2):
                        act.wait_ge(ssub.sem, ssub.now(it, 2 * pg + u))
                        nc.scalar.activation(sm[u], sm[u], ACT.Exp).then_inc(sexp.sem, 1)
                    for u in range(2):
                        act.wait_ge(ptt.sem, ptt.now(it, 2 * pg + u))
                        for j in range(1, 3):
                            nc.scalar.copy(pt[u][:, 4 * j:4 * j + 4, :],
                                           ps[:, 4 * u + j, :].rearrange("p (j c) -> p j c", j=4)).then_inc(pta.sem, 1)
                for u in range(2):
                    act.wait_ge(t2.sem, t2.now(it, u))
                    pack_high(nc, ps, 4 * u, pk[u], p2h)
                for u in range(2):
                    act.wait_ge(t3.sem, t3.now(it, u))
                    pack_high(nc, ps, 4 * u, pk[u], p3h)
                for u in range(2):
                    router.exponentials(act, it, u)
                for u in range(2):
                    act.wait_ge(fwps.sem, fwps.now(it, u))
                    nc.scalar.copy(fwt[u][0:16, :], ps[0:16, 4 * u + 3, :]).then_inc(fwh.sem, 1)
                for u in range(2):
                    act.wait_ge(st_pk[u].sem, st_pk[u].now(it, 0))
                    act.wait_ge(st_fw[u].sem, st_fw[u].now(it, 0))

        @block.tensor
        def _(pe):
            pe.wait_ge(identity, 2)
            pe.wait_ge(setup, 9)
            with pe.Fori(0, NT // 2) as it:
                for u in range(2):
                    pe.wait_ge(conv_h.sem, conv_h.now(it, u))
                    pe.wait_ge(conv_l.sem, conv_l.now(it, u))
                    hi, lo, m = 0, NC * 3 // 2, NC // 2
                    for c in range(2):
                        for h in range(2):
                            out = ps[:, 4 * u + 2 * c + h, 0:m]
                            w = w_at("pw", c * P, P)
                            xh, xl = cv[u][:, hi + h * m:hi + (h + 1) * m], cv[u][:, lo + h * m:lo + (h + 1) * m]
                            nc.tensor.matmul(out, W[:, 0, 0, w], xh, start=True, stop=False)
                            nc.tensor.matmul(out, W[:, 1, 0, w], xh, start=False, stop=False)
                            nc.tensor.matmul(out, W[:, 0, 0, w], xl, start=False, stop=False)
                            r = slice(64 * h, 64 * h + 64)
                            xh, xl = cv[u][r, hi + NC:hi + NC + m], cv[u][r, lo + NC:lo + NC + m]
                            nc.tensor.matmul(out, W[r, 0, 1, w], xh, start=False, stop=False)
                            nc.tensor.matmul(out, W[r, 1, 1, w], xh, start=False, stop=False)
                            last = nc.tensor.matmul(out, W[r, 0, 1, w], xl, start=False, stop=True)
                    last.then_inc(pw_done.sem, 1)
                for u in range(2):
                    pe.wait_ge(hp_h.sem, hp_h.now(it, u))
                    pe.wait_ge(hp_l.sem, hp_l.now(it, u))
                    for g in range(NG):
                        last = product5(nc, ps[:, 4 * u + g // 2, (g % 2) * 256:(g % 2) * 256 + 2 * KP], pk[u],
                                        slice(g * P, (g + 1) * P), W, w_at("fft"), False, True, True)
                    last.then_inc(ftd.sem, 1)
                for u in range(2):
                    pe.wait_ge(pq_h.sem, pq_h.now(it, u))
                    pe.wait_ge(pq_l.sem, pq_l.now(it, u))
                    for g in range(NG):
                        for c in range(2):
                            out = ps[:, 4 * u + 2 + g // 2, (g % 2) * 256 + c * KP:(g % 2) * 256 + (c + 1) * KP]
                            cc = slice(c * KP, (c + 1) * KP)
                            nc.tensor.matmul(out, CS[:, 0, c, :], pq[u][0][:, g, cc], start=True, stop=False)
                            nc.tensor.matmul(out, CS[:, 1, c, :], pq[u][0][:, g, cc], start=False, stop=False)
                            last = nc.tensor.matmul(out, CS[:, 0, c, :], pq[u][1][:, g, cc], start=False, stop=True)
                    last.then_inc(fts.sem, 1)
                for u in range(2):
                    pe.wait_ge(n1.sem, n1.now(it, u))
                    transpose_tile(nc, ps, 4 * u, nb[u], ident, t1)
                for u in range(2):
                    pe.wait_ge(p1h.sem, p1h.now(it, u))
                    pe.wait_ge(p1l.sem, p1l.now(it, u))
                    for c in range(2):
                        last = product5(nc, ps[:, 4 * u + 2 + c, :], pk[u], slice(0, N), W, w_at("q", c * P, P), True, True, True)
                    last.then_inc(q_ps.sem, 1)
                    for c in range(2):
                        last = product5(nc, ps[:, 4 * u + c, :], pk[u], slice(0, N), W, w_at("k", c * P, P), True, True, True)
                    last.then_inc(k_ps.sem, 1)
                for u in range(2):
                    pe.wait_ge(q_up.sem, q_up.now(it, u))
                    for g in range(NG):
                        last = product5(nc, ps[:, 4 * u + 2 + g // 2, (g % 2) * 256:(g % 2) * 256 + D], pk[u],
                                        slice(g * P, (g + 1) * P), W, w_at("v"), False, True, True)
                    last.then_inc(v_ps.sem, 1)
                for pg in range(2):
                    for u in range(2):
                        if pg == 0:
                            pe.wait_ge(ka_up.sem, ka_up.now(it, u))
                            pe.wait_ge(kv_up.sem, kv_up.now(it, u))
                            pe.wait_ge(v_up.sem, v_up.now(it, u))
                        else:
                            pe.wait_ge(at.sem, at.now(it, u))
                        for g in range(2):
                            for b in range(2):
                                tok = slice(((2 * pg + g) * 2 + b) * TP, ((2 * pg + g) * 2 + b + 1) * TP)
                                for j in range(PAIRS):
                                    c, r = divmod(j, 4)
                                    f = slice(32 * r, 32 * r + 32)
                                    last = nc.tensor.matmul(
                                        ps[64 * b:64 * b + 64, 4 * u + r, g * 256 + c * P:g * 256 + (c + 1) * P],
                                        q[u][f, c, tok], kx[u][f, c, :, tok], start=True, stop=True)
                        last.then_inc(sc.sem, 1)
                    for u in range(2):
                        pe.wait_ge(sexp.sem, sexp.now(it, 2 * pg + u))
                        for g in range(2):
                            for j in range(PAIRS):
                                k = g * PAIRS + j
                                last = nc.tensor.transpose(ps[:, 4 * u + k // 4, (k % 4) * P:(k % 4 + 1) * P],
                                                           sm[u][:, g, j, :], ident[:, :])
                        last.then_inc(ptt.sem, 1)
                    for u in range(2):
                        pe.wait_ge(pta.sem, pta.now(it, 2 * pg + u))
                        pe.wait_ge(ptv.sem, ptv.now(it, 2 * pg + u))
                        if pg == 0:
                            pe.wait_ge(vd_up.sem, vd_up.now(it, u))
                            pe.wait_ge(vo_up.sem, vo_up.now(it, u))
                        for g in range(2):
                            for b in range(2):
                                for j in range(PAIRS):
                                    k = g * PAIRS + j
                                    last = nc.tensor.matmul(
                                        ps[64 * b:64 * b + 64, 4 * u + 3, k * 34:(k + 1) * 34],
                                        pt[u][:, k, 64 * b:64 * b + 64],
                                        vblk[u][:, 2 * pg + g, b, j, :, :], start=True, stop=True)
                        last.then_inc(pv.sem, 1)
                for u in range(2):
                    pe.wait_ge(at.sem, at.now(it, 2 + u))
                    transpose_tile(nc, ps, 4 * u, nb[u], ident, t2)
                for u in range(2):
                    pe.wait_ge(p2h.sem, p2h.now(it, u))
                    pe.wait_ge(p2l.sem, p2l.now(it, u))
                    for g in range(NG):
                        last = product5(nc, ps[:, 4 * u + 2 + g // 2, (g % 2) * 256:(g % 2) * 256 + D], pk[u],
                                        slice(g * P, (g + 1) * P), W, w_at("proj"), False, True, True)
                    last.then_inc(pr.sem, 1)
                for u in range(2):
                    pe.wait_ge(tt.sem, tt.now(it, u))
                    transpose_tile(nc, ps, 4 * u, nb[u], ident, t3)
                for u in range(2):
                    pe.wait_ge(p3h.sem, p3h.now(it, u))
                    pe.wait_ge(p3l.sem, p3l.now(it, u))
                    for g in range(NG):
                        last = product5(nc, ps[:, 4 * u + 2, g * 16:(g + 1) * 16], pk[u],
                                        slice(g * P, (g + 1) * P), W, w_at("gate"), False, True, True)
                    last.then_inc(gt.sem, 1)
                for u in range(2):
                    router.spread(pe, ps, 4 * u + 3, ident, fwps, it, u)


HID = 3072
CHUNKS = HID // P
LAG = 3


def round_constants(nc, stack, prefix, src, out):
    with ExitStack() as ctx:
        stage = ctx.enter_context(nc.sbuf_tensor(f"{prefix}_stage", list(src.shape), F32))
        loaded = stack.new(f"{prefix}_loaded")
        rounded = stack.new(f"{prefix}_rounded")
        block = ctx.enter_context(nc.Block())

        @block.sync
        def _(sp):
            sp.dma_start(stage[:, :], src).then_inc(loaded, 16)

        @block.vector
        def _(dve):
            dve.wait_ge(loaded, 16)
            nc.vector.tensor_copy(out[:, :], stage[:, :]).then_inc(rounded, 1)


def moe_phase(nc, stack, io, pre, gated, x_in, gates_in, base_in, out):
    halves = 2 if gated else 1
    WAYS = 2 * CHUNKS
    with ExitStack() as ctx:
        sb = lambda n, shape, dt=F32: ctx.enter_context(nc.sbuf_tensor(f"{pre}_sb_{n}", shape, dt))
        sig = lambda n, per=1, step=1, ways=2, credit=False: Signal(nc, stack, f"{pre}_{n}", per, ways, step, credit)
        chunk = lambda n: sig(n, ways=WAYS, credit=True)
        dma = lambda n, credit=False: [sig(f"{n}{u}", 1, 16, 1, credit) for u in range(2)]
        ps = ctx.enter_context(nc.psum_tensor(f"{pre}_ps", [P, 8, 512], F32))
        W1 = sb("W1", [P, 2, 2, halves * HID], F32R)
        W2 = sb("W2", [P, 2, CHUNKS, D], F32R)
        B2 = sb("B2", [64, 2, D], F32R)
        SEL = sb("SEL", [64, HID], F32R)
        b1 = sb("b1", [P, halves, CHUNKS])
        flat = lambda ap: ap.rearrange("p a n -> p (a n)")
        split_weights(nc, stack, f"{pre}w", [
            (io[f"{pre}_w1"].rearrange("p a n -> p (a n)"), flat(W1[:, 0]), flat(W1[:, 1])),
            (io[f"{pre}_w2"].rearrange("p a n -> p (a n)"), flat(W2[:, 0]), flat(W2[:, 1])),
            (io[f"{pre}_b2"], B2[:, 0, :], B2[:, 1, :])])
        round_constants(nc, stack, f"{pre}s", io[f"{pre}_sel"], SEL)
        pk = [sb(f"pk{u}", [P, 3, N], F32R) for u in range(2)]
        fwt = [sb(f"fwt{u}", [64, N], F32R) for u in range(2)]
        hb = [sb(f"hb{u}", [P, NG, D]) for u in range(2)]
        g = [sb(f"g{j}", [P, N]) for j in range(3)]
        s = [sb(f"s{j}", [P, N]) for j in range(2)]
        lin = [sb(f"lin{j}", [P, N]) for j in range(2)]
        hh = [sb(f"hh{j}", [P, N], F32R) for j in range(3)]
        hl = [sb(f"hl{j}", [P, N], F32R) for j in range(3)]
        in_x, in_f, in_b = dma("inx"), dma("inf"), dma("inb")
        stored = dma("st", credit=True)
        consts = stack.new(f"{pre}_consts")
        plus = stack.new(f"{pre}_plus")
        up, act1, mul, gat, high, low = (chunk(n) for n in ("up", "act1", "mul", "gat", "high", "low"))
        pre_g, pre_l, mix, down = (chunk(n) for n in ("preg", "prel", "mix", "down"))
        summed = sig("summed", credit=True)
        block = ctx.enter_context(nc.Block())

        @block.sync
        def _(sp):
            sp.dma_start(b1[:, :, :], io[f"{pre}_b1"]).then_inc(consts, 16)
            with sp.Fori(0, NT // 2) as it:
                for u in range(2):
                    sp.wait_ge(stored[u].sem, stored[u].last(it, 0))
                    sp.sem_inc(stack.passed, 1)
                    sp.wait_ge(down.sem, down.last(it, u * CHUNKS + CHUNKS - 1))
                    sp.sem_inc(stack.passed, 1)
                    sp.dma_start(pk[u][:, :, :].bitcast(F32), x_in[it * 2 + u]).then_inc(in_x[u].sem, 16)
                    sp.dma_start(fwt[u][:, :].bitcast(F32), gates_in[it * 2 + u]).then_inc(in_f[u].sem, 16)
                    sp.dma_start(hb[u][:, :, :], base_in[it * 2 + u]).then_inc(in_b[u].sem, 16)
            for u in range(2):
                sp.wait_ge(stored[u].sem, stored[u].now(NT // 2 - 1, 0))
                sp.sem_inc(stack.passed, 1)

        @block.gpsimd
        def _(pool):
            if gated:
                for sg in (mul, low):
                    sg.credit(pool)
                with pool.Fori(0, NT // 2) as it:
                    for k in range(WAYS + 1):
                        if k < WAYS:
                            pool.wait_ge(act1.sem, act1.now(it, k))
                            nc.gpsimd.tensor_tensor(g[k % 3][:, :], g[k % 3][:, :], s[k % 2][:, :], ALU.mult).then_inc(mul.sem, 1)
                        if k >= 1:
                            j = k - 1
                            pool.wait_ge(high.sem, high.now(it, j))
                            nc.gpsimd.tensor_tensor(hl[j % 3][:, :], g[j % 3][:, :], hh[j % 3][:, :].bitcast(F32),
                                                    ALU.subtract).then_inc(low.sem, 1)

        @block.scalar
        def _(act):
            act.wait_ge(consts, 16)
            for u in range(2):
                stored[u].credit(act)
            act1.credit(act)
            high.credit(act)

            def to_high(it, j):
                act.wait_ge(gat.sem, gat.now(it, j))
                act.wait_ge(down.sem, down.back(it, j - 3))
                nc.scalar.copy(hh[j % 3][:, :], g[j % 3][:, :]).then_inc(high.sem, 1)

            def store(it, u):
                act.wait_ge(summed.sem, summed.now(it, u))
                act.dma_start(out[it * 2 + u], hb[u][:, :, :]).then_inc(stored[u].sem, 16)

            with act.Fori(0, NT // 2) as it:
                for k in range(WAYS + 1):
                    if k < WAYS:
                        if gated:
                            act.wait_ge(pre_g.sem, pre_g.now(it, k))
                            act.wait_ge(mul.sem, mul.back(it, k - 2))
                            nc.scalar.activation(s[k % 2][:, :], g[k % 3][:, :], ACT.Sigmoid, scale=1.702).then_inc(act1.sem, 1)
                        else:
                            act.wait_ge(up.sem, up.now(it, k))
                            act.wait_ge(gat.sem, gat.back(it, k - 2))
                            nc.scalar.activation(s[k % 2][:, :], ps[:, k % 2, :], ACT.Gelu,
                                                 bias=b1[:, 0, k % CHUNKS:k % CHUNKS + 1]).then_inc(act1.sem, 1)
                    if k >= 1:
                        to_high(it, k - 1)
                    if k == CHUNKS + LAG + 1:
                        store(it, 0)
                store(it, 1)

        @block.vector
        def _(dve):
            dve.wait_ge(consts, 16)
            if gated:
                nc.vector.tensor_scalar(b1[:, 1, :], b1[:, 1, :], 1.0, None, ALU.add).then_inc(plus, 1)
                dve.wait_ge(plus, 1)
            for sg in ((pre_g, pre_l, mix, gat) if gated else (low, gat)):
                sg.credit(dve)
            summed.credit(dve)

            def sum_up(it, u):
                dve.wait_ge(down.sem, down.now(it, u * CHUNKS + CHUNKS - 1))
                dve.wait_ge(in_b[u].sem, in_b[u].now(it, 0))
                o = ps[:, 6:8, :].rearrange("p b (h n) -> p b h n", h=2)[:, :, :, 0:D]
                hv = hb[u][:, :, :].rearrange("p (b h) n -> p b h n", b=2)
                nc.vector.tensor_tensor(hv, o, hv, ALU.add).then_inc(summed.sem, 1)

            with dve.Fori(0, NT // 2) as it:
                for k in range(WAYS + 1):
                    c = k % CHUNKS
                    if k < WAYS and gated:
                        dve.wait_ge(up.sem, up.now(it, k))
                        dve.wait_ge(low.sem, low.back(it, k - 3))
                        nc.vector.tensor_scalar(g[k % 3][:, :], ps[:, k % 2, :], b1[:, 0, c:c + 1], 7.0,
                                                ALU.add, ALU.min).then_inc(pre_g.sem, 1)
                        dve.wait_ge(mix.sem, mix.back(it, k - 2))
                        nc.vector.tensor_scalar(lin[k % 2][:, :], ps[:, 2 + k % 2, :], b1[:, 1, c:c + 1], 8.0,
                                                ALU.add, ALU.min).then_inc(pre_l.sem, 1)
                    if k >= 1:
                        j = k - 1
                        if gated:
                            dve.wait_ge(mul.sem, mul.now(it, j))
                            dve.wait_ge(pre_l.sem, pre_l.now(it, j))
                            nc.vector.scalar_tensor_tensor(g[j % 3][:, :], lin[j % 2][:, :], -6.0, g[j % 3][:, :],
                                                           ALU.max, ALU.mult).then_inc(mix.sem, 1)
                            dve.wait_ge(mix.sem, mix.now(it, j))
                            nc.vector.tensor_tensor(g[j % 3][:, :], g[j % 3][:, :], ps[:, 4 + j % 2, :],
                                                    ALU.mult).then_inc(gat.sem, 1)
                        else:
                            dve.wait_ge(act1.sem, act1.now(it, j))
                            dve.wait_ge(low.sem, low.back(it, j - 3))
                            nc.vector.tensor_tensor(g[j % 3][:, :], s[j % 2][:, :], ps[:, 4 + j % 2, :],
                                                    ALU.mult).then_inc(gat.sem, 1)
                            dve.wait_ge(high.sem, high.now(it, j))
                            nc.vector.tensor_tensor(hl[j % 3][:, :], g[j % 3][:, :], hh[j % 3][:, :].bitcast(F32),
                                                    ALU.subtract).then_inc(low.sem, 1)
                    if k == CHUNKS + LAG:
                        sum_up(it, 0)
                sum_up(it, 1)

        @block.tensor
        def _(pe):
            for sg in (up, down):
                sg.credit(pe)

            def first(it, k):
                u, c = divmod(k, CHUNKS)
                if c == 0:
                    pe.wait_ge(in_x[u].sem, in_x[u].now(it, 0))
                    pe.wait_ge(in_f[u].sem, in_f[u].now(it, 0))
                if gated:
                    pe.wait_ge(pre_l.sem, pre_l.back(it, k - 2))
                else:
                    pe.wait_ge(act1.sem, act1.back(it, k - 2))
                for h in range(halves):
                    at = (c * halves + h) * P
                    product5(nc, ps[:, 2 * h + k % 2, :], pk[u], slice(0, N), W1, slice(at, at + P), True, True, True)
                pe.wait_ge(gat.sem, gat.back(it, k - 2))
                nc.tensor.matmul(ps[:, 4 + k % 2, :], SEL[:, c * P:(c + 1) * P], fwt[u][:, :],
                                 start=True, stop=True).then_inc(up.sem, 1)

            def second(it, k):
                u, c = divmod(k, CHUNKS)
                outs = [ps[:, 6 + t // 2, (t % 2) * 256:(t % 2) * 256 + D] for t in range(NG)]
                if c == 0:
                    pe.wait_ge(summed.sem, summed.back(it, u - 1))
                    for t in range(NG):
                        for hlw in range(2):
                            nc.tensor.matmul(outs[t], fwt[u][:, t * P:(t + 1) * P], B2[:, hlw, :],
                                             start=t % 2 == 0 and hlw == 0, stop=False, skip_group_check=True)
                pe.wait_ge(high.sem, high.now(it, k))
                pe.wait_ge(low.sem, low.now(it, k))
                for t in range(NG):
                    tok = slice(t * P, (t + 1) * P)
                    for a, hlw in ((hh, 0), (hh, 1), (hl, 0)):
                        last = nc.tensor.matmul(outs[t], a[k % 3][:, tok], W2[:, hlw, c, :], start=False,
                                                stop=c == CHUNKS - 1 and a is hl, skip_group_check=True)
                last.then_inc(down.sem, 1)

            with pe.Fori(0, NT // 2) as it:
                for k in range(WAYS + LAG):
                    if k < WAYS:
                        first(it, k)
                    if k >= LAG:
                        second(it, k - LAG)


KEYS = N + N // 2
KF = 4 * D
KFC = KF // P


def phase_c(nc, stack, io):
    with ExitStack() as ctx:
        sb = lambda n, shape, dt=F32: ctx.enter_context(nc.sbuf_tensor(f"c_sb_{n}", shape, dt))
        two = lambda n, shape, dt=F32: [sb(f"{n}{u}", shape, dt) for u in range(2)]
        sig = lambda n, per=1, step=1, ways=2, credit=False: Signal(nc, stack, f"c_{n}", per, ways, step, credit)
        dma = lambda n, credit=False: [sig(f"{n}{u}", 1, 16, 1, credit) for u in range(2)]
        ps = ctx.enter_context(nc.psum_tensor("c_ps", [P, 8, 512], F32))
        W = sb("W", [P, 2, 2, C_TOT], F32R)
        WV = sb("WV", [P, 2, KFC, D], F32R)
        rows = sb("rows", [P, len(C_ROW), D])
        decay, bonus = sb("decay", [P, KEYS]), sb("bonus", [P, KEYS])
        ident = sb("ident", [P, P])
        half = sb("half", [P, NG])
        flat = lambda ap: ap.rearrange("p a n -> p (a n)")
        split_weights(nc, stack, "cw", [
            (flat(io["c_w"]), flat(W[:, 0]), flat(W[:, 1])),
            (flat(io["c_wv"]), flat(WV[:, 0]), flat(WV[:, 1]))])
        pk = two("pk", [P, 3, N], F32R)
        hb, xb, nb = two("hb", [P, NG, D]), two("xb", [P, NG, D]), two("nb", [P, NG, D])
        kk, vv, er = two("kk", [P, KEYS]), two("vv", [P, KEYS]), two("er", [P, KEYS])
        ms, sa, sb_ = (two(n, [P, 2, KEYS + 1]) for n in ("ms", "sa", "sbb"))
        e1, e2 = two("e1", [P, 2, KEYS]), two("e2", [P, 2, KEYS])
        t1, t2 = two("t1", [P, KEYS]), two("t2", [P, KEYS])
        yh, yl = two("yh", [P, KEYS], F32R), two("yl", [P, KEYS], F32R)
        rl = [sb(f"rl{j}", [P, N]) for j in range(2)]
        fh = [sb(f"fh{j}", [P, N], F32R) for j in range(2)]
        fl = [sb(f"fl{j}", [P, N], F32R) for j in range(2)]
        st, mv = two("st", [P, NG, 6]), two("mv", [P, NG, 2])
        ra, rb, rs, rc = (two(n, [P, NG]) for n in ("ra", "rb", "rs", "rc"))
        fwt = two("fwt", [64, N], F32R)
        router = Router(nc, stack, ctx, "cr", 4, 1)

        consts = stack.new("c_consts")
        identity = stack.new("c_identity")
        setup, cleared = (stack.new(n) for n in ("c_setup", "c_cleared"))
        loaded = dma("loaded")
        st_pk, st_fw, st_base = dma("stpk", True), dma("stfw", True), dma("stbase", True)
        s1, m1, pl1, n3, l1, l1w, l1b = sig("s1", 4), sig("m1", 4), sig("pl1", 7), sig("n3", 4), sig("l1", 4), sig("l1w"), sig("l1b")
        tr1, p1h, p1l = sig("tr1"), sig("p1h", 2), sig("p1l", 2)
        k_ps, v_ps, r_ps = sig("kps"), sig("vps"), sig("rps")
        k_up, v_up, r_up, kpad = sig("kup", 3), sig("vup", 3), sig("rup", 3), sig("kpad")
        mscan, x1a, x1b, x2, kb = sig("mscan", 2), sig("x1a", 2), sig("x1b", 2), sig("x2", 2), sig("kb")
        ex1, ex2, ev, ascan, bscan = sig("ex1", 2), sig("ex2", 2), sig("ev", 2), sig("ascan", 2), sig("bscan", 2)
        mm, df, exd, wa, wb, wv_ = sig("mm", 2), sig("df", 3), sig("exd", 3), sig("wa", 2), sig("wb", 2), sig("wv")
        nsum, dsum, den, dinv, yy, y_h, y_l = sig("nsum", 2), sig("dsum", 2), sig("den"), sig("dinv"), sig("yy"), sig("yh"), sig("yl")
        o_ps, x_up = sig("ops"), sig("xup")
        s2, m2, pl2, l2, l2w, l2b = sig("s2", 4), sig("m2", 4), sig("pl2", 2), sig("l2", 4), sig("l2w"), sig("l2b")
        tr2, p2h, p2l = sig("tr2"), sig("p2h", 2), sig("p2l", 2)
        g_ps, g_ex, g_kv, x2_up, h_up = sig("gps"), sig("gex"), sig("gkv"), sig("x2up"), sig("hup")
        seq = lambda n: sig(n, ways=2 * KFC, credit=True)
        f_ps, f_relu, f_sq, f_h, f_l, f_used = (seq(n) for n in ("fps", "frelu", "fsq", "fh", "fl", "fused"))
        s3, m3, pl3, n4 = sig("s3", 4), sig("m3", 4), sig("pl3", 2), sig("n4", 4)
        tr3, p3h, p3l = sig("tr3"), sig("p3h", 2), sig("p3l", 2)
        gt, fwps, fwh, fwl = sig("gt"), sig("fwps"), sig("fwh"), sig("fwl")
        block = ctx.enter_context(nc.Block())
        row = lambda n: rows[:, C_ROW[n], :]
        w_at = lambda n, a=0, m=None: slice(C_AT[n][0] + a, C_AT[n][0] + a + (m or C_AT[n][1]))
        before = lambda x, d: x[:, d, 0:KEYS] if d == 0 else x[:, d, 1:KEYS + 1]
        after = lambda x, d: x[:, d, 1:KEYS + 1] if d == 0 else x[:, d, 0:KEYS]

        def scan(out, d0, d1, initial, op0, op1, d):
            if d == 1:
                out, d0, d1 = out[:, ::-1], d0[:, ::-1], d1[:, ::-1]
            return nc.vector.tensor_tensor_scan(out, d0, d1, initial, op0=op0, op1=op1)

        def two_banks(u, b0, n):
            return ps[:, 4 * u + b0:4 * u + b0 + 2, :].rearrange("p b (h n) -> p b h n", h=2)[:, :, :, 0:n]

        def split4(ap):
            return ap.rearrange("p (b h) n -> p b h n", b=2)

        @block.sync
        def _(sp):
            sp.dma_start(rows[:, :, :], io["c_rows"]).then_inc(consts, 16)
            sp.dma_start(decay[:, :], io["c_decay"]).then_inc(consts, 16)
            sp.dma_start(bonus[:, :], io["c_bonus"]).then_inc(consts, 16)
            for s in (*st_base, *st_pk, *st_fw):
                s.credit(sp)
            with sp.Fori(0, NT // 2) as it:
                for u in range(2):
                    sp.wait_ge(st_base[u].sem, st_base[u].last(it, 0))
                    sp.sem_inc(stack.passed, 1)
                    sp.dma_start(hb[u][:, :, :], io["h2"][it * 2 + u]).then_inc(loaded[u].sem, 16)
                for u in range(2):
                    sp.wait_ge(h_up.sem, h_up.now(it, u))
                    sp.sem_inc(stack.passed, 1)
                    sp.dma_start(io["h3"][it * 2 + u], hb[u][:, :, :]).then_inc(st_base[u].sem, 16)
                for u in range(2):
                    sp.wait_ge(p3h.sem, p3h.now(it, u))
                    sp.sem_inc(stack.passed, 1)
                    sp.wait_ge(p3l.sem, p3l.now(it, u))
                    sp.sem_inc(stack.passed, 1)
                    sp.dma_start(io["tp2"][it * 2 + u], pk[u][:, :, :].bitcast(F32)).then_inc(st_pk[u].sem, 16)
                for u in range(2):
                    sp.wait_ge(fwh.sem, fwh.now(it, u))
                    sp.sem_inc(stack.passed, 1)
                    sp.wait_ge(fwl.sem, fwl.now(it, u))
                    sp.sem_inc(stack.passed, 1)
                    sp.dma_start(io["fw2"][it * 2 + u], fwt[u][:, :].bitcast(F32)).then_inc(st_fw[u].sem, 16)
            for u in range(2):
                for s in (st_base, st_pk, st_fw):
                    sp.wait_ge(s[u].sem, s[u].now(NT // 2 - 1, 0))
                    sp.sem_inc(stack.passed, 1)

        @block.gpsimd
        def _(pool):
            fill_identity(nc, pool, ident, identity)
            nc.gpsimd.memset(half[:, :], -0.5).then_inc(setup, 1)
            pool.wait_ge(setup, 1)

            def power(out, x, s):
                nc.gpsimd.tensor_tensor(out[:, :], x[:, :], half[:, :], ALU.pow).then_inc(s.sem, 1)

            with pool.Fori(0, NT // 2) as it:
                for u in range(2):
                    var = mv[u][:, :, 1]
                    pool.wait_ge(m1.sem, m1.now(it, u))
                    pool.sem_inc(stack.passed, 1)
                    nc.gpsimd.tensor_scalar(ra[u][:, :], var, EPS, None, ALU.add).then_inc(pl1.sem, 1)
                    pool.wait_ge(pl1.sem, pl1.now(it, u, 1))
                    power(rs[u], ra[u], pl1)
                    pool.wait_ge(pl1.sem, pl1.now(it, u, 2))
                    nc.gpsimd.tensor_tensor(rb[u][:, :], rs[u][:, :], rs[u][:, :], ALU.mult).then_inc(pl1.sem, 1)
                    pool.wait_ge(pl1.sem, pl1.now(it, u, 3))
                    nc.gpsimd.tensor_tensor(rb[u][:, :], rb[u][:, :], var, ALU.mult).then_inc(pl1.sem, 1)
                    pool.wait_ge(pl1.sem, pl1.now(it, u, 4))
                    pool.sem_inc(stack.passed, 1)
                    nc.gpsimd.tensor_scalar(rb[u][:, :], rb[u][:, :], EPS, None, ALU.add).then_inc(pl1.sem, 1)
                    pool.wait_ge(pl1.sem, pl1.now(it, u, 5))
                    power(ra[u], rb[u], pl1)
                    pool.wait_ge(pl1.sem, pl1.now(it, u, 6))
                    nc.gpsimd.tensor_tensor(rc[u][:, :], rs[u][:, :], ra[u][:, :], ALU.mult).then_inc(pl1.sem, 1)
                for u in range(2):
                    pool.wait_ge(kpad.sem, kpad.now(it, u))
                    for d in range(2):
                        pool.wait_ge(mscan.sem, mscan.now(it, u, d + 1))
                        nc.gpsimd.tensor_tensor(e2[u][:, d, :], kk[u][:, :], after(ms[u], d), ALU.subtract).then_inc(x2.sem, 1)
                    pool.wait_ge(ev.sem, ev.now(it, u, 2))
                    pool.wait_ge(ascan.sem, ascan.now(it, u, 2))
                    nc.gpsimd.tensor_tensor(t1[u][:, :], kk[u][:, :], bonus[:, :], ALU.add).then_inc(kb.sem, 1)
                for u in range(2):
                    for d in range(2):
                        pool.wait_ge(exd.sem, exd.now(it, u, d + 1))
                        pool.wait_ge(bscan.sem, bscan.now(it, u, d + 1))
                        x = before(sb_[u], d)
                        nc.gpsimd.tensor_tensor(x, x, e1[u][:, d, :], ALU.mult).then_inc(wb.sem, 1)
                    pool.wait_ge(wb.sem, wb.now(it, u, 2))
                    nc.gpsimd.tensor_tensor(e2[u][:, 0, :], before(sb_[u], 1), before(sb_[u], 0), ALU.add).then_inc(dsum.sem, 1)
                    pool.wait_ge(dsum.sem, dsum.now(it, u, 1))
                    pool.wait_ge(exd.sem, exd.now(it, u, 3))
                    nc.gpsimd.tensor_tensor(e2[u][:, 0, :], e2[u][:, 0, :], t1[u][:, :], ALU.add).then_inc(dsum.sem, 1)
                for (m, pl) in ((m2, pl2), (m3, pl3)):
                    for u in range(2):
                        pool.wait_ge(m.sem, m.now(it, u))
                        pool.sem_inc(stack.passed, 1)
                        nc.gpsimd.tensor_scalar(ra[u][:, :], mv[u][:, :, 1], EPS, None, ALU.add).then_inc(pl.sem, 1)
                        pool.wait_ge(pl.sem, pl.now(it, u, 1))
                        power(rs[u], ra[u], pl)

        @block.vector
        def _(dve):
            dve.wait_ge(consts, 48)
            router.start(dve)
            live = lambda x: x[:, :].rearrange("p (b s) -> p b s", s=TP)[:, :, 0:T]
            nc.vector.tensor_scalar(live(decay), live(decay), 1.0 / T, None, ALU.mult).then_inc(cleared, 1)
            nc.vector.tensor_scalar(live(bonus), live(bonus), 1.0 / T, None, ALU.mult).then_inc(cleared, 1)
            for u in range(2):
                nc.vector.memset(fwt[u][:, :].bitcast(F32), 0.0).then_inc(cleared, 1)
                for x, v in ((ms, NEG), (sa, 0.0), (sb_, 0.0)):
                    nc.vector.memset(x[u][:, 0, 0:1], v).then_inc(cleared, 1)
                    nc.vector.memset(x[u][:, 1, KEYS:KEYS + 1], v).then_inc(cleared, 1)
            dve.wait_ge(setup, 1)
            dve.wait_ge(cleared, 16)
            for s in (f_sq, f_l):
                s.credit(dve)
            TT = nc.vector.tensor_tensor
            with dve.Fori(0, NT // 2) as it:
                for u in range(2):
                    dve.wait_ge(loaded[u].sem, loaded[u].now(it, 0))
                    norm_stats(nc, stack, dve, hb[u], st[u], mv[u], s1, m1, it, u)
                for u in range(2):
                    dve.wait_ge(pl1.sem, pl1.now(it, u))
                    norm_apply(nc, nb[u], hb[u], mv[u], rc[u], l1)
                for u in range(2):
                    dve.wait_ge(l1.sem, l1.now(it, u))
                    TT(nb[u][:, :, :], nb[u][:, :, :], bcast_groups(row("ln1w")), ALU.mult).then_inc(l1w.sem, 1)
                for u in range(2):
                    dve.wait_ge(l1w.sem, l1w.now(it, u))
                    TT(nb[u][:, :, :], nb[u][:, :, :], bcast_groups(row("ln1b")), ALU.add).then_inc(l1b.sem, 1)
                for u in range(2):
                    norm_apply(nc, xb[u], hb[u], mv[u], rs[u], n3)
                for u in range(2):
                    dve.wait_ge(tr1.sem, tr1.now(it, u))
                    pack_low(nc, dve, ps, 4 * u, pk[u], p1h, p1l, it, u)
                for u in range(2):
                    dve.wait_ge(k_up.sem, k_up.now(it, u))
                    nc.vector.memset(kk[u][:, :].rearrange("p (b s) -> p b s", s=TP)[:, :, T:TP], NEG).then_inc(kpad.sem, 1)
                for u in range(2):
                    dve.wait_ge(kpad.sem, kpad.now(it, u))
                    for d in range(2):
                        scan(after(ms[u], d), decay[:, :], kk[u][:, :], NEG, ALU.add, ALU.max, d).then_inc(mscan.sem, 1)
                for u in range(2):
                    for d in range(2):
                        dve.wait_ge(mscan.sem, mscan.now(it, u, d + 1))
                        TT(e1[u][:, d, :], before(ms[u], d), decay[:, :], ALU.add).then_inc(x1a.sem, 1)
                    for d in range(2):
                        dve.wait_ge(x1a.sem, x1a.now(it, u, d + 1))
                        TT(e1[u][:, d, :], e1[u][:, d, :], after(ms[u], d), ALU.subtract).then_inc(x1b.sem, 1)
                for u in range(2):
                    for d in range(2):
                        dve.wait_ge(ex1.sem, ex1.now(it, u, d + 1))
                        dve.wait_ge(ex2.sem, ex2.now(it, u, d + 1))
                        scan(after(sb_[u], d), e1[u][:, d, :], e2[u][:, d, :], 0.0, ALU.mult, ALU.add, d).then_inc(bscan.sem, 1)
                        dve.wait_ge(v_up.sem, v_up.now(it, u))
                        if d == 1:
                            dve.wait_ge(ascan.sem, ascan.now(it, u, 1))
                        TT(t1[u][:, :], e2[u][:, d, :], vv[u][:, :], ALU.mult).then_inc(ev.sem, 1)
                        dve.wait_ge(ev.sem, ev.now(it, u, d + 1))
                        scan(after(sa[u], d), e1[u][:, d, :], t1[u][:, :], 0.0, ALU.mult, ALU.add, d).then_inc(ascan.sem, 1)
                for u in range(2):
                    TT(t2[u][:, :], before(ms[u], 0), before(ms[u], 1), ALU.max).then_inc(mm.sem, 1)
                    dve.wait_ge(kb.sem, kb.now(it, u))
                    dve.wait_ge(mm.sem, mm.now(it, u, 1))
                    TT(t2[u][:, :], t2[u][:, :], t1[u][:, :], ALU.max).then_inc(mm.sem, 1)
                    dve.wait_ge(mm.sem, mm.now(it, u, 2))
                    dve.wait_ge(ascan.sem, ascan.now(it, u))
                    dve.wait_ge(bscan.sem, bscan.now(it, u))
                    for d in range(2):
                        TT(e1[u][:, d, :], before(ms[u], d), t2[u][:, :], ALU.subtract).then_inc(df.sem, 1)
                    TT(t1[u][:, :], t1[u][:, :], t2[u][:, :], ALU.subtract).then_inc(df.sem, 1)
                for u in range(2):
                    for d in range(2):
                        dve.wait_ge(exd.sem, exd.now(it, u, d + 1))
                        TT(before(sa[u], d), before(sa[u], d), e1[u][:, d, :], ALU.mult).then_inc(wa.sem, 1)
                    dve.wait_ge(exd.sem, exd.now(it, u, 3))
                    TT(vv[u][:, :], vv[u][:, :], t1[u][:, :], ALU.mult).then_inc(wv_.sem, 1)
                    for d in range(2):
                        dve.wait_ge(wa.sem, wa.now(it, u, d + 1))
                        if d == 0:
                            dve.wait_ge(wv_.sem, wv_.now(it, u))
                        else:
                            dve.wait_ge(nsum.sem, nsum.now(it, u, 1))
                        TT(vv[u][:, :], vv[u][:, :], before(sa[u], d), ALU.add).then_inc(nsum.sem, 1)
                for u in range(2):
                    dve.wait_ge(dsum.sem, dsum.now(it, u))
                    dve.wait_ge(r_up.sem, r_up.now(it, u))
                    nc.vector.scalar_tensor_tensor(t2[u][:, :], er[u][:, :], 1.0, e2[u][:, 0, :], ALU.add, ALU.mult).then_inc(den.sem, 1)
                    dve.wait_ge(den.sem, den.now(it, u))
                    nc.vector.reciprocal(t2[u][:, :], t2[u][:, :]).then_inc(dinv.sem, 1)
                    dve.wait_ge(dinv.sem, dinv.now(it, u))
                    dve.wait_ge(nsum.sem, nsum.now(it, u))
                    TT(t1[u][:, :], vv[u][:, :], t2[u][:, :], ALU.mult).then_inc(yy.sem, 1)
                for u in range(2):
                    dve.wait_ge(y_h.sem, y_h.now(it, u))
                    TT(yl[u][:, :], t1[u][:, :], yh[u][:, :].bitcast(F32), ALU.subtract).then_inc(y_l.sem, 1)
                for u in range(2):
                    dve.wait_ge(o_ps.sem, o_ps.now(it, u))
                    dve.wait_ge(n3.sem, n3.now(it, u))
                    TT(split4(xb[u][:, :, :]), two_banks(u, 0, D), split4(xb[u][:, :, :]), ALU.add).then_inc(x_up.sem, 1)
                for u in range(2):
                    dve.wait_ge(x_up.sem, x_up.now(it, u))
                    norm_stats(nc, stack, dve, xb[u], st[u], mv[u], s2, m2, it, u)
                for u in range(2):
                    dve.wait_ge(pl2.sem, pl2.now(it, u))
                    norm_apply(nc, nb[u], xb[u], mv[u], rs[u], l2)
                for u in range(2):
                    dve.wait_ge(l2.sem, l2.now(it, u))
                    TT(nb[u][:, :, :], nb[u][:, :, :], bcast_groups(row("ln2w")), ALU.mult).then_inc(l2w.sem, 1)
                for u in range(2):
                    dve.wait_ge(l2w.sem, l2w.now(it, u))
                    TT(nb[u][:, :, :], nb[u][:, :, :], bcast_groups(row("ln2b")), ALU.add).then_inc(l2b.sem, 1)
                for u in range(2):
                    dve.wait_ge(tr2.sem, tr2.now(it, u))
                    pack_low(nc, dve, ps, 4 * u + 2, pk[u], p2h, p2l, it, u)
                for k in range(2 * KFC + 1):
                    if k < 2 * KFC:
                        dve.wait_ge(f_relu.sem, f_relu.now(it, k))
                        TT(rl[k % 2][:, :], rl[k % 2][:, :], rl[k % 2][:, :], ALU.mult).then_inc(f_sq.sem, 1)
                    if k >= 1:
                        j = k - 1
                        dve.wait_ge(f_h.sem, f_h.now(it, j))
                        TT(fl[j % 2][:, :], rl[j % 2][:, :], fh[j % 2][:, :].bitcast(F32), ALU.subtract).then_inc(f_l.sem, 1)
                for u in range(2):
                    dve.wait_ge(f_used.sem, f_used.now(it, u * KFC + KFC - 1))
                    dve.wait_ge(g_ex.sem, g_ex.now(it, u))
                    TT(split4(nb[u][:, :, :]), two_banks(u, 0, D), split4(nb[u][:, :, :]), ALU.mult).then_inc(g_kv.sem, 1)
                    dve.wait_ge(g_kv.sem, g_kv.now(it, u))
                    TT(xb[u][:, :, :], xb[u][:, :, :], nb[u][:, :, :], ALU.add).then_inc(x2_up.sem, 1)
                    dve.wait_ge(x2_up.sem, x2_up.now(it, u))
                    TT(hb[u][:, :, :], hb[u][:, :, :], xb[u][:, :, :], ALU.add).then_inc(h_up.sem, 1)
                for u in range(2):
                    dve.wait_ge(h_up.sem, h_up.now(it, u))
                    norm_stats(nc, stack, dve, hb[u], st[u], mv[u], s3, m3, it, u)
                for u in range(2):
                    dve.wait_ge(pl3.sem, pl3.now(it, u))
                    norm_apply(nc, nb[u], hb[u], mv[u], rs[u], n4)
                for u in range(2):
                    dve.wait_ge(tr3.sem, tr3.now(it, u))
                    pack_low(nc, dve, ps, 4 * u + 2, pk[u], p3h, p3l, it, u)
                for u in range(2):
                    dve.wait_ge(gt.sem, gt.now(it, u))
                    router.choose(dve, ps[:, 4 * u, 0:NG * 16].rearrange("p (g e) -> p g e", g=NG)[:, :, 0:4], row("gateb"), it, u)
                for u in range(2):
                    dve.wait_ge(fwh.sem, fwh.now(it, u))
                    TT(fwt[u][32:48, :], ps[0:16, 4 * u + 1, :], fwt[u][0:16, :].bitcast(F32), ALU.subtract).then_inc(fwl.sem, 1)
                for u in range(2):
                    dve.wait_ge(st_pk[u].sem, st_pk[u].now(it, 0))
                    dve.wait_ge(st_fw[u].sem, st_fw[u].now(it, 0))

        @block.scalar
        def _(act):
            act.wait_ge(consts, 48)
            act.wait_ge(cleared, 16)
            for s in (f_relu, f_h):
                s.credit(act)

            def unfold(u, bank, out, sg, func=ACT.Copy, scale=1.0):
                h = N // 2
                for o, i in ((out[:, 0:N], ps[:, bank, :]), (out[0:D2, N:KEYS], ps[0:D2, bank + 1, 0:h]),
                             (out[D2:P, N:KEYS], ps[D2:P, bank + 1, h:N])):
                    nc.scalar.activation(o, i, func, scale=scale).then_inc(sg.sem, 1)

            with act.Fori(0, NT // 2) as it:
                for u in range(2):
                    act.wait_ge(tr1.sem, tr1.now(it, u))
                    pack_high(nc, ps, 4 * u, pk[u], p1h)
                for u in range(2):
                    act.wait_ge(k_ps.sem, k_ps.now(it, u))
                    unfold(u, 4 * u + 2, kk[u], k_up)
                for u in range(2):
                    act.wait_ge(v_ps.sem, v_ps.now(it, u))
                    unfold(u, 4 * u, vv[u], v_up)
                for u in range(2):
                    act.wait_ge(r_ps.sem, r_ps.now(it, u))
                    unfold(u, 4 * u + 2, er[u], r_up, ACT.Exp, -1.0)
                for u in range(2):
                    for d in range(2):
                        act.wait_ge(x2.sem, x2.now(it, u, d + 1))
                        nc.scalar.activation(e2[u][:, d, :], e2[u][:, d, :], ACT.Exp).then_inc(ex2.sem, 1)
                        act.wait_ge(x1b.sem, x1b.now(it, u, d + 1))
                        nc.scalar.activation(e1[u][:, d, :], e1[u][:, d, :], ACT.Exp).then_inc(ex1.sem, 1)
                for u in range(2):
                    for d in range(2):
                        act.wait_ge(df.sem, df.now(it, u, d + 1))
                        nc.scalar.activation(e1[u][:, d, :], e1[u][:, d, :], ACT.Exp).then_inc(exd.sem, 1)
                    act.wait_ge(df.sem, df.now(it, u, 3))
                    nc.scalar.activation(t1[u][:, :], t1[u][:, :], ACT.Exp).then_inc(exd.sem, 1)
                for u in range(2):
                    act.wait_ge(yy.sem, yy.now(it, u))
                    nc.scalar.copy(yh[u][:, :], t1[u][:, :]).then_inc(y_h.sem, 1)
                for u in range(2):
                    act.wait_ge(tr2.sem, tr2.now(it, u))
                    pack_high(nc, ps, 4 * u + 2, pk[u], p2h)
                for u in range(2):
                    act.wait_ge(g_ps.sem, g_ps.now(it, u))
                    nc.scalar.activation(split4(nb[u][:, :, :]), two_banks(u, 0, D), ACT.Sigmoid).then_inc(g_ex.sem, 1)
                for k in range(2 * KFC + 1):
                    if k < 2 * KFC:
                        act.wait_ge(f_ps.sem, f_ps.now(it, k))
                        act.wait_ge(f_l.sem, f_l.back(it, k - 2))
                        u = k // KFC
                        nc.scalar.activation(rl[k % 2][:, :], ps[:, 4 * u + 2 + k % 2, :], ACT.Relu).then_inc(f_relu.sem, 1)
                    if k >= 1:
                        j = k - 1
                        act.wait_ge(f_sq.sem, f_sq.now(it, j))
                        act.wait_ge(f_used.sem, f_used.back(it, j - 2))
                        nc.scalar.copy(fh[j % 2][:, :], rl[j % 2][:, :]).then_inc(f_h.sem, 1)
                for u in range(2):
                    act.wait_ge(tr3.sem, tr3.now(it, u))
                    pack_high(nc, ps, 4 * u + 2, pk[u], p3h)
                for u in range(2):
                    act.wait_ge(fwps.sem, fwps.now(it, u))
                    nc.scalar.copy(fwt[u][0:16, :], ps[0:16, 4 * u + 1, :]).then_inc(fwh.sem, 1)
                for u in range(2):
                    act.wait_ge(st_pk[u].sem, st_pk[u].now(it, 0))
                    act.wait_ge(st_fw[u].sem, st_fw[u].now(it, 0))

        @block.tensor
        def _(pe):
            pe.wait_ge(identity, 2)
            pe.wait_ge(cleared, 16)
            for s in (f_ps, f_used):
                s.credit(pe)

            def feature_major(u, b0, name, sg):
                for c in range(2):
                    last = product5(nc, ps[:, 4 * u + b0 + c, :], pk[u], slice(0, N), W, w_at(name, c * P, P), True, True, True)
                last.then_inc(sg.sem, 1)

            with pe.Fori(0, NT // 2) as it:
                for u in range(2):
                    pe.wait_ge(l1b.sem, l1b.now(it, u))
                    transpose_tile(nc, ps, 4 * u, nb[u], ident, tr1)
                for u in range(2):
                    pe.wait_ge(p1h.sem, p1h.now(it, u))
                    pe.wait_ge(p1l.sem, p1l.now(it, u))
                    feature_major(u, 2, "wk", k_ps)
                for u in range(2):
                    feature_major(u, 0, "wv", v_ps)
                for u in range(2):
                    pe.wait_ge(k_up.sem, k_up.now(it, u))
                    feature_major(u, 2, "wr", r_ps)
                for u in range(2):
                    pe.wait_ge(y_h.sem, y_h.now(it, u))
                    pe.wait_ge(y_l.sem, y_l.now(it, u))
                    for g in range(NG):
                        out = ps[:, 4 * u + g // 2, (g % 2) * 256:(g % 2) * 256 + D]
                        tok = slice(g * P, (g + 1) * P)
                        r = slice(D2 * (g // 2), D2 * (g // 2) + D2)
                        tail = slice(N + (g % 2) * P, N + (g % 2 + 1) * P)
                        w = w_at("wo")
                        steps = [(yh[u][:, tok], W[:, 0, 0, w]), (yh[u][:, tok], W[:, 1, 0, w]), (yl[u][:, tok], W[:, 0, 0, w]),
                                 (yh[u][r, tail], W[r, 0, 1, w]), (yh[u][r, tail], W[r, 1, 1, w]), (yl[u][r, tail], W[r, 0, 1, w])]
                        for n, (a, b) in enumerate(steps):
                            last = nc.tensor.matmul(out, a, b, start=n == 0, stop=n == 5)
                    last.then_inc(o_ps.sem, 1)
                for u in range(2):
                    pe.wait_ge(l2b.sem, l2b.now(it, u))
                    pe.wait_ge(r_up.sem, r_up.now(it, u))
                    transpose_tile(nc, ps, 4 * u + 2, nb[u], ident, tr2)
                for u in range(2):
                    pe.wait_ge(p2h.sem, p2h.now(it, u))
                    pe.wait_ge(p2l.sem, p2l.now(it, u))
                    for g in range(NG):
                        last = product5(nc, ps[:, 4 * u + g // 2, (g % 2) * 256:(g % 2) * 256 + D], pk[u],
                                        slice(g * P, (g + 1) * P), W, w_at("rf"), False, True, True)
                    last.then_inc(g_ps.sem, 1)

                def hidden(k):
                    u, c = divmod(k, KFC)
                    pe.wait_ge(f_relu.sem, f_relu.back(it, k - 2))
                    product5(nc, ps[:, 4 * u + 2 + k % 2, :], pk[u], slice(0, N), W,
                             w_at("kf", c * P, P), True, True, True).then_inc(f_ps.sem, 1)

                def values(k):
                    u, c = divmod(k, KFC)
                    if c == 0:
                        pe.wait_ge(g_ex.sem, g_ex.now(it, u))
                    pe.wait_ge(f_h.sem, f_h.now(it, k))
                    pe.wait_ge(f_l.sem, f_l.now(it, k))
                    for g in range(NG):
                        tok = slice(g * P, (g + 1) * P)
                        out = ps[:, 4 * u + g // 2, (g % 2) * 256:(g % 2) * 256 + D]
                        for n, (a, hlw) in enumerate(((fh, 0), (fh, 1), (fl, 0))):
                            last = nc.tensor.matmul(out, a[k % 2][:, tok], WV[:, hlw, c, :],
                                                    start=c == 0 and n == 0 and g % 2 == 0, stop=c == KFC - 1 and n == 2,
                                                    skip_group_check=True)
                    last.then_inc(f_used.sem, 1)

                for k in range(2 * KFC + 2):
                    if k < 2 * KFC:
                        hidden(k)
                    if k >= 2:
                        values(k - 2)
                for u in range(2):
                    pe.wait_ge(n4.sem, n4.now(it, u))
                    transpose_tile(nc, ps, 4 * u + 2, nb[u], ident, tr3)
                for u in range(2):
                    pe.wait_ge(p3h.sem, p3h.now(it, u))
                    pe.wait_ge(p3l.sem, p3l.now(it, u))
                    for g in range(NG):
                        last = product5(nc, ps[:, 4 * u, g * 16:(g + 1) * 16], pk[u],
                                        slice(g * P, (g + 1) * P), W, w_at("gate"), False, True, True)
                    last.then_inc(gt.sem, 1)
                for u in range(2):
                    router.spread(pe, ps, 4 * u + 1, ident, fwps, it, u)


def build(nc, io):
    phases = (
        lambda stack: phase_a(nc, stack, io),
        lambda stack: moe_phase(nc, stack, io, "b", True, io["tp"], io["fw"], io["base"], io["h2"]),
        lambda stack: phase_c(nc, stack, io),
        lambda stack: moe_phase(nc, stack, io, "d", False, io["tp2"], io["fw2"], io["h3"], io["out"]),
    )
    for n, phase in enumerate(phases):
        stack = Semaphores(nc, n)
        phase(stack)
        stack.end()



SPECTRUM = list(range(KC)) + [D - j for j in range(1, KC - 1)]


def _parts(w):
    w = np.asarray(w)
    return np.stack([w[:P], np.concatenate([w[P:], w[P:]])], axis=1)


def _outs(w):
    return np.concatenate([w, w[:, P:]], axis=1)


def _twice(v):
    return np.concatenate([v[P:], v[P:]])


def _shape_constants():
    d, k = np.arange(D)[:, None], np.arange(KC)[None]
    ang = 2 * np.pi * ((d * k) % D) / D
    fft = np.zeros((D, 2 * KP))
    fft[:, :KC], fft[:, KP:KP + KC] = np.cos(ang), np.sin(ang)
    fft[:, KP], fft[:, KP + KC - 1] = 0, 0
    t = np.arange(T)
    ang = 2 * np.pi * ((t[:, None] * t[None]) % T) / T
    dft_t = np.zeros((2, TP, 2, 2, TP))
    for b in range(2):
        dft_t[b, :T, 0, b, :T] = np.cos(ang)
        dft_t[b, :T, 1, b, :T] = np.sin(ang)
    keys, queries = np.arange(TP)[None], np.arange(TP)[:, None]
    seen = np.where((keys <= queries) & (keys < T), 0.0, MASKED)
    return fft.astype(np.float32), dft_t.reshape(P, 2 * P).astype(np.float32), np.tile(seen, (2, 2)).astype(np.float32)


def _layout_a(i):
    fft, dft_t, mask = _shape_constants()
    f = np.float32
    x = np.zeros((D, B, CONV_T + 2 * HALO), f)
    x[:, :, HALO:HALO + S] = i["x"].transpose(2, 0, 1)
    x = x.reshape(D, NT, NB, -1)
    h = NB // 2
    tail = np.concatenate([x[P:, :, :h], x[P:, :, h:]], axis=0)
    xt = np.ascontiguousarray(np.concatenate([x[:P], tail], axis=2).transpose(1, 0, 2, 3))
    wa, ba = i["L0_attn_w_attn"][SPECTRUM], i["L0_attn_b_attn"]
    wq, wk, wv = wa[:, :D], wa[:, D:2 * D], wa[:, 2 * D:]
    w = np.concatenate([_outs(np.ascontiguousarray(i["L0_tok_w_pw"][:, :, 0].T)), fft, _outs(wq), _outs(wk), wv,
                        i["L0_attn_w_proj"][:, SPECTRUM], i["L0_ffn_gate_w"].T[SPECTRUM]], axis=1)
    cols = np.zeros((P, len(A_COL)), f)
    dw = i["L0_tok_w_dw"][:, 0, :]
    put = lambda n, v: cols.__setitem__((slice(None), A_COL[n]), v)
    for j in range(TAPS):
        put(f"tap{j}a", dw[:P, j])
        put(f"tap{j}b", _twice(dw[:, j]))
    for n, v in (("bdw", i["L0_tok_b_dw"]), ("bpw", i["L0_tok_b_pw"]), ("bq", ba[:D])):
        put(n + "a", v[:P])
        put(n + "b", _twice(v))
    par = (np.arange(P) // HD) % 2
    bk = ba[D:2 * D]
    for n, p in (("e", 0), ("o", 1)):
        own = par == p
        cols[own, A_COL[f"bk{n}a"]] = bk[:P][own]
        cols[own, A_COL[f"bk{n}b"]] = _twice(bk)[own]
    cols[par == 0, A_COL["even"]] = 1
    cols[par == 1, A_COL["odd"]] = 1
    rows = np.zeros((P, len(A_ROW), D), f)
    sp = lambda n: i[n][SPECTRUM]
    for n, v in (("gamma", sp("L0_tok_gamma")), ("beta", sp("L0_tok_beta")), ("bv", ba[2 * D:]),
                 ("bproj", sp("L0_attn_b_proj")), ("scale", sp("L0_ffn_scale")), ("gateb", i["L0_ffn_gate_b"])):
        rows[:, A_ROW[n], :len(v)] = v
    return {"x": xt, "a_w": _parts(w), "dft_t": dft_t, "a_cols": cols, "a_rows": rows, "a_mask": mask}


def _sel(experts):
    sel = np.zeros((64, HID), np.float32)
    for e in range(experts):
        n = HID // experts
        sel[e, e * n:(e + 1) * n] = sel[32 + e, e * n:(e + 1) * n] = 1
    return sel


def _bias_rows(b2, experts):
    out = np.zeros((64, D), np.float32)
    out[:experts] = out[32:32 + experts] = b2[:, SPECTRUM]
    return out


def _layout_b(i):
    w1, b1, w2 = i["L0_ffn_w1"][:, SPECTRUM], i["L0_ffn_b1"], i["L0_ffn_w2"][:, :, SPECTRUM]
    e, i2 = w1.shape[0], w1.shape[2] // 2
    parts = [w1[:, :, h * i2:(h + 1) * i2].transpose(1, 0, 2).reshape(D, CHUNKS, 1, P) for h in range(2)]
    w = np.concatenate(parts, axis=2).reshape(D, 2 * HID)
    b = np.stack([b1[:, h * i2:(h + 1) * i2].reshape(CHUNKS, P).T for h in range(2)], axis=1)
    return {"b_w1": _parts(w), "b_w2": w2.reshape(CHUNKS, P, D).transpose(1, 0, 2), "b_b1": b,
            "b_b2": _bias_rows(i["L0_ffn_b2"], e), "b_sel": _sel(e)}


def _layout_d(i):
    w1, b1, w2 = i["L1_ffn_W1"][:, SPECTRUM], i["L1_ffn_b1"], i["L1_ffn_W2"][:, :, SPECTRUM]
    e = w1.shape[0]
    return {"d_w1": _parts(w1.transpose(1, 0, 2).reshape(D, HID)),
            "d_w2": w2.reshape(CHUNKS, P, D).transpose(1, 0, 2), "d_b1": b1.reshape(CHUNKS, P).T[:, None],
            "d_b2": _bias_rows(i["L1_ffn_b2"], e), "d_sel": _sel(e)}


def _layout_c(i):
    f = np.float32
    t = lambda n: i[n].T
    gate = np.zeros((D, 16), f)
    gate[:, :4] = i["L1_ffn_Wg"][SPECTRUM]
    w = np.concatenate([_outs(t("L1_attn_Wk_a")[SPECTRUM]), _outs(t("L1_attn_Wv_a")[SPECTRUM]), _outs(t("L1_attn_Wr_a")[SPECTRUM]),
                        t("L1_attn_Wo_a")[:, SPECTRUM], t("L1_attn_Wr_f")[SPECTRUM][:, SPECTRUM],
                        t("L1_attn_Wk_f")[SPECTRUM], gate], axis=1)
    wv = t("L1_attn_Wv_f")[:, SPECTRUM].reshape(KFC, P, D).transpose(1, 0, 2)
    rows = np.zeros((P, len(C_ROW), D), f)
    for n, v in (("ln1w", i["L1_attn_ln1_w"][SPECTRUM]), ("ln1b", i["L1_attn_ln1_b"][SPECTRUM]),
                 ("ln2w", i["L1_attn_ln2_w"][SPECTRUM]), ("ln2b", i["L1_attn_ln2_b"][SPECTRUM]), ("gateb", i["L1_ffn_bg"])):
        rows[:, C_ROW[n], :len(v)] = v

    def table(v, pad):
        out = np.full((P, KEYS // TP, TP), pad, f)
        out[:, :NB, :T] = v[:P, None, None]
        out[:, NB:, :T] = _twice(v)[:, None, None]
        return out.reshape(P, KEYS)

    return {"c_w": _parts(w), "c_wv": wv, "c_rows": rows, "c_decay": table(i["L1_attn_decay"], NEG),
            "c_bonus": table(i["L1_attn_first"], 0.0)}


_SCRATCH = {"tp": (NT, P, 3, N), "fw": (NT, 64, N), "base": (NT, P, NG, D), "h2": (NT, P, NG, D),
            "tp2": (NT, P, 3, N), "fw2": (NT, 64, N), "h3": (NT, P, NG, D)}


def kernel(**inputs):
    import concourse.bacc as _bacc
    from concourse.bass_utils import run_bass_kernel_spmd as _run

    i = {n: np.asarray(a) for n, a in inputs.items()}
    arrays = {}
    for layout in (_layout_a, _layout_b, _layout_c, _layout_d):
        arrays.update({n: np.ascontiguousarray(a) for n, a in layout(i).items()})
    nc = _bacc.Bacc("TRN2", target_bir_lowering=False, num_devices=1)
    io = {n: nc.dram_tensor(n, a.shape, F32, kind="ExternalInput").ap() for n, a in arrays.items()}
    io.update({n: nc.dram_tensor(n, shape, F32, kind="Internal").ap() for n, shape in _SCRATCH.items()})
    io["out"] = nc.dram_tensor("out", (NT, P, NG, D), F32, kind="ExternalOutput").ap()
    build(nc, io)
    r = _run(nc, [arrays], core_ids=[0]).results[0]["out"]
    y = r.reshape(NT, 2, TP, NG, D).transpose(0, 3, 1, 2, 4).reshape(B, TP, D)[:, :T]
    out = np.empty((B, T, D), np.float32)
    out[:, :, SPECTRUM] = y
    return out
```

```python
from contextlib import ExitStack

import numpy as np

import concourse.bass as bass
from concourse import mybir

F32 = mybir.dt.float32
F32R = mybir.dt.float32r
I32 = mybir.dt.int32
ALU = mybir.AluOpType
ACT = mybir.ActivationFunctionType
AXX = mybir.AxisListType.X

P = 128
B, S, D = 128, 125, 192
T = S // 2
TP = 64
TAPS = 7
HALO = TAPS // 2
NB = 8
NT = B // NB
NG = NB // 2
N = NB * TP
D2 = D - P
HEADS, HD = 12, 16
PAIRS = HEADS // 2
CONV_T = 2 * T
KC = D // 2 + 1
KP = KC + 1
EPS = 1e-5
NEG = -1.0e38
MASKED = -1.0e30
FREE = 3.0e38

A_COLS = {"pw": 256, "fft": 2 * KP, "q": 256, "k": 256, "v": 192, "proj": 192, "gate": 16}
C_COLS = {"wk": 256, "wv": 256, "wr": 256, "wo": 192, "rf": 192, "kf": 768, "gate": 16}


def offsets(cols):
    at, out = 0, {}
    for name, n in cols.items():
        out[name] = (at, n)
        at += n
    return out, at


A_AT, A_TOT = offsets(A_COLS)
C_AT, C_TOT = offsets(C_COLS)

A_COL = {n: k for k, n in enumerate(
    [f"tap{j}a" for j in range(TAPS)] + [f"tap{j}b" for j in range(TAPS)]
    + ["bdwa", "bdwb", "bpwa", "bpwb", "bqa", "bqb", "bkea", "bkoa", "bkeb", "bkob", "even", "odd"])}
A_ROW = {n: k for k, n in enumerate(["gamma", "beta", "bv", "bproj", "scale", "gateb"])}
C_ROW = {n: k for k, n in enumerate(["ln1w", "ln1b", "ln2w", "ln2b", "gateb"])}


class Semaphores:

    def __init__(self, nc, phase):
        self.nc, self.all = nc, []
        self.passed = self.new(f"passed{phase}")

    def new(self, name):
        self.all.append(self.nc.alloc_semaphore(name=name))
        return self.all[-1]

    def end(self):
        self.nc.all_engine_barrier()
        self.nc.clear_and_free_semaphores(self.all)
        self.nc.all_engine_barrier()


class Signal:

    def __init__(self, nc, stack, name, per=1, ways=2, step=1, credit=False):
        self.sem = stack.new(name)
        self.per, self.ways, self.step = per, ways, step
        self.primed = per * ways * step if credit else 0

    def credit(self, eng):
        eng.sem_inc(self.sem, self.primed)

    def now(self, it, u, n=None):
        n = self.per if n is None else n
        return it * (self.per * self.ways * self.step) + (u * self.per + n) * self.step + self.primed

    def last(self, it, u, n=None):
        n = self.per if n is None else n
        return it * (self.per * self.ways * self.step) + (u * self.per + n) * self.step

    def back(self, it, k):
        return self.now(it, k) if k >= 0 else self.last(it, self.ways + k)


class Count:

    def __init__(self, sem):
        self.sem, self.value = sem, 0

    def of(self, instruction):
        self.value += 1
        return instruction.then_inc(self.sem, 1)


def product5(nc, out, act, act_cols, w, w_cols, act_moves, start, stop):
    passes = ((0, 0, 0), (0, 1, 0), (1, 0, 0), (2, 0, 1), (2, 1, 1))
    last = None
    for k, (a, hl, part) in enumerate(passes):
        x = act[:, a, act_cols]
        y = w[:, hl, part, w_cols]
        lhs, rhs = (y, x) if act_moves else (x, y)
        last = nc.tensor.matmul(out, lhs, rhs, start=start and k == 0, stop=stop and k == 4,
                                skip_group_check=True)
    return last


class SplitWeights:
    CH, SLOTS = 1024, 4

    def __init__(self, nc, stack, ctx, prefix, jobs):
        self.nc, self.pieces = nc, []
        for src, hi, lo in jobs:
            p, n = src.shape
            for c in range(0, n, self.CH):
                m = min(self.CH, n - c)
                self.pieces.append((src[:, c:c + m], hi[:, c:c + m], lo[:, c:c + m], p, m))
        self.stage = ctx.enter_context(nc.sbuf_tensor(f"{prefix}_stage", [P, self.SLOTS, self.CH], F32))
        self.loaded = [stack.new(f"{prefix}_loaded{j}") for j in range(self.SLOTS)]
        self.high = stack.new(f"{prefix}_high")
        self.low = stack.new(f"{prefix}_low")

    def load(self, sp):
        for k, (src, hi, lo, p, m) in enumerate(self.pieces):
            j = k % self.SLOTS
            if k >= self.SLOTS:
                sp.wait_ge(self.low, k - self.SLOTS + 1)
            sp.dma_start(self.stage[0:p, j, 0:m], src).then_inc(self.loaded[j], 16)

    def round(self, act):
        for k, (src, hi, lo, p, m) in enumerate(self.pieces):
            j = k % self.SLOTS
            act.wait_ge(self.loaded[j], 16 * (k // self.SLOTS + 1))
            self.nc.scalar.copy(hi, self.stage[0:p, j, 0:m]).then_inc(self.high, 1)

    def subtract(self, dve):
        for k, (src, hi, lo, p, m) in enumerate(self.pieces):
            dve.wait_ge(self.high, k + 1)
            self.nc.vector.tensor_tensor(lo, self.stage[0:p, k % self.SLOTS, 0:m], hi.bitcast(F32),
                                         ALU.subtract).then_inc(self.low, 1)


def split_weights(nc, stack, prefix, jobs):
    with ExitStack() as ctx:
        split = SplitWeights(nc, stack, ctx, prefix, jobs)
        block = ctx.enter_context(nc.Block())

        @block.sync
        def _(sp):
            split.load(sp)

        @block.scalar
        def _(act):
            split.round(act)

        @block.vector
        def _(dve):
            split.subtract(dve)


def fill_identity(nc, pool, ident, sem):
    pool.memset(ident[:, :], 0.0).then_inc(sem, 1)
    pool.wait_ge(sem, 1)
    pool.affine_select(out=ident[:, :], in_=ident[:, :], compare_op=ALU.not_equal, fill=1.0,
                       base=0, pattern=[[-1, P]], channel_multiplier=1).then_inc(sem, 1)


def norm_stats(nc, stack, dve, src, st, mv, stats_ready, moments_ready, it, u):
    for g in range(NG):
        nc.vector.bn_stats(st[:, g, :], src[:, g, :]).then_inc(stats_ready.sem, 1)
    dve.wait_ge(stats_ready.sem, stats_ready.now(it, u))
    dve.sem_inc(stack.passed, 1)
    for g in range(NG):
        nc.vector.bn_aggr(mv[:, g, :], st[:, g, :]).then_inc(moments_ready.sem, 1)


def norm_apply(nc, out, src, mv, rs, sig):
    for g in range(NG):
        nc.vector.tensor_scalar(out[:, g, :], src[:, g, :], mv[:, g, 0:1], rs[:, g:g + 1],
                                ALU.subtract, ALU.mult).then_inc(sig.sem, 1)


def transpose_tile(nc, ps, b0, src, ident, sig):
    for g in range(NG):
        nc.tensor.transpose(ps[:, b0, g * P:(g + 1) * P], src[:, g, 0:P], ident[:, :])
    for g in range(NG):
        last = nc.tensor.transpose(ps[0:D2, b0 + 1, g * P:(g + 1) * P], src[:, g, P:D], ident[:, :])
    last.then_inc(sig.sem, 1)


def pack_high(nc, ps, b0, pk, sig):
    nc.scalar.copy(pk[:, 0, :], ps[:, b0, :]).then_inc(sig.sem, 1)
    nc.scalar.copy(pk[0:D2, 2, :], ps[0:D2, b0 + 1, :]).then_inc(sig.sem, 1)


def pack_low(nc, dve, ps, b0, pk, high, sig, it, u):
    dve.wait_ge(high.sem, high.now(it, u, 1))
    nc.vector.tensor_tensor(pk[:, 1, :], ps[:, b0, :], pk[:, 0, :].bitcast(F32),
                            ALU.subtract).then_inc(sig.sem, 1)
    dve.wait_ge(high.sem, high.now(it, u, 2))
    nc.vector.tensor_tensor(pk[D2:P, 2, :], ps[0:D2, b0 + 1, :], pk[0:D2, 2, :].bitcast(F32),
                            ALU.subtract).then_inc(sig.sem, 1)


def bcast_groups(row, n=D):
    return row[:, 0:n].unsqueeze(1).to_broadcast([P, NG, n])


class Router:

    def __init__(self, nc, stack, ctx, prefix, experts, k):
        self.nc, self.e, self.k, self.stack = nc, experts, k, stack
        sb = lambda n, shape: ctx.enter_context(nc.sbuf_tensor(f"{prefix}_{n}", shape, F32))
        self.gb = [sb(f"gb{u}", [P, NG, 24]) for u in range(2)]
        self.rep = [sb(f"rep{u}", [P, NG, 24]) for u in range(2)]
        self.m8 = [sb(f"m8{u}", [P, NG, 8]) for u in range(2)]
        self.sh = [sb(f"sh{u}", [P, NG, 16]) for u in range(2)]
        self.ex = [sb(f"ex{u}", [P, NG, 16]) for u in range(2)]
        self.wm = [sb(f"wm{u}", [P, NG, 16]) for u in range(2)]
        self.den = [sb(f"den{u}", [P, NG]) for u in range(2)]
        self.fw = [sb(f"fw{u}", [P, NG, 16]) for u in range(2)]
        sig = lambda n, per=1: Signal(nc, stack, f"{prefix}_{n}", per)
        self.biased, self.found, self.cut = sig("biased"), sig("found", NG), sig("cut")
        self.replaced, self.masked = sig("replaced", NG), sig("masked")
        self.shifted, self.exped = sig("shifted"), sig("exped")
        self.weighed, self.summed, self.inverse = sig("weighed"), sig("summed"), sig("inverse")
        self.gates = sig("gates")
        self.init = stack.new(f"{prefix}_init")

    def start(self, dve):
        nc = self.nc
        for u in range(2):
            nc.vector.memset(self.gb[u][:, :, 0:16], -FREE)
            nc.vector.memset(self.gb[u][:, :, 16:24], FREE)
            nc.vector.memset(self.wm[u][:, :, :], 0.0)
            nc.vector.memset(self.fw[u][:, :, :], 0.0).then_inc(self.init, 1)
        dve.wait_ge(self.init, 2)

    def choose(self, dve, logits, bias_row, it, u):
        nc, e, k = self.nc, self.e, self.k
        gb, rep, m8 = self.gb[u], self.rep[u], self.m8[u]
        nc.vector.tensor_tensor(gb[:, :, 0:e], logits, bcast_groups(bias_row, e),
                                ALU.add).then_inc(self.biased.sem, 1)
        dve.wait_ge(self.biased.sem, self.biased.now(it, u))
        dve.sem_inc(self.stack.passed, 1)
        for g in range(NG):
            nc.vector.max(m8[:, g, :], gb[:, g, 0:16]).then_inc(self.found.sem, 1)
        dve.wait_ge(self.found.sem, self.found.now(it, u))
        nc.vector.memset(m8[:, :, k:8], FREE).then_inc(self.cut.sem, 1)
        if k > 1:
            nc.vector.tensor_tensor(self.sh[u][:, :, :], gb[:, :, 0:16],
                                    m8[:, :, 0:1].to_broadcast([P, NG, 16]),
                                    ALU.subtract).then_inc(self.shifted.sem, 1)
        dve.wait_ge(self.cut.sem, self.cut.now(it, u))
        dve.sem_inc(self.stack.passed, 1)
        for g in range(NG):
            nc.vector.match_replace(rep[:, g, :], m8[:, g, :], gb[:, g, :], -FREE / 2
                                    ).then_inc(self.replaced.sem, 1)
        dve.wait_ge(self.replaced.sem, self.replaced.now(it, u))
        if k == 1:
            nc.vector.tensor_tensor(self.fw[u][:, :, 0:e], rep[:, :, 0:e], gb[:, :, 0:e],
                                    ALU.not_equal).then_inc(self.gates.sem, 1)
            return
        nc.vector.tensor_tensor(self.wm[u][:, :, :], rep[:, :, 0:16], gb[:, :, 0:16],
                                ALU.not_equal).then_inc(self.masked.sem, 1)
        dve.wait_ge(self.masked.sem, self.masked.now(it, u))
        dve.wait_ge(self.exped.sem, self.exped.now(it, u))
        nc.vector.tensor_tensor(self.wm[u][:, :, :], self.wm[u][:, :, :], self.ex[u][:, :, :],
                                ALU.mult).then_inc(self.weighed.sem, 1)
        dve.wait_ge(self.weighed.sem, self.weighed.now(it, u))
        nc.vector.tensor_reduce(self.den[u][:, :], self.wm[u][:, :, :], AXX, ALU.add
                                ).then_inc(self.summed.sem, 1)
        dve.wait_ge(self.summed.sem, self.summed.now(it, u))
        nc.vector.reciprocal(self.den[u][:, :], self.den[u][:, :]).then_inc(self.inverse.sem, 1)
        dve.wait_ge(self.inverse.sem, self.inverse.now(it, u))
        nc.vector.tensor_tensor(self.fw[u][:, :, :], self.wm[u][:, :, :],
                                self.den[u][:, :].unsqueeze(2).to_broadcast([P, NG, 16]),
                                ALU.mult).then_inc(self.gates.sem, 1)

    def exponentials(self, act, it, u):
        act.wait_ge(self.shifted.sem, self.shifted.now(it, u))
        self.nc.scalar.activation(self.ex[u][:, :, :], self.sh[u][:, :, :], ACT.Exp
                                  ).then_inc(self.exped.sem, 1)

    def spread(self, pe, ps, bank, ident, sig, it, u):
        pe.wait_ge(self.gates.sem, self.gates.now(it, u))
        for g in range(NG):
            last = self.nc.tensor.transpose(ps[0:16, bank, g * P:(g + 1) * P],
                                            self.fw[u][:, g, :], ident[:, :])
        last.then_inc(sig.sem, 1)


def phase_a(nc, stack, io):
    with ExitStack() as ctx:
        sb = lambda n, shape, dt=F32: ctx.enter_context(nc.sbuf_tensor(f"a_sb_{n}", shape, dt))
        two = lambda n, shape, dt=F32: [sb(f"{n}{u}", shape, dt) for u in range(2)]
        sig = lambda n, per=1, step=1, ways=2, credit=False: Signal(nc, stack, f"a_{n}", per, ways, step, credit)
        sig4 = lambda n, per=1: sig(n, per, ways=4)
        ps = ctx.enter_context(nc.psum_tensor("a_ps", [P, 8, 512], F32))

        W = sb("W", [P, 2, 2, A_TOT], F32R)
        CS = sb("CS", [P, 2, 2, P], F32R)
        cols = sb("cols", [P, len(A_COL)])
        rows = sb("rows", [P, len(A_ROW), D])
        mask = sb("mask", [P, P])
        ident = sb("ident", [P, P])
        split_weights(nc, stack, "aw", [
            (io["a_w"].rearrange("p a n -> p (a n)"),
             W[:, 0].rearrange("p a n -> p (a n)"), W[:, 1].rearrange("p a n -> p (a n)")),
            (io["dft_t"], CS[:, 0].rearrange("p a n -> p (a n)"), CS[:, 1].rearrange("p a n -> p (a n)"))])

        xin = two("xin", [P, NB + NB // 2, CONV_T + 2 * HALO])
        acc = two("acc", [P, (NB + NB // 2) * CONV_T])
        cv = two("cv", [P, 2 * (NB + NB // 2) * CONV_T], F32R)
        mx = two("mx", [P, 2, NB, TP])
        pk = two("pk", [P, 3, N], F32R)
        bs = two("bs", [P, NG, KP])
        yb, hb, nb = two("yb", [P, NG, D]), two("hb", [P, NG, D]), two("nb", [P, NG, D])
        q = two("q", [P, 2, N])
        kx = two("kx", [P, 2, 2, N])
        vblk = two("vblk", [P, NG, 2, PAIRS, 2, HD + 1])
        pt = two("pt", [P, 2 * PAIRS, P])
        sm_mx = two("smmx", [P, 2 * HEADS])
        rden = two("rden", [P, 2 * HEADS])
        st, mv = two("st", [P, NG, 6]), two("mv", [P, NG, 2])
        rs = two("rs", [P, NG])
        ra, rb, rc = two("ra", [P, NG]), two("rb", [P, NG]), two("rc", [P, NG])
        half = sb("half", [P, NG])
        fwt = two("fwt", [64, N], F32R)
        router = Router(nc, stack, ctx, "ar", 16, 4)

        dma = lambda n: [sig(f"{n}{u}", 1, 16, 1) for u in range(2)]
        loaded, consts = dma("loaded"), stack.new("a_consts")
        setup = stack.new("a_setup")
        cleared = stack.new("a_cleared")
        identity = stack.new("a_identity")
        conv0, conv, conv_h, conv_l = sig("conv0", 2), sig("conv", 2 * (TAPS - 1), credit=True), sig("convh", 2), sig("convl", 2)
        pw_done, pooled, act_r = sig("pwdone"), sig("pooled", 2), sig("relu", 2)
        hp_h, hp_l = sig("hph", 2), sig("hpl", 2)
        ftd, pq_h, pq_l = sig("ftd"), sig("pqh"), sig("pql")
        fts, bs_up, y_ready = sig("fts"), sig("bsup"), sig("y", 2)
        s1, m1, v1, r1, a1, g1, h0 = sig("s1", 4), sig("m1", 4), sig("v1"), sig("r1"), sig("a1", 4), sig("g1"), sig("h0")
        s2, m2, v2, r2, n1 = sig("s2", 4), sig("m2", 4), sig("v2"), sig("r2"), sig("n1", 4)
        t1, p1h, p1l = sig("t1"), sig("p1h", 2), sig("p1l", 2)
        q_ps, q_up, k_ps, v_ps, v_up = sig("qps"), sig("qup", 2), sig("kps"), sig("vps"), sig("vup")
        ka_up, kv_up, vd_up, vo_up = sig("kaup", 2), sig("kvup", 2), sig("vdup", 2), sig("voup", 2)
        sc, sadd, smax, ssub, sexp = sig4("sc"), sig4("sadd", 4), sig4("smax"), sig4("ssub"), sig4("sexp")
        ptt, pta, ptv, pv, rd, at = sig4("ptt"), sig4("pta", 2), sig4("ptv"), sig4("pv"), sig4("rd"), sig4("at")
        t2, p2h, p2l = sig("t2"), sig("p2h", 2), sig("p2l", 2)
        hbias, pr, h1 = sig("hbias"), sig("pr"), sig("h1")
        s3, m3, pl3, n2, base, tt = sig("s3", 4), sig("m3", 4), sig("pl3", 6), sig("n2", 4), sig("base"), sig("tt", 4)
        t3, p3h, p3l = sig("t3"), sig("p3h", 2), sig("p3l", 2)
        gt, fwps, fwh, fwl = sig("gt"), sig("fwps"), sig("fwh"), sig("fwl")
        st_pk, st_fw, st_base = dma("stpk"), dma("stfw"), dma("stbase")
        block = ctx.enter_context(nc.Block())
        col = lambda n, p0=0, p1=P: cols[p0:p1, A_COL[n]:A_COL[n] + 1]
        row = lambda n: rows[:, A_ROW[n], :]
        w_at = lambda n, a=0, m=None: slice(A_AT[n][0] + a, A_AT[n][0] + a + (m or A_AT[n][1]))
        NC = NB * CONV_T
        acc0 = [a[:, 0:NC].rearrange("p (b s) -> p b s", b=NB) for a in acc]
        acc1 = [a[:, NC:NC + NC // 2].rearrange("p (b s) -> p b s", b=NB // 2) for a in acc]
        sm = [a[:, 0:2 * PAIRS * P].rearrange("p (g j c) -> p g j c", g=2, j=PAIRS) for a in [
            sb(f"sm{u}", [P, 2 * PAIRS * P]) for u in range(2)]]
        pqn = NG * 2 * KP
        pq = [[c[:, hl * pqn:(hl + 1) * pqn].rearrange("p (g n) -> p g n", g=NG) for hl in range(2)] for c in cv]

        def dft_out(u, b0):
            return ps[:, 4 * u + b0:4 * u + b0 + 2, :].rearrange("p b (h n) -> p b h n", h=2)[:, :, :, 0:2 * KP]

        def two_banks(u, b0, n):
            return ps[:, 4 * u + b0:4 * u + b0 + 2, :].rearrange("p b (h n) -> p b h n", h=2)[:, :, :, 0:n]

        def split4(ap):
            return ap.rearrange("p (b h) n -> p b h n", b=2)

        @block.sync
        def _(sp):
            sp.dma_start(cols[:, :], io["a_cols"]).then_inc(consts, 16)
            sp.dma_start(rows[:, :, :], io["a_rows"]).then_inc(consts, 16)
            sp.dma_start(mask[:, :], io["a_mask"]).then_inc(consts, 16)
            with sp.Fori(0, NT // 2) as it:
                for u in range(2):
                    sp.wait_ge(conv.sem, conv.last(it, u))
                    sp.sem_inc(stack.passed, 1)
                    sp.dma_start(xin[u][:, :, :], io["x"][it * 2 + u]).then_inc(loaded[u].sem, 16)
                for u in range(2):
                    sp.wait_ge(base.sem, base.now(it, u))
                    sp.sem_inc(stack.passed, 1)
                    sp.dma_start(io["base"][it * 2 + u], hb[u][:, :, :]).then_inc(st_base[u].sem, 16)
                for u in range(2):
                    sp.wait_ge(p3h.sem, p3h.now(it, u))
                    sp.sem_inc(stack.passed, 1)
                    sp.wait_ge(p3l.sem, p3l.now(it, u))
                    sp.sem_inc(stack.passed, 1)
                    sp.dma_start(io["tp"][it * 2 + u], pk[u][:, :, :].bitcast(F32)).then_inc(st_pk[u].sem, 16)
                for u in range(2):
                    sp.wait_ge(fwh.sem, fwh.now(it, u))
                    sp.sem_inc(stack.passed, 1)
                    sp.wait_ge(fwl.sem, fwl.now(it, u))
                    sp.sem_inc(stack.passed, 1)
                    sp.dma_start(io["fw"][it * 2 + u], fwt[u][:, :].bitcast(F32)).then_inc(st_fw[u].sem, 16)
                for u in range(2):
                    sp.wait_ge(st_base[u].sem, st_base[u].now(it, 0))
                    sp.sem_inc(stack.passed, 1)
                    sp.wait_ge(st_pk[u].sem, st_pk[u].now(it, 0))
                    sp.sem_inc(stack.passed, 1)
                    sp.wait_ge(st_fw[u].sem, st_fw[u].now(it, 0))
                    sp.sem_inc(stack.passed, 1)

        @block.gpsimd
        def _(pool):
            fill_identity(nc, pool, ident, identity)
            nc.gpsimd.memset(half[:, :], -0.5).then_inc(setup, 1)
            for u in range(2):
                nc.gpsimd.memset(vblk[u][:, :, :, :, :, :], 0.0).then_inc(setup, 1)
                nc.gpsimd.memset(mx[u][:, :, :, :], 0.0).then_inc(setup, 1)
            pool.wait_ge(setup, 5)
            for u in range(2):
                for par in range(2):
                    nc.gpsimd.memset(vblk[u][64 * par:64 * par + 64, :, :, :, par, HD:HD + 1], 1.0).then_inc(setup, 1)
            pool.wait_ge(setup, 9)
            with pool.Fori(0, NT // 2) as it:
                for (m, v, r) in ((m1, v1, r1), (m2, v2, r2)):
                    for u in range(2):
                        pool.wait_ge(m.sem, m.now(it, u))
                        pool.sem_inc(stack.passed, 1)
                        nc.gpsimd.tensor_scalar(ra[u][:, :], mv[u][:, :, 1], EPS, None, ALU.add).then_inc(v.sem, 1)
                        pool.wait_ge(v.sem, v.now(it, u))
                        nc.gpsimd.tensor_tensor(rs[u][:, :], ra[u][:, :], half[:, :], ALU.pow).then_inc(r.sem, 1)
                for u in range(2):
                    pool.wait_ge(v_up.sem, v_up.now(it, u))
                    pool.sem_inc(stack.passed, 1)
                    for b in range(2):
                        for par in range(2):
                            if b != par:
                                continue
                            nc.gpsimd.tensor_copy(
                                vblk[u][64 * par:64 * par + 64, :, b, :, par, 0:HD],
                                yb[u][64 * b:64 * b + 64, :, :].rearrange("p g (j a c) -> p g j a c", j=PAIRS, a=2)[:, :, :, par, :]
                            ).then_inc(vd_up.sem, 1)
                pool.wait_ge(vd_up.sem, vd_up.now(it, 1))
                for pg in range(2):
                    for u in range(2):
                        pool.wait_ge(smax.sem, smax.now(it, 2 * pg + u))
                        nc.gpsimd.tensor_tensor(
                            sm[u].rearrange("p g j (a c) -> p (g j a) c", a=2),
                            sm[u].rearrange("p g j (a c) -> p (g j a) c", a=2),
                            sm_mx[u][:, :].unsqueeze(2).to_broadcast([P, 2 * HEADS, TP]),
                            ALU.subtract).then_inc(ssub.sem, 1)
                for u in range(2):
                    pool.wait_ge(p1l.sem, p1l.now(it, u))
                    pool.wait_ge(h0.sem, h0.now(it, u))
                    nc.gpsimd.tensor_tensor(hb[u][:, :, :], hb[u][:, :, :], bcast_groups(row("bproj")), ALU.add).then_inc(hbias.sem, 1)
                for u in range(2):
                    pool.wait_ge(m3.sem, m3.now(it, u))
                    pool.sem_inc(stack.passed, 1)
                    nc.gpsimd.tensor_scalar(ra[u][:, :], mv[u][:, :, 1], EPS, None, ALU.add).then_inc(pl3.sem, 1)
                    pool.wait_ge(pl3.sem, pl3.now(it, u, 1))
                    nc.gpsimd.tensor_tensor(rs[u][:, :], ra[u][:, :], half[:, :], ALU.pow).then_inc(pl3.sem, 1)
                    pool.wait_ge(pl3.sem, pl3.now(it, u, 2))
                    nc.gpsimd.tensor_tensor(rb[u][:, :], rs[u][:, :], rs[u][:, :], ALU.mult).then_inc(pl3.sem, 1)
                    pool.wait_ge(pl3.sem, pl3.now(it, u, 3))
                    nc.gpsimd.tensor_tensor(rb[u][:, :], rb[u][:, :], mv[u][:, :, 1], ALU.mult).then_inc(pl3.sem, 1)
                    pool.wait_ge(pl3.sem, pl3.now(it, u, 4))
                    pool.sem_inc(stack.passed, 1)
                    nc.gpsimd.tensor_scalar(rb[u][:, :], rb[u][:, :], EPS, None, ALU.add).then_inc(pl3.sem, 1)
                    pool.wait_ge(pl3.sem, pl3.now(it, u, 5))
                    nc.gpsimd.tensor_tensor(rc[u][:, :], rb[u][:, :], half[:, :], ALU.pow).then_inc(pl3.sem, 1)

        @block.vector
        def _(dve):
            dve.wait_ge(consts, 48)
            router.start(dve)
            for u in range(2):
                nc.vector.memset(fwt[u][:, :].bitcast(F32), 0.0).then_inc(cleared, 1)
            dve.wait_ge(setup, 9)
            dve.wait_ge(cleared, 2)
            conv.credit(dve)
            with dve.Fori(0, NT // 2) as it:
                for u in range(2):
                    xa, xb = xin[u][:, 0:NB, :], xin[u][:, NB:NB + NB // 2, :]
                    dve.wait_ge(conv0.sem, conv0.now(it, u))
                    for j in range(1, TAPS):
                        for c, (x, a) in enumerate(((xa, acc0[u]), (xb, acc1[u]))):
                            if j > 1:
                                dve.wait_ge(conv.sem, conv.now(it, u, 2 * (j - 2) + c + 1))
                            nc.vector.scalar_tensor_tensor(
                                a, x[:, :, j:j + CONV_T], col(f"tap{j}{'ab'[c]}"), a,
                                ALU.mult, ALU.add).then_inc(conv.sem, 1)
                    for c, (c0, c1) in enumerate(((0, NC), (NC, NC + NC // 2))):
                        dve.wait_ge(conv_h.sem, conv_h.now(it, u, c + 1))
                        nc.vector.tensor_tensor(cv[u][:, NC * 3 // 2 + c0:NC * 3 // 2 + c1], acc[u][:, c0:c1],
                                                cv[u][:, c0:c1].bitcast(F32), ALU.subtract).then_inc(conv_l.sem, 1)
                for u in range(2):
                    dve.wait_ge(pw_done.sem, pw_done.now(it, u))
                    for c in range(2):
                        src = ps[:, 4 * u + 2 * c:4 * u + 2 * c + 2, 0:NC // 2].rearrange(
                            "p h (b s t) -> p h b s t", b=NB // 2, t=2)
                        nc.vector.tensor_reduce(
                            mx[u][:, c, :, 0:T].rearrange("p (h b) s -> p h b s", h=2), src, AXX, ALU.max
                        ).then_inc(pooled.sem, 1)
                for u in range(2):
                    dve.wait_ge(hp_h.sem, hp_h.now(it, u, 1))
                    nc.vector.tensor_tensor(pk[u][:, 1, :], mx[u][:, 0].rearrange("p b s -> p (b s)"),
                                            pk[u][:, 0, :].bitcast(F32), ALU.subtract).then_inc(hp_l.sem, 1)
                    dve.wait_ge(hp_h.sem, hp_h.now(it, u, 2))
                    nc.vector.tensor_tensor(pk[u][D2:P, 2, :], mx[u][0:D2, 1].rearrange("p b s -> p (b s)"),
                                            pk[u][0:D2, 2, :].bitcast(F32), ALU.subtract).then_inc(hp_l.sem, 1)
                for u in range(2):
                    dve.wait_ge(pq_h.sem, pq_h.now(it, u))
                    nc.vector.tensor_tensor(split4(pq[u][1]), dft_out(u, 0), split4(pq[u][0].bitcast(F32)),
                                            ALU.subtract).then_inc(pq_l.sem, 1)
                for u in range(2):
                    dve.wait_ge(bs_up.sem, bs_up.now(it, u))
                    a = two_banks(u, 2, KP)
                    nc.vector.tensor_tensor(split4(yb[u][:, :, 0:KC]), a[:, :, :, 0:KC], split4(bs[u][:, :, 0:KC]),
                                            ALU.subtract).then_inc(y_ready.sem, 1)
                    nc.vector.tensor_tensor(split4(yb[u][:, :, KC:D]), a[:, :, :, 1:KC - 1],
                                            split4(bs[u][:, :, 1:KC - 1]), ALU.add).then_inc(y_ready.sem, 1)
                for u in range(2):
                    dve.wait_ge(y_ready.sem, y_ready.now(it, u))
                    norm_stats(nc, stack, dve, yb[u], st[u], mv[u], s1, m1, it, u)
                for u in range(2):
                    dve.wait_ge(r1.sem, r1.now(it, u))
                    norm_apply(nc, nb[u], yb[u], mv[u], rs[u], a1)
                for u in range(2):
                    dve.wait_ge(a1.sem, a1.now(it, u))
                    nc.vector.tensor_tensor(nb[u][:, :, :], nb[u][:, :, :], bcast_groups(row("gamma")), ALU.mult).then_inc(g1.sem, 1)
                for u in range(2):
                    dve.wait_ge(g1.sem, g1.now(it, u))
                    nc.vector.tensor_tensor(hb[u][:, :, :], nb[u][:, :, :], bcast_groups(row("beta")), ALU.add).then_inc(h0.sem, 1)
                for u in range(2):
                    dve.wait_ge(h0.sem, h0.now(it, u))
                    norm_stats(nc, stack, dve, hb[u], st[u], mv[u], s2, m2, it, u)
                for u in range(2):
                    dve.wait_ge(r2.sem, r2.now(it, u))
                    norm_apply(nc, nb[u], hb[u], mv[u], rs[u], n1)
                for u in range(2):
                    dve.wait_ge(t1.sem, t1.now(it, u))
                    pack_low(nc, dve, ps, 4 * u, pk[u], p1h, p1l, it, u)
                for u in range(2):
                    dve.wait_ge(k_ps.sem, k_ps.now(it, u))
                    nc.vector.tensor_scalar(kx[u][0:D2, 1, 0, :], ps[0:D2, 4 * u + 1, :], col("even", 0, D2), col("bkeb", 0, D2),
                                            ALU.mult, ALU.add).then_inc(kv_up.sem, 1)
                    nc.vector.tensor_scalar(kx[u][0:D2, 1, 1, :], ps[0:D2, 4 * u + 1, :], col("odd", 0, D2), col("bkob", 0, D2),
                                            ALU.mult, ALU.add).then_inc(kv_up.sem, 1)
                for u in range(2):
                    dve.wait_ge(v_ps.sem, v_ps.now(it, u))
                    nc.vector.tensor_tensor(split4(yb[u][:, :, :]), two_banks(u, 2, D),
                                            row("bv").unsqueeze(1).unsqueeze(1).to_broadcast([P, 2, 2, D]), ALU.add).then_inc(v_up.sem, 1)
                for pg in range(2):
                    for u in range(2):
                        dve.wait_ge(sc.sem, sc.now(it, 2 * pg + u))
                        if pg == 1:
                            dve.wait_ge(ptt.sem, ptt.now(it, u))
                        s = ps[:, 4 * u:4 * u + 4, :].rearrange("p r (g s c) -> p g s r c", g=2, s=2)
                        for g in range(2):
                            nc.vector.tensor_tensor(sm[u][:, g, 0:4, :], s[:, g, 0, :, :],
                                                    mask[:, :].unsqueeze(1).to_broadcast([P, 4, P]), ALU.add).then_inc(sadd.sem, 1)
                            nc.vector.tensor_tensor(sm[u][:, g, 4:6, :], s[:, g, 1, 0:2, :],
                                                    mask[:, :].unsqueeze(1).to_broadcast([P, 2, P]), ALU.add).then_inc(sadd.sem, 1)
                        dve.wait_ge(sadd.sem, sadd.now(it, 2 * pg + u))
                        nc.vector.tensor_reduce(sm_mx[u][:, :], sm[u].rearrange("p g j (a c) -> p (g j a) c", a=2),
                                                AXX, ALU.max).then_inc(smax.sem, 1)
                    for u in range(2):
                        dve.wait_ge(ptt.sem, ptt.now(it, 2 * pg + u))
                        nc.vector.tensor_copy(pt[u][:, 0:4, :], ps[:, 4 * u, :].rearrange("p (j c) -> p j c", j=4)).then_inc(ptv.sem, 1)
                    for u in range(2):
                        dve.wait_ge(pv.sem, pv.now(it, 2 * pg + u))
                        o = ps[:, 4 * u + 3, 0:2 * HEADS * (HD + 1)].rearrange("p (h c) -> p h c", c=HD + 1)
                        nc.vector.reciprocal(rden[u][:, :], o[:, :, HD]).then_inc(rd.sem, 1)
                        dve.wait_ge(rd.sem, rd.now(it, 2 * pg + u))
                        nc.vector.tensor_tensor(
                            nb[u][:, 2 * pg:2 * pg + 2, :].rearrange("p g (h c) -> p (g h) c", c=HD), o[:, :, 0:HD],
                            rden[u][:, :].unsqueeze(2).to_broadcast([P, 2 * HEADS, HD]), ALU.mult).then_inc(at.sem, 1)
                for u in range(2):
                    dve.wait_ge(t2.sem, t2.now(it, u))
                    pack_low(nc, dve, ps, 4 * u, pk[u], p2h, p2l, it, u)
                for u in range(2):
                    dve.wait_ge(pr.sem, pr.now(it, u))
                    dve.wait_ge(hbias.sem, hbias.now(it, u))
                    nc.vector.tensor_tensor(split4(hb[u][:, :, :]), two_banks(u, 2, D), split4(hb[u][:, :, :]), ALU.add).then_inc(h1.sem, 1)
                for u in range(2):
                    dve.wait_ge(h1.sem, h1.now(it, u))
                    norm_stats(nc, stack, dve, hb[u], st[u], mv[u], s3, m3, it, u)
                for u in range(2):
                    dve.wait_ge(pl3.sem, pl3.now(it, u))
                    norm_apply(nc, yb[u], hb[u], mv[u], rs[u], n2)
                for u in range(2):
                    dve.wait_ge(n2.sem, n2.now(it, u))
                    nc.vector.tensor_tensor(hb[u][:, :, :], hb[u][:, :, :], yb[u][:, :, :], ALU.add).then_inc(base.sem, 1)
                    for g in range(NG):
                        nc.vector.scalar_tensor_tensor(nb[u][:, g, :], yb[u][:, g, :], rc[u][:, g:g + 1],
                                                       row("scale"), ALU.mult, ALU.mult).then_inc(tt.sem, 1)
                for u in range(2):
                    dve.wait_ge(t3.sem, t3.now(it, u))
                    pack_low(nc, dve, ps, 4 * u, pk[u], p3h, p3l, it, u)
                for u in range(2):
                    dve.wait_ge(gt.sem, gt.now(it, u))
                    router.choose(dve, ps[:, 4 * u + 2, 0:NG * 16].rearrange("p (g e) -> p g e", g=NG), row("gateb"), it, u)
                for u in range(2):
                    dve.wait_ge(fwh.sem, fwh.now(it, u))
                    nc.vector.tensor_tensor(fwt[u][32:48, :], ps[0:16, 4 * u + 3, :], fwt[u][0:16, :].bitcast(F32),
                                            ALU.subtract).then_inc(fwl.sem, 1)
                for u in range(2):
                    dve.wait_ge(st_base[u].sem, st_base[u].now(it, 0))
                    dve.wait_ge(st_pk[u].sem, st_pk[u].now(it, 0))
                    dve.wait_ge(st_fw[u].sem, st_fw[u].now(it, 0))

        @block.scalar
        def _(act):
            act.wait_ge(consts, 48)
            act.wait_ge(setup, 9)
            act.wait_ge(cleared, 2)
            with act.Fori(0, NT // 2) as it:
                for u in range(2):
                    act.wait_ge(loaded[u].sem, loaded[u].now(it, 0))
                    nc.scalar.activation(acc0[u], xin[u][:, 0:NB, 0:CONV_T], ACT.Identity,
                                         bias=col("bdwa"), scale=col("tap0a")).then_inc(conv0.sem, 1)
                    nc.scalar.activation(acc1[u], xin[u][:, NB:NB + NB // 2, 0:CONV_T], ACT.Identity,
                                         bias=col("bdwb"), scale=col("tap0b")).then_inc(conv0.sem, 1)
                for u in range(2):
                    for c, (c0, c1) in enumerate(((0, NC), (NC, NC + NC // 2))):
                        act.wait_ge(conv.sem, conv.now(it, u, 2 * (TAPS - 2) + c + 1))
                        nc.scalar.copy(cv[u][:, c0:c1], acc[u][:, c0:c1]).then_inc(conv_h.sem, 1)
                for u in range(2):
                    for c in range(2):
                        act.wait_ge(pooled.sem, pooled.now(it, u, c + 1))
                        nc.scalar.activation(mx[u][:, c, :, 0:T], mx[u][:, c, :, 0:T], ACT.Relu,
                                             bias=col(f"bpw{'ab'[c]}")).then_inc(act_r.sem, 1)
                    act.wait_ge(act_r.sem, act_r.now(it, u, 1))
                    nc.scalar.copy(pk[u][:, 0, :], mx[u][:, 0].rearrange("p b s -> p (b s)")).then_inc(hp_h.sem, 1)
                    act.wait_ge(act_r.sem, act_r.now(it, u, 2))
                    nc.scalar.copy(pk[u][0:D2, 2, :], mx[u][0:D2, 1].rearrange("p b s -> p (b s)")).then_inc(hp_h.sem, 1)
                for u in range(2):
                    act.wait_ge(ftd.sem, ftd.now(it, u))
                    nc.scalar.copy(split4(pq[u][0]), dft_out(u, 0)).then_inc(pq_h.sem, 1)
                for u in range(2):
                    act.wait_ge(fts.sem, fts.now(it, u))
                    nc.scalar.copy(split4(bs[u][:, :, :]), two_banks(u, 2, 2 * KP)[:, :, :, KP:2 * KP]).then_inc(bs_up.sem, 1)
                for u in range(2):
                    act.wait_ge(t1.sem, t1.now(it, u))
                    pack_high(nc, ps, 4 * u, pk[u], p1h)
                for u in range(2):
                    act.wait_ge(q_ps.sem, q_ps.now(it, u))
                    nc.scalar.activation(q[u][:, 0, :], ps[:, 4 * u + 2, :], ACT.Identity, bias=col("bqa")).then_inc(q_up.sem, 1)
                    nc.scalar.activation(q[u][0:D2, 1, :], ps[0:D2, 4 * u + 3, :], ACT.Identity, bias=col("bqb", 0, D2)).then_inc(q_up.sem, 1)
                for u in range(2):
                    act.wait_ge(k_ps.sem, k_ps.now(it, u))
                    nc.scalar.activation(kx[u][:, 0, 0, :], ps[:, 4 * u, :], ACT.Identity, bias=col("bkea"), scale=col("even")).then_inc(ka_up.sem, 1)
                    nc.scalar.activation(kx[u][:, 0, 1, :], ps[:, 4 * u, :], ACT.Identity, bias=col("bkoa"), scale=col("odd")).then_inc(ka_up.sem, 1)
                for u in range(2):
                    act.wait_ge(v_up.sem, v_up.now(it, u))
                    for b in range(2):
                        par = 1 - b
                        nc.scalar.copy(
                            vblk[u][64 * par:64 * par + 64, :, b, :, par, 0:HD],
                            yb[u][64 * b:64 * b + 64, :, :].rearrange("p g (j a c) -> p g j a c", j=PAIRS, a=2)[:, :, :, par, :]
                        ).then_inc(vo_up.sem, 1)
                for pg in range(2):
                    for u in range(2):
                        act.wait_ge(ssub.sem, ssub.now(it, 2 * pg + u))
                        nc.scalar.activation(sm[u], sm[u], ACT.Exp).then_inc(sexp.sem, 1)
                    for u in range(2):
                        act.wait_ge(ptt.sem, ptt.now(it, 2 * pg + u))
                        for j in range(1, 3):
                            nc.scalar.copy(pt[u][:, 4 * j:4 * j + 4, :],
                                           ps[:, 4 * u + j, :].rearrange("p (j c) -> p j c", j=4)).then_inc(pta.sem, 1)
                for u in range(2):
                    act.wait_ge(t2.sem, t2.now(it, u))
                    pack_high(nc, ps, 4 * u, pk[u], p2h)
                for u in range(2):
                    act.wait_ge(t3.sem, t3.now(it, u))
                    pack_high(nc, ps, 4 * u, pk[u], p3h)
                for u in range(2):
                    router.exponentials(act, it, u)
                for u in range(2):
                    act.wait_ge(fwps.sem, fwps.now(it, u))
                    nc.scalar.copy(fwt[u][0:16, :], ps[0:16, 4 * u + 3, :]).then_inc(fwh.sem, 1)
                for u in range(2):
                    act.wait_ge(st_pk[u].sem, st_pk[u].now(it, 0))
                    act.wait_ge(st_fw[u].sem, st_fw[u].now(it, 0))

        @block.tensor
        def _(pe):
            pe.wait_ge(identity, 2)
            pe.wait_ge(setup, 9)
            with pe.Fori(0, NT // 2) as it:
                for u in range(2):
                    pe.wait_ge(conv_h.sem, conv_h.now(it, u))
                    pe.wait_ge(conv_l.sem, conv_l.now(it, u))
                    hi, lo, m = 0, NC * 3 // 2, NC // 2
                    for c in range(2):
                        for h in range(2):
                            out = ps[:, 4 * u + 2 * c + h, 0:m]
                            w = w_at("pw", c * P, P)
                            xh, xl = cv[u][:, hi + h * m:hi + (h + 1) * m], cv[u][:, lo + h * m:lo + (h + 1) * m]
                            nc.tensor.matmul(out, W[:, 0, 0, w], xh, start=True, stop=False)
                            nc.tensor.matmul(out, W[:, 1, 0, w], xh, start=False, stop=False)
                            nc.tensor.matmul(out, W[:, 0, 0, w], xl, start=False, stop=False)
                            r = slice(64 * h, 64 * h + 64)
                            xh, xl = cv[u][r, hi + NC:hi + NC + m], cv[u][r, lo + NC:lo + NC + m]
                            nc.tensor.matmul(out, W[r, 0, 1, w], xh, start=False, stop=False)
                            nc.tensor.matmul(out, W[r, 1, 1, w], xh, start=False, stop=False)
                            last = nc.tensor.matmul(out, W[r, 0, 1, w], xl, start=False, stop=True)
                    last.then_inc(pw_done.sem, 1)
                for u in range(2):
                    pe.wait_ge(hp_h.sem, hp_h.now(it, u))
                    pe.wait_ge(hp_l.sem, hp_l.now(it, u))
                    for g in range(NG):
                        last = product5(nc, ps[:, 4 * u + g // 2, (g % 2) * 256:(g % 2) * 256 + 2 * KP], pk[u],
                                        slice(g * P, (g + 1) * P), W, w_at("fft"), False, True, True)
                    last.then_inc(ftd.sem, 1)
                for u in range(2):
                    pe.wait_ge(pq_h.sem, pq_h.now(it, u))
                    pe.wait_ge(pq_l.sem, pq_l.now(it, u))
                    for g in range(NG):
                        for c in range(2):
                            out = ps[:, 4 * u + 2 + g // 2, (g % 2) * 256 + c * KP:(g % 2) * 256 + (c + 1) * KP]
                            cc = slice(c * KP, (c + 1) * KP)
                            nc.tensor.matmul(out, CS[:, 0, c, :], pq[u][0][:, g, cc], start=True, stop=False)
                            nc.tensor.matmul(out, CS[:, 1, c, :], pq[u][0][:, g, cc], start=False, stop=False)
                            last = nc.tensor.matmul(out, CS[:, 0, c, :], pq[u][1][:, g, cc], start=False, stop=True)
                    last.then_inc(fts.sem, 1)
                for u in range(2):
                    pe.wait_ge(n1.sem, n1.now(it, u))
                    transpose_tile(nc, ps, 4 * u, nb[u], ident, t1)
                for u in range(2):
                    pe.wait_ge(p1h.sem, p1h.now(it, u))
                    pe.wait_ge(p1l.sem, p1l.now(it, u))
                    for c in range(2):
                        last = product5(nc, ps[:, 4 * u + 2 + c, :], pk[u], slice(0, N), W, w_at("q", c * P, P), True, True, True)
                    last.then_inc(q_ps.sem, 1)
                    for c in range(2):
                        last = product5(nc, ps[:, 4 * u + c, :], pk[u], slice(0, N), W, w_at("k", c * P, P), True, True, True)
                    last.then_inc(k_ps.sem, 1)
                for u in range(2):
                    pe.wait_ge(q_up.sem, q_up.now(it, u))
                    for g in range(NG):
                        last = product5(nc, ps[:, 4 * u + 2 + g // 2, (g % 2) * 256:(g % 2) * 256 + D], pk[u],
                                        slice(g * P, (g + 1) * P), W, w_at("v"), False, True, True)
                    last.then_inc(v_ps.sem, 1)
                for pg in range(2):
                    for u in range(2):
                        if pg == 0:
                            pe.wait_ge(ka_up.sem, ka_up.now(it, u))
                            pe.wait_ge(kv_up.sem, kv_up.now(it, u))
                            pe.wait_ge(v_up.sem, v_up.now(it, u))
                        else:
                            pe.wait_ge(at.sem, at.now(it, u))
                        for g in range(2):
                            for b in range(2):
                                tok = slice(((2 * pg + g) * 2 + b) * TP, ((2 * pg + g) * 2 + b + 1) * TP)
                                for j in range(PAIRS):
                                    c, r = divmod(j, 4)
                                    f = slice(32 * r, 32 * r + 32)
                                    last = nc.tensor.matmul(
                                        ps[64 * b:64 * b + 64, 4 * u + r, g * 256 + c * P:g * 256 + (c + 1) * P],
                                        q[u][f, c, tok], kx[u][f, c, :, tok], start=True, stop=True)
                        last.then_inc(sc.sem, 1)
                    for u in range(2):
                        pe.wait_ge(sexp.sem, sexp.now(it, 2 * pg + u))
                        for g in range(2):
                            for j in range(PAIRS):
                                k = g * PAIRS + j
                                last = nc.tensor.transpose(ps[:, 4 * u + k // 4, (k % 4) * P:(k % 4 + 1) * P],
                                                           sm[u][:, g, j, :], ident[:, :])
                        last.then_inc(ptt.sem, 1)
                    for u in range(2):
                        pe.wait_ge(pta.sem, pta.now(it, 2 * pg + u))
                        pe.wait_ge(ptv.sem, ptv.now(it, 2 * pg + u))
                        if pg == 0:
                            pe.wait_ge(vd_up.sem, vd_up.now(it, u))
                            pe.wait_ge(vo_up.sem, vo_up.now(it, u))
                        for g in range(2):
                            for b in range(2):
                                for j in range(PAIRS):
                                    k = g * PAIRS + j
                                    last = nc.tensor.matmul(
                                        ps[64 * b:64 * b + 64, 4 * u + 3, k * 34:(k + 1) * 34],
                                        pt[u][:, k, 64 * b:64 * b + 64],
                                        vblk[u][:, 2 * pg + g, b, j, :, :], start=True, stop=True)
                        last.then_inc(pv.sem, 1)
                for u in range(2):
                    pe.wait_ge(at.sem, at.now(it, 2 + u))
                    transpose_tile(nc, ps, 4 * u, nb[u], ident, t2)
                for u in range(2):
                    pe.wait_ge(p2h.sem, p2h.now(it, u))
                    pe.wait_ge(p2l.sem, p2l.now(it, u))
                    for g in range(NG):
                        last = product5(nc, ps[:, 4 * u + 2 + g // 2, (g % 2) * 256:(g % 2) * 256 + D], pk[u],
                                        slice(g * P, (g + 1) * P), W, w_at("proj"), False, True, True)
                    last.then_inc(pr.sem, 1)
                for u in range(2):
                    pe.wait_ge(tt.sem, tt.now(it, u))
                    transpose_tile(nc, ps, 4 * u, nb[u], ident, t3)
                for u in range(2):
                    pe.wait_ge(p3h.sem, p3h.now(it, u))
                    pe.wait_ge(p3l.sem, p3l.now(it, u))
                    for g in range(NG):
                        last = product5(nc, ps[:, 4 * u + 2, g * 16:(g + 1) * 16], pk[u],
                                        slice(g * P, (g + 1) * P), W, w_at("gate"), False, True, True)
                    last.then_inc(gt.sem, 1)
                for u in range(2):
                    router.spread(pe, ps, 4 * u + 3, ident, fwps, it, u)


HID = 3072
CHUNKS = HID // P
LAG = 3


def round_constants(nc, stack, prefix, src, out):
    with ExitStack() as ctx:
        stage = ctx.enter_context(nc.sbuf_tensor(f"{prefix}_stage", list(src.shape), F32))
        loaded = stack.new(f"{prefix}_loaded")
        rounded = stack.new(f"{prefix}_rounded")
        block = ctx.enter_context(nc.Block())

        @block.sync
        def _(sp):
            sp.dma_start(stage[:, :], src).then_inc(loaded, 16)

        @block.vector
        def _(dve):
            dve.wait_ge(loaded, 16)
            nc.vector.tensor_copy(out[:, :], stage[:, :]).then_inc(rounded, 1)


def moe_phase(nc, stack, io, pre, gated, x_in, gates_in, base_in, out):
    halves = 2 if gated else 1
    WAYS = 2 * CHUNKS
    with ExitStack() as ctx:
        sb = lambda n, shape, dt=F32: ctx.enter_context(nc.sbuf_tensor(f"{pre}_sb_{n}", shape, dt))
        sig = lambda n, per=1, step=1, ways=2, credit=False: Signal(nc, stack, f"{pre}_{n}", per, ways, step, credit)
        chunk = lambda n: sig(n, ways=WAYS, credit=True)
        dma = lambda n, credit=False: [sig(f"{n}{u}", 1, 16, 1, credit) for u in range(2)]
        ps = ctx.enter_context(nc.psum_tensor(f"{pre}_ps", [P, 8, 512], F32))
        W1 = sb("W1", [P, 2, 2, halves * HID], F32R)
        W2 = sb("W2", [P, 2, CHUNKS, D], F32R)
        B2 = sb("B2", [64, 2, D], F32R)
        SEL = sb("SEL", [64, HID], F32R)
        b1 = sb("b1", [P, halves, CHUNKS])
        flat = lambda ap: ap.rearrange("p a n -> p (a n)")
        split_weights(nc, stack, f"{pre}w", [
            (io[f"{pre}_w1"].rearrange("p a n -> p (a n)"), flat(W1[:, 0]), flat(W1[:, 1])),
            (io[f"{pre}_w2"].rearrange("p a n -> p (a n)"), flat(W2[:, 0]), flat(W2[:, 1])),
            (io[f"{pre}_b2"], B2[:, 0, :], B2[:, 1, :])])
        round_constants(nc, stack, f"{pre}s", io[f"{pre}_sel"], SEL)
        pk = [sb(f"pk{u}", [P, 3, N], F32R) for u in range(2)]
        fwt = [sb(f"fwt{u}", [64, N], F32R) for u in range(2)]
        hb = [sb(f"hb{u}", [P, NG, D]) for u in range(2)]
        g = [sb(f"g{j}", [P, N]) for j in range(3)]
        s = [sb(f"s{j}", [P, N]) for j in range(2)]
        lin = [sb(f"lin{j}", [P, N]) for j in range(2)]
        hh = [sb(f"hh{j}", [P, N], F32R) for j in range(3)]
        hl = [sb(f"hl{j}", [P, N], F32R) for j in range(3)]
        in_x, in_f, in_b = dma("inx"), dma("inf"), dma("inb")
        stored = dma("st", credit=True)
        consts = stack.new(f"{pre}_consts")
        plus = stack.new(f"{pre}_plus")
        up, act1, mul, gat, high, low = (chunk(n) for n in ("up", "act1", "mul", "gat", "high", "low"))
        pre_g, pre_l, mix, down = (chunk(n) for n in ("preg", "prel", "mix", "down"))
        summed = sig("summed", credit=True)
        block = ctx.enter_context(nc.Block())

        @block.sync
        def _(sp):
            sp.dma_start(b1[:, :, :], io[f"{pre}_b1"]).then_inc(consts, 16)
            with sp.Fori(0, NT // 2) as it:
                for u in range(2):
                    sp.wait_ge(stored[u].sem, stored[u].last(it, 0))
                    sp.sem_inc(stack.passed, 1)
                    sp.wait_ge(down.sem, down.last(it, u * CHUNKS + CHUNKS - 1))
                    sp.sem_inc(stack.passed, 1)
                    sp.dma_start(pk[u][:, :, :].bitcast(F32), x_in[it * 2 + u]).then_inc(in_x[u].sem, 16)
                    sp.dma_start(fwt[u][:, :].bitcast(F32), gates_in[it * 2 + u]).then_inc(in_f[u].sem, 16)
                    sp.dma_start(hb[u][:, :, :], base_in[it * 2 + u]).then_inc(in_b[u].sem, 16)
            for u in range(2):
                sp.wait_ge(stored[u].sem, stored[u].now(NT // 2 - 1, 0))
                sp.sem_inc(stack.passed, 1)

        @block.gpsimd
        def _(pool):
            if gated:
                for sg in (mul, low):
                    sg.credit(pool)
                with pool.Fori(0, NT // 2) as it:
                    for k in range(WAYS + 1):
                        if k < WAYS:
                            pool.wait_ge(act1.sem, act1.now(it, k))
                            nc.gpsimd.tensor_tensor(g[k % 3][:, :], g[k % 3][:, :], s[k % 2][:, :], ALU.mult).then_inc(mul.sem, 1)
                        if k >= 1:
                            j = k - 1
                            pool.wait_ge(high.sem, high.now(it, j))
                            nc.gpsimd.tensor_tensor(hl[j % 3][:, :], g[j % 3][:, :], hh[j % 3][:, :].bitcast(F32),
                                                    ALU.subtract).then_inc(low.sem, 1)

        @block.scalar
        def _(act):
            act.wait_ge(consts, 16)
            for u in range(2):
                stored[u].credit(act)
            act1.credit(act)
            high.credit(act)

            def to_high(it, j):
                act.wait_ge(gat.sem, gat.now(it, j))
                act.wait_ge(down.sem, down.back(it, j - 3))
                nc.scalar.copy(hh[j % 3][:, :], g[j % 3][:, :]).then_inc(high.sem, 1)

            def store(it, u):
                act.wait_ge(summed.sem, summed.now(it, u))
                act.dma_start(out[it * 2 + u], hb[u][:, :, :]).then_inc(stored[u].sem, 16)

            with act.Fori(0, NT // 2) as it:
                for k in range(WAYS + 1):
                    if k < WAYS:
                        if gated:
                            act.wait_ge(pre_g.sem, pre_g.now(it, k))
                            act.wait_ge(mul.sem, mul.back(it, k - 2))
                            nc.scalar.activation(s[k % 2][:, :], g[k % 3][:, :], ACT.Sigmoid, scale=1.702).then_inc(act1.sem, 1)
                        else:
                            act.wait_ge(up.sem, up.now(it, k))
                            act.wait_ge(gat.sem, gat.back(it, k - 2))
                            nc.scalar.activation(s[k % 2][:, :], ps[:, k % 2, :], ACT.Gelu,
                                                 bias=b1[:, 0, k % CHUNKS:k % CHUNKS + 1]).then_inc(act1.sem, 1)
                    if k >= 1:
                        to_high(it, k - 1)
                    if k == CHUNKS + LAG + 1:
                        store(it, 0)
                store(it, 1)

        @block.vector
        def _(dve):
            dve.wait_ge(consts, 16)
            if gated:
                nc.vector.tensor_scalar(b1[:, 1, :], b1[:, 1, :], 1.0, None, ALU.add).then_inc(plus, 1)
                dve.wait_ge(plus, 1)
            for sg in ((pre_g, pre_l, mix, gat) if gated else (low, gat)):
                sg.credit(dve)
            summed.credit(dve)

            def sum_up(it, u):
                dve.wait_ge(down.sem, down.now(it, u * CHUNKS + CHUNKS - 1))
                dve.wait_ge(in_b[u].sem, in_b[u].now(it, 0))
                o = ps[:, 6:8, :].rearrange("p b (h n) -> p b h n", h=2)[:, :, :, 0:D]
                hv = hb[u][:, :, :].rearrange("p (b h) n -> p b h n", b=2)
                nc.vector.tensor_tensor(hv, o, hv, ALU.add).then_inc(summed.sem, 1)

            with dve.Fori(0, NT // 2) as it:
                for k in range(WAYS + 1):
                    c = k % CHUNKS
                    if k < WAYS and gated:
                        dve.wait_ge(up.sem, up.now(it, k))
                        dve.wait_ge(low.sem, low.back(it, k - 3))
                        nc.vector.tensor_scalar(g[k % 3][:, :], ps[:, k % 2, :], b1[:, 0, c:c + 1], 7.0,
                                                ALU.add, ALU.min).then_inc(pre_g.sem, 1)
                        dve.wait_ge(mix.sem, mix.back(it, k - 2))
                        nc.vector.tensor_scalar(lin[k % 2][:, :], ps[:, 2 + k % 2, :], b1[:, 1, c:c + 1], 8.0,
                                                ALU.add, ALU.min).then_inc(pre_l.sem, 1)
                    if k >= 1:
                        j = k - 1
                        if gated:
                            dve.wait_ge(mul.sem, mul.now(it, j))
                            dve.wait_ge(pre_l.sem, pre_l.now(it, j))
                            nc.vector.scalar_tensor_tensor(g[j % 3][:, :], lin[j % 2][:, :], -6.0, g[j % 3][:, :],
                                                           ALU.max, ALU.mult).then_inc(mix.sem, 1)
                            dve.wait_ge(mix.sem, mix.now(it, j))
                            nc.vector.tensor_tensor(g[j % 3][:, :], g[j % 3][:, :], ps[:, 4 + j % 2, :],
                                                    ALU.mult).then_inc(gat.sem, 1)
                        else:
                            dve.wait_ge(act1.sem, act1.now(it, j))
                            dve.wait_ge(low.sem, low.back(it, j - 3))
                            nc.vector.tensor_tensor(g[j % 3][:, :], s[j % 2][:, :], ps[:, 4 + j % 2, :],
                                                    ALU.mult).then_inc(gat.sem, 1)
                            dve.wait_ge(high.sem, high.now(it, j))
                            nc.vector.tensor_tensor(hl[j % 3][:, :], g[j % 3][:, :], hh[j % 3][:, :].bitcast(F32),
                                                    ALU.subtract).then_inc(low.sem, 1)
                    if k == CHUNKS + LAG:
                        sum_up(it, 0)
                sum_up(it, 1)

        @block.tensor
        def _(pe):
            for sg in (up, down):
                sg.credit(pe)

            def first(it, k):
                u, c = divmod(k, CHUNKS)
                if c == 0:
                    pe.wait_ge(in_x[u].sem, in_x[u].now(it, 0))
                    pe.wait_ge(in_f[u].sem, in_f[u].now(it, 0))
                if gated:
                    pe.wait_ge(pre_l.sem, pre_l.back(it, k - 2))
                else:
                    pe.wait_ge(act1.sem, act1.back(it, k - 2))
                for h in range(halves):
                    at = (c * halves + h) * P
                    product5(nc, ps[:, 2 * h + k % 2, :], pk[u], slice(0, N), W1, slice(at, at + P), True, True, True)
                pe.wait_ge(gat.sem, gat.back(it, k - 2))
                nc.tensor.matmul(ps[:, 4 + k % 2, :], SEL[:, c * P:(c + 1) * P], fwt[u][:, :],
                                 start=True, stop=True).then_inc(up.sem, 1)

            def second(it, k):
                u, c = divmod(k, CHUNKS)
                outs = [ps[:, 6 + t // 2, (t % 2) * 256:(t % 2) * 256 + D] for t in range(NG)]
                if c == 0:
                    pe.wait_ge(summed.sem, summed.back(it, u - 1))
                    for t in range(NG):
                        for hlw in range(2):
                            nc.tensor.matmul(outs[t], fwt[u][:, t * P:(t + 1) * P], B2[:, hlw, :],
                                             start=t % 2 == 0 and hlw == 0, stop=False, skip_group_check=True)
                pe.wait_ge(high.sem, high.now(it, k))
                pe.wait_ge(low.sem, low.now(it, k))
                for t in range(NG):
                    tok = slice(t * P, (t + 1) * P)
                    for a, hlw in ((hh, 0), (hh, 1), (hl, 0)):
                        last = nc.tensor.matmul(outs[t], a[k % 3][:, tok], W2[:, hlw, c, :], start=False,
                                                stop=c == CHUNKS - 1 and a is hl, skip_group_check=True)
                last.then_inc(down.sem, 1)

            with pe.Fori(0, NT // 2) as it:
                for k in range(WAYS + LAG):
                    if k < WAYS:
                        first(it, k)
                    if k >= LAG:
                        second(it, k - LAG)


KEYS = N + N // 2
KF = 4 * D
KFC = KF // P


def phase_c(nc, stack, io):
    with ExitStack() as ctx:
        sb = lambda n, shape, dt=F32: ctx.enter_context(nc.sbuf_tensor(f"c_sb_{n}", shape, dt))
        two = lambda n, shape, dt=F32: [sb(f"{n}{u}", shape, dt) for u in range(2)]
        sig = lambda n, per=1, step=1, ways=2, credit=False: Signal(nc, stack, f"c_{n}", per, ways, step, credit)
        dma = lambda n, credit=False: [sig(f"{n}{u}", 1, 16, 1, credit) for u in range(2)]
        ps = ctx.enter_context(nc.psum_tensor("c_ps", [P, 8, 512], F32))
        W = sb("W", [P, 2, 2, C_TOT], F32R)
        WV = sb("WV", [P, 2, KFC, D], F32R)
        rows = sb("rows", [P, len(C_ROW), D])
        decay, bonus = sb("decay", [P, KEYS]), sb("bonus", [P, KEYS])
        ident = sb("ident", [P, P])
        half = sb("half", [P, NG])
        flat = lambda ap: ap.rearrange("p a n -> p (a n)")
        split_weights(nc, stack, "cw", [
            (flat(io["c_w"]), flat(W[:, 0]), flat(W[:, 1])),
            (flat(io["c_wv"]), flat(WV[:, 0]), flat(WV[:, 1]))])
        pk = two("pk", [P, 3, N], F32R)
        hb, xb, nb = two("hb", [P, NG, D]), two("xb", [P, NG, D]), two("nb", [P, NG, D])
        kk, vv, er = two("kk", [P, KEYS]), two("vv", [P, KEYS]), two("er", [P, KEYS])
        ms, sa, sb_ = (two(n, [P, 2, KEYS + 1]) for n in ("ms", "sa", "sbb"))
        e1, e2 = two("e1", [P, 2, KEYS]), two("e2", [P, 2, KEYS])
        t1, t2 = two("t1", [P, KEYS]), two("t2", [P, KEYS])
        yh, yl = two("yh", [P, KEYS], F32R), two("yl", [P, KEYS], F32R)
        rl = [sb(f"rl{j}", [P, N]) for j in range(2)]
        fh = [sb(f"fh{j}", [P, N], F32R) for j in range(2)]
        fl = [sb(f"fl{j}", [P, N], F32R) for j in range(2)]
        st, mv = two("st", [P, NG, 6]), two("mv", [P, NG, 2])
        ra, rb, rs, rc = (two(n, [P, NG]) for n in ("ra", "rb", "rs", "rc"))
        router = Router(nc, stack, ctx, "cr", 4, 1)

        consts = stack.new("c_consts")
        identity = stack.new("c_identity")
        setup, cleared = (stack.new(n) for n in ("c_setup", "c_cleared"))
        loaded = dma("loaded")
        st_x, st_mask, st_base = dma("stx", True), dma("stmask", True), dma("stbase", True)
        s1, m1, pl1, n3, l1, l1w, l1b = sig("s1", 4), sig("m1", 4), sig("pl1", 7), sig("n3", 4), sig("l1", 4), sig("l1w"), sig("l1b")
        tr1, p1h, p1l = sig("tr1"), sig("p1h", 2), sig("p1l", 2)
        k_ps, v_ps, r_ps = sig("kps"), sig("vps"), sig("rps")
        k_up, v_up, r_up, kpad = sig("kup", 3), sig("vup", 3), sig("rup", 3), sig("kpad")
        mscan, x1a, x1b, x2, kb = sig("mscan", 2), sig("x1a", 2), sig("x1b", 2), sig("x2", 2), sig("kb")
        ex1, ex2, ev, ascan, bscan = sig("ex1", 2), sig("ex2", 2), sig("ev", 2), sig("ascan", 2), sig("bscan", 2)
        mm, df, exd, wa, wb, wv_ = sig("mm", 2), sig("df", 3), sig("exd", 3), sig("wa", 2), sig("wb", 2), sig("wv")
        nsum, dsum, den, dinv, yy, y_h, y_l = sig("nsum", 2), sig("dsum", 2), sig("den"), sig("dinv"), sig("yy"), sig("yh"), sig("yl")
        o_ps, x_up = sig("ops"), sig("xup")
        s2, m2, pl2, l2, l2w, l2b = sig("s2", 4), sig("m2", 4), sig("pl2", 2), sig("l2", 4), sig("l2w"), sig("l2b")
        tr2, p2h, p2l = sig("tr2"), sig("p2h", 2), sig("p2l", 2)
        g_ps, g_ex, g_kv, x2_up, h_up = sig("gps"), sig("gex"), sig("gkv"), sig("x2up"), sig("hup")
        seq = lambda n: sig(n, ways=2 * KFC, credit=True)
        f_ps, f_relu, f_sq, f_h, f_l, f_used = (seq(n) for n in ("fps", "frelu", "fsq", "fh", "fl", "fused"))
        s3, m3, pl3, n4 = sig("s3", 4), sig("m3", 4), sig("pl3", 2), sig("n4", 4)
        tr3, p3h, p3l = sig("tr3"), sig("p3h", 2), sig("p3l", 2)
        gt = sig("gt")
        block = ctx.enter_context(nc.Block())
        row = lambda n: rows[:, C_ROW[n], :]
        w_at = lambda n, a=0, m=None: slice(C_AT[n][0] + a, C_AT[n][0] + a + (m or C_AT[n][1]))
        before = lambda x, d: x[:, d, 0:KEYS] if d == 0 else x[:, d, 1:KEYS + 1]
        after = lambda x, d: x[:, d, 1:KEYS + 1] if d == 0 else x[:, d, 0:KEYS]

        def scan(out, d0, d1, initial, op0, op1, d):
            if d == 1:
                out, d0, d1 = out[:, ::-1], d0[:, ::-1], d1[:, ::-1]
            return nc.vector.tensor_tensor_scan(out, d0, d1, initial, op0=op0, op1=op1)

        def two_banks(u, b0, n):
            return ps[:, 4 * u + b0:4 * u + b0 + 2, :].rearrange("p b (h n) -> p b h n", h=2)[:, :, :, 0:n]

        def split4(ap):
            return ap.rearrange("p (b h) n -> p b h n", b=2)

        def token_rows(tile):
            return io["rows2"].rearrange("(t g p) d -> t p g d", g=NG, p=P)[tile]

        @block.sync
        def _(sp):
            sp.dma_start(rows[:, :, :], io["c_rows"]).then_inc(consts, 16)
            sp.dma_start(decay[:, :], io["c_decay"]).then_inc(consts, 16)
            sp.dma_start(bonus[:, :], io["c_bonus"]).then_inc(consts, 16)
            for s in (*st_base, *st_x, *st_mask):
                s.credit(sp)
            with sp.Fori(0, NT // 2) as it:
                for u in range(2):
                    sp.wait_ge(st_base[u].sem, st_base[u].last(it, 0))
                    sp.sem_inc(stack.passed, 1)
                    sp.dma_start(hb[u][:, :, :], io["h2"][it * 2 + u]).then_inc(loaded[u].sem, 16)
                for u in range(2):
                    sp.wait_ge(h_up.sem, h_up.now(it, u))
                    sp.sem_inc(stack.passed, 1)
                    sp.dma_start(token_rows(it * 2 + u)[:, :, D:2 * D], hb[u][:, :, :]).then_inc(st_base[u].sem, 16)
                for u in range(2):
                    sp.wait_ge(n4.sem, n4.now(it, u))
                    sp.sem_inc(stack.passed, 1)
                    sp.dma_start(token_rows(it * 2 + u)[:, :, 0:D], nb[u][:, :, :]).then_inc(st_x[u].sem, 16)
                for u in range(2):
                    sp.wait_ge(router.gates.sem, router.gates.now(it, u))
                    sp.sem_inc(stack.passed, 1)
                    sp.dma_start(io["mask2"].rearrange("p (t g) e -> t p g e", g=NG)[it * 2 + u],
                                 router.fw[u][:, :, 0:4]).then_inc(st_mask[u].sem, 16)
            for u in range(2):
                for s in (st_base, st_x, st_mask):
                    sp.wait_ge(s[u].sem, s[u].now(NT // 2 - 1, 0))
                    sp.sem_inc(stack.passed, 1)

        @block.gpsimd
        def _(pool):
            fill_identity(nc, pool, ident, identity)
            nc.gpsimd.memset(half[:, :], -0.5).then_inc(setup, 1)
            pool.wait_ge(setup, 1)

            def power(out, x, s):
                nc.gpsimd.tensor_tensor(out[:, :], x[:, :], half[:, :], ALU.pow).then_inc(s.sem, 1)

            with pool.Fori(0, NT // 2) as it:
                for u in range(2):
                    var = mv[u][:, :, 1]
                    pool.wait_ge(m1.sem, m1.now(it, u))
                    pool.sem_inc(stack.passed, 1)
                    nc.gpsimd.tensor_scalar(ra[u][:, :], var, EPS, None, ALU.add).then_inc(pl1.sem, 1)
                    pool.wait_ge(pl1.sem, pl1.now(it, u, 1))
                    power(rs[u], ra[u], pl1)
                    pool.wait_ge(pl1.sem, pl1.now(it, u, 2))
                    nc.gpsimd.tensor_tensor(rb[u][:, :], rs[u][:, :], rs[u][:, :], ALU.mult).then_inc(pl1.sem, 1)
                    pool.wait_ge(pl1.sem, pl1.now(it, u, 3))
                    nc.gpsimd.tensor_tensor(rb[u][:, :], rb[u][:, :], var, ALU.mult).then_inc(pl1.sem, 1)
                    pool.wait_ge(pl1.sem, pl1.now(it, u, 4))
                    pool.sem_inc(stack.passed, 1)
                    nc.gpsimd.tensor_scalar(rb[u][:, :], rb[u][:, :], EPS, None, ALU.add).then_inc(pl1.sem, 1)
                    pool.wait_ge(pl1.sem, pl1.now(it, u, 5))
                    power(ra[u], rb[u], pl1)
                    pool.wait_ge(pl1.sem, pl1.now(it, u, 6))
                    nc.gpsimd.tensor_tensor(rc[u][:, :], rs[u][:, :], ra[u][:, :], ALU.mult).then_inc(pl1.sem, 1)
                for u in range(2):
                    pool.wait_ge(kpad.sem, kpad.now(it, u))
                    for d in range(2):
                        pool.wait_ge(mscan.sem, mscan.now(it, u, d + 1))
                        nc.gpsimd.tensor_tensor(e2[u][:, d, :], kk[u][:, :], after(ms[u], d), ALU.subtract).then_inc(x2.sem, 1)
                    pool.wait_ge(ev.sem, ev.now(it, u, 2))
                    pool.wait_ge(ascan.sem, ascan.now(it, u, 2))
                    nc.gpsimd.tensor_tensor(t1[u][:, :], kk[u][:, :], bonus[:, :], ALU.add).then_inc(kb.sem, 1)
                for u in range(2):
                    for d in range(2):
                        pool.wait_ge(exd.sem, exd.now(it, u, d + 1))
                        pool.wait_ge(bscan.sem, bscan.now(it, u, d + 1))
                        x = before(sb_[u], d)
                        nc.gpsimd.tensor_tensor(x, x, e1[u][:, d, :], ALU.mult).then_inc(wb.sem, 1)
                    pool.wait_ge(wb.sem, wb.now(it, u, 2))
                    nc.gpsimd.tensor_tensor(e2[u][:, 0, :], before(sb_[u], 1), before(sb_[u], 0), ALU.add).then_inc(dsum.sem, 1)
                    pool.wait_ge(dsum.sem, dsum.now(it, u, 1))
                    pool.wait_ge(exd.sem, exd.now(it, u, 3))
                    nc.gpsimd.tensor_tensor(e2[u][:, 0, :], e2[u][:, 0, :], t1[u][:, :], ALU.add).then_inc(dsum.sem, 1)
                for (m, pl) in ((m2, pl2), (m3, pl3)):
                    for u in range(2):
                        pool.wait_ge(m.sem, m.now(it, u))
                        pool.sem_inc(stack.passed, 1)
                        nc.gpsimd.tensor_scalar(ra[u][:, :], mv[u][:, :, 1], EPS, None, ALU.add).then_inc(pl.sem, 1)
                        pool.wait_ge(pl.sem, pl.now(it, u, 1))
                        power(rs[u], ra[u], pl)

        @block.vector
        def _(dve):
            dve.wait_ge(consts, 48)
            router.start(dve)
            live = lambda x: x[:, :].rearrange("p (b s) -> p b s", s=TP)[:, :, 0:T]
            nc.vector.tensor_scalar(live(decay), live(decay), 1.0 / T, None, ALU.mult).then_inc(cleared, 1)
            nc.vector.tensor_scalar(live(bonus), live(bonus), 1.0 / T, None, ALU.mult).then_inc(cleared, 1)
            for u in range(2):
                for x, v in ((ms, NEG), (sa, 0.0), (sb_, 0.0)):
                    nc.vector.memset(x[u][:, 0, 0:1], v).then_inc(cleared, 1)
                    nc.vector.memset(x[u][:, 1, KEYS:KEYS + 1], v).then_inc(cleared, 1)
            dve.wait_ge(setup, 1)
            dve.wait_ge(cleared, 14)
            for s in (f_sq, f_l):
                s.credit(dve)
            TT = nc.vector.tensor_tensor
            with dve.Fori(0, NT // 2) as it:
                for u in range(2):
                    dve.wait_ge(loaded[u].sem, loaded[u].now(it, 0))
                    norm_stats(nc, stack, dve, hb[u], st[u], mv[u], s1, m1, it, u)
                for u in range(2):
                    dve.wait_ge(pl1.sem, pl1.now(it, u))
                    norm_apply(nc, nb[u], hb[u], mv[u], rc[u], l1)
                for u in range(2):
                    dve.wait_ge(l1.sem, l1.now(it, u))
                    TT(nb[u][:, :, :], nb[u][:, :, :], bcast_groups(row("ln1w")), ALU.mult).then_inc(l1w.sem, 1)
                for u in range(2):
                    dve.wait_ge(l1w.sem, l1w.now(it, u))
                    TT(nb[u][:, :, :], nb[u][:, :, :], bcast_groups(row("ln1b")), ALU.add).then_inc(l1b.sem, 1)
                for u in range(2):
                    norm_apply(nc, xb[u], hb[u], mv[u], rs[u], n3)
                for u in range(2):
                    dve.wait_ge(tr1.sem, tr1.now(it, u))
                    pack_low(nc, dve, ps, 4 * u, pk[u], p1h, p1l, it, u)
                for u in range(2):
                    dve.wait_ge(k_up.sem, k_up.now(it, u))
                    nc.vector.memset(kk[u][:, :].rearrange("p (b s) -> p b s", s=TP)[:, :, T:TP], NEG).then_inc(kpad.sem, 1)
                for u in range(2):
                    dve.wait_ge(kpad.sem, kpad.now(it, u))
                    for d in range(2):
                        scan(after(ms[u], d), decay[:, :], kk[u][:, :], NEG, ALU.add, ALU.max, d).then_inc(mscan.sem, 1)
                for u in range(2):
                    for d in range(2):
                        dve.wait_ge(mscan.sem, mscan.now(it, u, d + 1))
                        TT(e1[u][:, d, :], before(ms[u], d), decay[:, :], ALU.add).then_inc(x1a.sem, 1)
                    for d in range(2):
                        dve.wait_ge(x1a.sem, x1a.now(it, u, d + 1))
                        TT(e1[u][:, d, :], e1[u][:, d, :], after(ms[u], d), ALU.subtract).then_inc(x1b.sem, 1)
                for u in range(2):
                    for d in range(2):
                        dve.wait_ge(ex1.sem, ex1.now(it, u, d + 1))
                        dve.wait_ge(ex2.sem, ex2.now(it, u, d + 1))
                        scan(after(sb_[u], d), e1[u][:, d, :], e2[u][:, d, :], 0.0, ALU.mult, ALU.add, d).then_inc(bscan.sem, 1)
                        dve.wait_ge(v_up.sem, v_up.now(it, u))
                        if d == 1:
                            dve.wait_ge(ascan.sem, ascan.now(it, u, 1))
                        TT(t1[u][:, :], e2[u][:, d, :], vv[u][:, :], ALU.mult).then_inc(ev.sem, 1)
                        dve.wait_ge(ev.sem, ev.now(it, u, d + 1))
                        scan(after(sa[u], d), e1[u][:, d, :], t1[u][:, :], 0.0, ALU.mult, ALU.add, d).then_inc(ascan.sem, 1)
                for u in range(2):
                    TT(t2[u][:, :], before(ms[u], 0), before(ms[u], 1), ALU.max).then_inc(mm.sem, 1)
                    dve.wait_ge(kb.sem, kb.now(it, u))
                    dve.wait_ge(mm.sem, mm.now(it, u, 1))
                    TT(t2[u][:, :], t2[u][:, :], t1[u][:, :], ALU.max).then_inc(mm.sem, 1)
                    dve.wait_ge(mm.sem, mm.now(it, u, 2))
                    dve.wait_ge(ascan.sem, ascan.now(it, u))
                    dve.wait_ge(bscan.sem, bscan.now(it, u))
                    for d in range(2):
                        TT(e1[u][:, d, :], before(ms[u], d), t2[u][:, :], ALU.subtract).then_inc(df.sem, 1)
                    TT(t1[u][:, :], t1[u][:, :], t2[u][:, :], ALU.subtract).then_inc(df.sem, 1)
                for u in range(2):
                    for d in range(2):
                        dve.wait_ge(exd.sem, exd.now(it, u, d + 1))
                        TT(before(sa[u], d), before(sa[u], d), e1[u][:, d, :], ALU.mult).then_inc(wa.sem, 1)
                    dve.wait_ge(exd.sem, exd.now(it, u, 3))
                    TT(vv[u][:, :], vv[u][:, :], t1[u][:, :], ALU.mult).then_inc(wv_.sem, 1)
                    for d in range(2):
                        dve.wait_ge(wa.sem, wa.now(it, u, d + 1))
                        if d == 0:
                            dve.wait_ge(wv_.sem, wv_.now(it, u))
                        else:
                            dve.wait_ge(nsum.sem, nsum.now(it, u, 1))
                        TT(vv[u][:, :], vv[u][:, :], before(sa[u], d), ALU.add).then_inc(nsum.sem, 1)
                for u in range(2):
                    dve.wait_ge(dsum.sem, dsum.now(it, u))
                    dve.wait_ge(r_up.sem, r_up.now(it, u))
                    nc.vector.scalar_tensor_tensor(t2[u][:, :], er[u][:, :], 1.0, e2[u][:, 0, :], ALU.add, ALU.mult).then_inc(den.sem, 1)
                    dve.wait_ge(den.sem, den.now(it, u))
                    nc.vector.reciprocal(t2[u][:, :], t2[u][:, :]).then_inc(dinv.sem, 1)
                    dve.wait_ge(dinv.sem, dinv.now(it, u))
                    dve.wait_ge(nsum.sem, nsum.now(it, u))
                    TT(t1[u][:, :], vv[u][:, :], t2[u][:, :], ALU.mult).then_inc(yy.sem, 1)
                for u in range(2):
                    dve.wait_ge(y_h.sem, y_h.now(it, u))
                    TT(yl[u][:, :], t1[u][:, :], yh[u][:, :].bitcast(F32), ALU.subtract).then_inc(y_l.sem, 1)
                for u in range(2):
                    dve.wait_ge(o_ps.sem, o_ps.now(it, u))
                    dve.wait_ge(n3.sem, n3.now(it, u))
                    TT(split4(xb[u][:, :, :]), two_banks(u, 0, D), split4(xb[u][:, :, :]), ALU.add).then_inc(x_up.sem, 1)
                for u in range(2):
                    dve.wait_ge(x_up.sem, x_up.now(it, u))
                    norm_stats(nc, stack, dve, xb[u], st[u], mv[u], s2, m2, it, u)
                for u in range(2):
                    dve.wait_ge(pl2.sem, pl2.now(it, u))
                    norm_apply(nc, nb[u], xb[u], mv[u], rs[u], l2)
                for u in range(2):
                    dve.wait_ge(l2.sem, l2.now(it, u))
                    TT(nb[u][:, :, :], nb[u][:, :, :], bcast_groups(row("ln2w")), ALU.mult).then_inc(l2w.sem, 1)
                for u in range(2):
                    dve.wait_ge(l2w.sem, l2w.now(it, u))
                    TT(nb[u][:, :, :], nb[u][:, :, :], bcast_groups(row("ln2b")), ALU.add).then_inc(l2b.sem, 1)
                for u in range(2):
                    dve.wait_ge(tr2.sem, tr2.now(it, u))
                    pack_low(nc, dve, ps, 4 * u + 2, pk[u], p2h, p2l, it, u)
                for k in range(2 * KFC + 1):
                    if k < 2 * KFC:
                        dve.wait_ge(f_relu.sem, f_relu.now(it, k))
                        TT(rl[k % 2][:, :], rl[k % 2][:, :], rl[k % 2][:, :], ALU.mult).then_inc(f_sq.sem, 1)
                    if k >= 1:
                        j = k - 1
                        dve.wait_ge(f_h.sem, f_h.now(it, j))
                        TT(fl[j % 2][:, :], rl[j % 2][:, :], fh[j % 2][:, :].bitcast(F32), ALU.subtract).then_inc(f_l.sem, 1)
                for u in range(2):
                    dve.wait_ge(f_used.sem, f_used.now(it, u * KFC + KFC - 1))
                    dve.wait_ge(g_ex.sem, g_ex.now(it, u))
                    TT(split4(nb[u][:, :, :]), two_banks(u, 0, D), split4(nb[u][:, :, :]), ALU.mult).then_inc(g_kv.sem, 1)
                    dve.wait_ge(g_kv.sem, g_kv.now(it, u))
                    TT(xb[u][:, :, :], xb[u][:, :, :], nb[u][:, :, :], ALU.add).then_inc(x2_up.sem, 1)
                    dve.wait_ge(x2_up.sem, x2_up.now(it, u))
                    TT(hb[u][:, :, :], hb[u][:, :, :], xb[u][:, :, :], ALU.add).then_inc(h_up.sem, 1)
                for u in range(2):
                    dve.wait_ge(h_up.sem, h_up.now(it, u))
                    norm_stats(nc, stack, dve, hb[u], st[u], mv[u], s3, m3, it, u)
                for u in range(2):
                    dve.wait_ge(pl3.sem, pl3.now(it, u))
                    norm_apply(nc, nb[u], hb[u], mv[u], rs[u], n4)
                for u in range(2):
                    dve.wait_ge(tr3.sem, tr3.now(it, u))
                    pack_low(nc, dve, ps, 4 * u + 2, pk[u], p3h, p3l, it, u)
                for u in range(2):
                    dve.wait_ge(gt.sem, gt.now(it, u))
                    router.choose(dve, ps[:, 4 * u, 0:NG * 16].rearrange("p (g e) -> p g e", g=NG)[:, :, 0:4], row("gateb"), it, u)
                for u in range(2):
                    dve.wait_ge(st_x[u].sem, st_x[u].now(it, 0))
                    dve.wait_ge(st_mask[u].sem, st_mask[u].now(it, 0))

        @block.scalar
        def _(act):
            act.wait_ge(consts, 48)
            act.wait_ge(cleared, 14)
            for s in (f_relu, f_h):
                s.credit(act)

            def unfold(u, bank, out, sg, func=ACT.Copy, scale=1.0):
                h = N // 2
                for o, i in ((out[:, 0:N], ps[:, bank, :]), (out[0:D2, N:KEYS], ps[0:D2, bank + 1, 0:h]),
                             (out[D2:P, N:KEYS], ps[D2:P, bank + 1, h:N])):
                    nc.scalar.activation(o, i, func, scale=scale).then_inc(sg.sem, 1)

            with act.Fori(0, NT // 2) as it:
                for u in range(2):
                    act.wait_ge(tr1.sem, tr1.now(it, u))
                    pack_high(nc, ps, 4 * u, pk[u], p1h)
                for u in range(2):
                    act.wait_ge(k_ps.sem, k_ps.now(it, u))
                    unfold(u, 4 * u + 2, kk[u], k_up)
                for u in range(2):
                    act.wait_ge(v_ps.sem, v_ps.now(it, u))
                    unfold(u, 4 * u, vv[u], v_up)
                for u in range(2):
                    act.wait_ge(r_ps.sem, r_ps.now(it, u))
                    unfold(u, 4 * u + 2, er[u], r_up, ACT.Exp, -1.0)
                for u in range(2):
                    for d in range(2):
                        act.wait_ge(x2.sem, x2.now(it, u, d + 1))
                        nc.scalar.activation(e2[u][:, d, :], e2[u][:, d, :], ACT.Exp).then_inc(ex2.sem, 1)
                        act.wait_ge(x1b.sem, x1b.now(it, u, d + 1))
                        nc.scalar.activation(e1[u][:, d, :], e1[u][:, d, :], ACT.Exp).then_inc(ex1.sem, 1)
                for u in range(2):
                    for d in range(2):
                        act.wait_ge(df.sem, df.now(it, u, d + 1))
                        nc.scalar.activation(e1[u][:, d, :], e1[u][:, d, :], ACT.Exp).then_inc(exd.sem, 1)
                    act.wait_ge(df.sem, df.now(it, u, 3))
                    nc.scalar.activation(t1[u][:, :], t1[u][:, :], ACT.Exp).then_inc(exd.sem, 1)
                for u in range(2):
                    act.wait_ge(yy.sem, yy.now(it, u))
                    nc.scalar.copy(yh[u][:, :], t1[u][:, :]).then_inc(y_h.sem, 1)
                for u in range(2):
                    act.wait_ge(tr2.sem, tr2.now(it, u))
                    pack_high(nc, ps, 4 * u + 2, pk[u], p2h)
                for u in range(2):
                    act.wait_ge(g_ps.sem, g_ps.now(it, u))
                    nc.scalar.activation(split4(nb[u][:, :, :]), two_banks(u, 0, D), ACT.Sigmoid).then_inc(g_ex.sem, 1)
                for k in range(2 * KFC + 1):
                    if k < 2 * KFC:
                        act.wait_ge(f_ps.sem, f_ps.now(it, k))
                        act.wait_ge(f_l.sem, f_l.back(it, k - 2))
                        u = k // KFC
                        nc.scalar.activation(rl[k % 2][:, :], ps[:, 4 * u + 2 + k % 2, :], ACT.Relu).then_inc(f_relu.sem, 1)
                    if k >= 1:
                        j = k - 1
                        act.wait_ge(f_sq.sem, f_sq.now(it, j))
                        act.wait_ge(f_used.sem, f_used.back(it, j - 2))
                        nc.scalar.copy(fh[j % 2][:, :], rl[j % 2][:, :]).then_inc(f_h.sem, 1)
                for u in range(2):
                    act.wait_ge(tr3.sem, tr3.now(it, u))
                    pack_high(nc, ps, 4 * u + 2, pk[u], p3h)

        @block.tensor
        def _(pe):
            pe.wait_ge(identity, 2)
            pe.wait_ge(cleared, 14)
            for s in (f_ps, f_used):
                s.credit(pe)

            def feature_major(u, b0, name, sg):
                for c in range(2):
                    last = product5(nc, ps[:, 4 * u + b0 + c, :], pk[u], slice(0, N), W, w_at(name, c * P, P), True, True, True)
                last.then_inc(sg.sem, 1)

            with pe.Fori(0, NT // 2) as it:
                for u in range(2):
                    pe.wait_ge(l1b.sem, l1b.now(it, u))
                    transpose_tile(nc, ps, 4 * u, nb[u], ident, tr1)
                for u in range(2):
                    pe.wait_ge(p1h.sem, p1h.now(it, u))
                    pe.wait_ge(p1l.sem, p1l.now(it, u))
                    feature_major(u, 2, "wk", k_ps)
                for u in range(2):
                    feature_major(u, 0, "wv", v_ps)
                for u in range(2):
                    pe.wait_ge(k_up.sem, k_up.now(it, u))
                    feature_major(u, 2, "wr", r_ps)
                for u in range(2):
                    pe.wait_ge(y_h.sem, y_h.now(it, u))
                    pe.wait_ge(y_l.sem, y_l.now(it, u))
                    for g in range(NG):
                        out = ps[:, 4 * u + g // 2, (g % 2) * 256:(g % 2) * 256 + D]
                        tok = slice(g * P, (g + 1) * P)
                        r = slice(D2 * (g // 2), D2 * (g // 2) + D2)
                        tail = slice(N + (g % 2) * P, N + (g % 2 + 1) * P)
                        w = w_at("wo")
                        steps = [(yh[u][:, tok], W[:, 0, 0, w]), (yh[u][:, tok], W[:, 1, 0, w]), (yl[u][:, tok], W[:, 0, 0, w]),
                                 (yh[u][r, tail], W[r, 0, 1, w]), (yh[u][r, tail], W[r, 1, 1, w]), (yl[u][r, tail], W[r, 0, 1, w])]
                        for n, (a, b) in enumerate(steps):
                            last = nc.tensor.matmul(out, a, b, start=n == 0, stop=n == 5)
                    last.then_inc(o_ps.sem, 1)
                for u in range(2):
                    pe.wait_ge(l2b.sem, l2b.now(it, u))
                    pe.wait_ge(r_up.sem, r_up.now(it, u))
                    transpose_tile(nc, ps, 4 * u + 2, nb[u], ident, tr2)
                for u in range(2):
                    pe.wait_ge(p2h.sem, p2h.now(it, u))
                    pe.wait_ge(p2l.sem, p2l.now(it, u))
                    for g in range(NG):
                        last = product5(nc, ps[:, 4 * u + g // 2, (g % 2) * 256:(g % 2) * 256 + D], pk[u],
                                        slice(g * P, (g + 1) * P), W, w_at("rf"), False, True, True)
                    last.then_inc(g_ps.sem, 1)

                def hidden(k):
                    u, c = divmod(k, KFC)
                    pe.wait_ge(f_relu.sem, f_relu.back(it, k - 2))
                    product5(nc, ps[:, 4 * u + 2 + k % 2, :], pk[u], slice(0, N), W,
                             w_at("kf", c * P, P), True, True, True).then_inc(f_ps.sem, 1)

                def values(k):
                    u, c = divmod(k, KFC)
                    if c == 0:
                        pe.wait_ge(g_ex.sem, g_ex.now(it, u))
                    pe.wait_ge(f_h.sem, f_h.now(it, k))
                    pe.wait_ge(f_l.sem, f_l.now(it, k))
                    for g in range(NG):
                        tok = slice(g * P, (g + 1) * P)
                        out = ps[:, 4 * u + g // 2, (g % 2) * 256:(g % 2) * 256 + D]
                        for n, (a, hlw) in enumerate(((fh, 0), (fh, 1), (fl, 0))):
                            last = nc.tensor.matmul(out, a[k % 2][:, tok], WV[:, hlw, c, :],
                                                    start=c == 0 and n == 0 and g % 2 == 0, stop=c == KFC - 1 and n == 2,
                                                    skip_group_check=True)
                    last.then_inc(f_used.sem, 1)

                for k in range(2 * KFC + 2):
                    if k < 2 * KFC:
                        hidden(k)
                    if k >= 2:
                        values(k - 2)
                for u in range(2):
                    pe.wait_ge(n4.sem, n4.now(it, u))
                    transpose_tile(nc, ps, 4 * u + 2, nb[u], ident, tr3)
                for u in range(2):
                    pe.wait_ge(p3h.sem, p3h.now(it, u))
                    pe.wait_ge(p3l.sem, p3l.now(it, u))
                    for g in range(NG):
                        last = product5(nc, ps[:, 4 * u, g * 16:(g + 1) * 16], pk[u],
                                        slice(g * P, (g + 1) * P), W, w_at("gate"), False, True, True)
                    last.then_inc(gt.sem, 1)


GROUPS = NT * NG
ROWS = GROUPS * P
LISTS = 4
WAYS_S = 6
NOWHERE = float(1 << 22)


def slot_blocks(k, experts):
    most = -(-B * T * k // P) + experts
    return -(-most // WAYS_S) * WAYS_S


E_D, K_D = 4, 1
BLK_D = slot_blocks(K_D, E_D)


def routing(nc, stack, io, pre, experts, blocks, mask_in, lists, row_ids, table, jobs):
    E, GE = experts, GROUPS * experts
    with ExitStack() as ctx:
        sb = lambda n, shape, dt=F32: ctx.enter_context(nc.sbuf_tensor(f"{pre}_rt_{n}", shape, dt))
        ps = ctx.enter_context(nc.psum_tensor(f"{pre}_rt_ps", [P, 4, 512], F32))
        assert GE % 512 in (0, GE) and GE <= 1024
        banks, width = -(-GE // 512), min(GE, 512)
        stage = sb("stage", [P, 2, P])
        tri = sb("tri", [P, 2, P], F32R)
        pad = sb("pad", [P, 2])
        steps = sb("steps", [P, GROUPS])
        order = sb("order", [P, blocks])
        ident = sb("ids", [P, GROUPS])
        mask = sb("mask", [P, GROUPS, E])
        chosen = sb("chosen", [P, GROUPS, E], F32R)
        ones = sb("ones", [P, GE])
        tot, inc = sb("tot", [P, E, GROUPS]), sb("inc", [P, E, GROUPS])
        cum, cnt = sb("cum", [P, E + 1]), sb("cnt", [P, E])
        more = sb("more", [P, E, GROUPS])
        nbk, end, off = sb("nbk", [P, E]), sb("end", [P, E]), sb("off", [P, E])
        pos = sb("pos", [P, GROUPS, E])
        slot, hi = sb("slot", [P, GROUPS]), sb("hi", [P, GROUPS])
        slot_i = sb("sloti", [P, GROUPS], I32)
        passed_b = sb("passedb", [P, blocks, E])
        of = sb("of", [P, blocks])
        zero = sb("zero", [P, blocks])
        got = [sb(f"got{q}", [P, blocks]) for q in range(LISTS)]
        loaded, cleared = stack.new(f"{pre}_rt_loaded"), stack.new(f"{pre}_rt_cleared")
        tri_ready, mask_ready = stack.new(f"{pre}_rt_tri"), stack.new(f"{pre}_rt_mask")
        counted = stack.new(f"{pre}_rt_counted")
        planned = Count(stack.new(f"{pre}_rt_planned"))
        slots_ready = stack.new(f"{pre}_rt_slots")
        filled = [stack.new(f"{pre}_rt_filled{q}") for q in range(LISTS)]
        fetched = stack.new(f"{pre}_rt_fetched")
        split = SplitWeights(nc, stack, ctx, f"{pre}w", jobs)
        block = ctx.enter_context(nc.Block())
        per_list = GROUPS // LISTS

        @block.sync
        def _(sp):
            sp.dma_start(stage[:, :, :], io["rt_tri"]).then_inc(loaded, 16)
            sp.dma_start(pad[:, :], io["rt_pad"]).then_inc(loaded, 16)
            sp.dma_start(steps[:, :], io["rt_steps"]).then_inc(loaded, 16)
            sp.dma_start(order[:, :], io["rt_order"][:, 0:blocks]).then_inc(loaded, 16)
            sp.dma_start(ident[:, :], io["rt_ids"]).then_inc(loaded, 16)
            sp.dma_start(mask[:, :, :], mask_in).then_inc(loaded, 16)
            sp.wait_ge(planned.sem, 1)
            for q in range(LISTS):
                sp.dma_start(lists[q].rearrange("(p b) o -> p (b o)", p=P), zero[:, :]).then_inc(cleared, 16)
            split.load(sp)
            for q in range(LISTS):
                sp.wait_ge(filled[q], 16 * per_list)
                sp.dma_start(got[q][:, :], lists[q].rearrange("(p b) o -> p (b o)", p=P)).then_inc(fetched, 16)

        @block.scalar
        def _(act):
            split.round(act)

        @block.gpsimd
        def _(pool):
            pool.wait_ge(loaded, 96)
            pool.wait_ge(cleared, 16 * LISTS)
            pool.wait_ge(slots_ready, 1)
            for g in range(GROUPS):
                q, n = g % LISTS, g // LISTS
                if n:
                    pool.wait_ge(filled[q], 16 * n)
                nc.gpsimd.indirect_dma_start(lists[q], bass.IndirectOffsetOnAxis(slot_i[:, g:g + 1], 0),
                                             ident[:, g:g + 1], None, bounds_check=P * blocks - 1,
                                             oob_is_err=False).then_inc(filled[q], 16)

        @block.tensor
        def _(pe):
            pe.wait_ge(tri_ready, 1)
            pe.wait_ge(mask_ready, 1)
            flat = chosen[:, :, :].rearrange("p g e -> p (g e)")
            for h in range(banks):
                cols = slice(h * width, (h + 1) * width)
                nc.tensor.matmul(ps[:, h, 0:width], tri[:, 0, :], flat[:, cols], start=True, stop=True)
                last = nc.tensor.matmul(ps[:, 2 + h, 0:width], tri[:, 1, :], flat[:, cols], start=True, stop=True)
            last.then_inc(counted, 1)

        @block.vector
        def _(dve):
            V = nc.vector
            planned.of(V.memset(zero[:, :], 0.0))
            V.memset(ones[:, :], 1.0)
            planned.of(V.memset(cum[:, 0:1], 0.0))
            dve.wait_ge(loaded, 96)
            V.tensor_copy(tri[:, :, :], stage[:, :, :]).then_inc(tri_ready, 1)
            V.tensor_scalar(chosen[:, :, :], mask[:, :, :], pad[:, 0:1], None, ALU.mult).then_inc(mask_ready, 1)
            dve.wait_ge(counted, 1)
            banked = lambda b0: ps[:, b0:b0 + banks, 0:width].rearrange("p b n -> p (b n)").rearrange("p (g e) -> p g e", e=E)
            planned.of(V.tensor_copy(tot[:, :, :], banked(2).rearrange("p g e -> p e g")))
            dve.wait_ge(planned.sem, planned.value)
            rows = lambda x: x[:, :, :].rearrange("p e g -> p (e g)")
            planned.of(V.tensor_tensor_scan(rows(inc), ones[:, :], rows(tot), 0.0, op0=ALU.mult, op1=ALU.add))
            dve.wait_ge(planned.sem, planned.value)
            planned.of(V.tensor_tensor(tot[:, :, :], inc[:, :, :], tot[:, :, :], ALU.subtract))
            planned.of(V.tensor_copy(cum[:, 1:E + 1], inc[:, :, GROUPS - 1]))
            dve.wait_ge(planned.sem, planned.value)
            planned.of(V.tensor_tensor(cnt[:, :], cum[:, 1:E + 1], cum[:, 0:E], ALU.subtract))
            dve.wait_ge(planned.sem, planned.value)
            planned.of(V.tensor_tensor(more[:, :, :], cnt[:, :].unsqueeze(2).to_broadcast([P, E, GROUPS]),
                                       steps[:, :].unsqueeze(1).to_broadcast([P, E, GROUPS]), ALU.is_gt))
            dve.wait_ge(planned.sem, planned.value)
            planned.of(V.tensor_reduce(nbk[:, :], more[:, :, :], AXX, ALU.add))
            dve.wait_ge(planned.sem, planned.value)
            planned.of(V.tensor_tensor_scan(end[:, :], ones[:, 0:E], nbk[:, :], 0.0, op0=ALU.mult, op1=ALU.add))
            dve.wait_ge(planned.sem, planned.value)
            planned.of(V.tensor_tensor(off[:, :], end[:, :], nbk[:, :], ALU.subtract))
            dve.wait_ge(planned.sem, planned.value)
            planned.of(V.scalar_tensor_tensor(off[:, :], off[:, :], float(P), cum[:, 0:E], ALU.mult, ALU.subtract))
            dve.wait_ge(planned.sem, planned.value)
            planned.of(V.tensor_tensor(tot[:, :, :], tot[:, :, :], off[:, :].unsqueeze(2).to_broadcast([P, E, GROUPS]), ALU.add))
            dve.wait_ge(planned.sem, planned.value)
            planned.of(V.tensor_tensor(pos[:, :, :], banked(0), tot[:, :, :].rearrange("p e g -> p g e"), ALU.add))
            dve.wait_ge(planned.sem, planned.value)
            planned.of(V.tensor_tensor(pos[:, :, :], pos[:, :, :], chosen[:, :, :].bitcast(F32), ALU.mult))
            dve.wait_ge(planned.sem, planned.value)
            planned.of(V.tensor_reduce(slot[:, :], pos[:, :, :], AXX, ALU.add))
            dve.wait_ge(planned.sem, planned.value)
            planned.of(V.tensor_copy(slot_i[:, :], slot[:, :]))
            dve.wait_ge(planned.sem, planned.value)
            planned.of(V.tensor_scalar(slot_i[:, :], slot_i[:, :], 7, None, ALU.arith_shift_right))
            dve.wait_ge(planned.sem, planned.value)
            planned.of(V.tensor_copy(hi[:, :], slot_i[:, :]))
            planned.of(V.tensor_scalar(slot[:, :], slot[:, :], float(blocks), pad[:, 1:2], ALU.mult, ALU.add))
            dve.wait_ge(planned.sem, planned.value)
            planned.of(V.scalar_tensor_tensor(slot[:, :], hi[:, :], float(1 - P * blocks), slot[:, :], ALU.mult, ALU.add))
            dve.wait_ge(planned.sem, planned.value)
            V.tensor_copy(slot_i[:, :], slot[:, :]).then_inc(slots_ready, 1)
            planned.of(V.tensor_tensor(passed_b[:, :, :], order[:, :].unsqueeze(2).to_broadcast([P, blocks, E]),
                                       end[:, :].unsqueeze(1).to_broadcast([P, blocks, E]), ALU.is_ge))
            dve.wait_ge(planned.sem, planned.value)
            planned.of(V.tensor_reduce(of[:, :], passed_b[:, :, :], AXX, ALU.add))
            dve.wait_ge(planned.sem, planned.value)
            planned.of(V.tensor_scalar(of[:, :], of[:, :], float(E - 1), None, ALU.min))
            dve.wait_ge(planned.sem, planned.value)
            V.tensor_copy(table[:, :], of[0:1, :])
            split.subtract(dve)
            dve.wait_ge(fetched, 16 * LISTS)
            for q in range(1, LISTS):
                planned.of(V.tensor_tensor(got[0][:, :], got[0][:, :], got[q][:, :], ALU.add))
                dve.wait_ge(planned.sem, planned.value)
            planned.of(V.tensor_scalar(of[:, :], got[0][:, :], 0.0, NOWHERE, ALU.is_equal, ALU.mult))
            dve.wait_ge(planned.sem, planned.value)
            planned.of(V.scalar_tensor_tensor(of[:, :], got[0][:, :], -1.0, of[:, :], ALU.add, ALU.add))
            dve.wait_ge(planned.sem, planned.value)
            V.tensor_copy(row_ids[:, :], of[:, :])


def last_experts(nc, stack, io):
    pre, E, blocks, W_ = "d", E_D, BLK_D, WAYS_S
    HE = HID // E
    HC = HE // P
    HH = HE // 2
    with ExitStack() as ctx:
        sb = lambda n, shape, dt=F32: ctx.enter_context(nc.sbuf_tensor(f"{pre}_sb_{n}", shape, dt))
        sig = lambda n, per=1, step=1: Signal(nc, stack, f"{pre}_{n}", per, W_, step)
        row_ids, table = sb("rowids", [P, blocks], I32), sb("table", [1, blocks], I32)
        W1 = sb("W1", [P, 2, 2, E, HE], F32R)
        W2 = sb("W2", [P, 2, E, HC, D], F32R)
        BR = sb("BR", [64, E, HE + D], F32R)
        stage = sb("stage", [1, E, HE + D])
        routing(nc, stack, io, pre, E, blocks, io["mask2"], io["lists2"], row_ids, table, [
            (io["d_w1"].rearrange("p a n -> p (a n)"), W1[:, 0].rearrange("p a e n -> p (a e n)"),
             W1[:, 1].rearrange("p a e n -> p (a e n)")),
            (io["d_w2"].rearrange("p a n -> p (a n)"), W2[:, 0].rearrange("p e c n -> p (e c n)"),
             W2[:, 1].rearrange("p e c n -> p (e c n)"))])
        ident, pick = sb("ident", [P, P]), sb("pick", [64, P], F32R)
        X = [sb(f"X{j}", [P, 2 * D]) for j in range(W_)]
        own = [sb(f"own{j}", [P, 1], I32) for j in range(W_)]
        pk = [sb(f"pk{j}", [P, 3, P], F32R) for j in range(2)]
        h = [sb(f"h{j}", [P, HE]) for j in range(2)]
        hh, hl = ([sb(f"{n}{j}", [P, HE], F32R) for j in range(2)] for n in ("hh", "hl"))
        y = [sb(f"y{j}", [P, D]) for j in range(2)]
        ps = ctx.enter_context(nc.psum_tensor(f"{pre}_ps", [P, 8, 512], F32))
        consts, identity, setup = (stack.new(f"{pre}_{n}") for n in ("consts", "identity", "setup"))
        split = stack.new(f"{pre}_split")
        owned = sig("owned")
        gathered = [Signal(nc, stack, f"{pre}_gathered{j}", 1, 1, 16) for j in range(W_)]
        scattered = sig("scattered", 1, 16)
        x_t, x_h, x_l, up, gelu, h_t, h_h, h_l = (
            sig(n, per) for n, per in (("xt", 1), ("xh", 2), ("xl", 2), ("up", 1), ("gelu", 2), ("ht", 1), ("hh", 1), ("hl", 1)))
        down, summed = sig("down"), sig("summed")
        block = ctx.enter_context(nc.Block())

        def passes(eng, step, first, last):
            for n in range(first, W_):
                step(0, n, lambda m: 0 <= m)
            with eng.Fori(1, blocks // W_ - 1) as it:
                for u in range(W_):
                    step(it, u, lambda m: True)
            for n in range(W_, 2 * W_ + last):
                step(blocks // W_ - 2, n, lambda m: m < 2 * W_)

        @block.sync
        def _(sp):
            sp.dma_start(stage[:, :, :], io["d_bias"]).then_inc(consts, 16)

        @block.gpsimd
        def _(pool):
            fill_identity(nc, pool, ident, identity)

            def step(it, u, there):
                m = u + 2
                if there(m):
                    j = m % W_
                    if not (isinstance(it, int) and it * W_ + m < W_):
                        pool.wait_ge(summed.sem, summed.now(it, m - W_))
                        pool.sem_inc(stack.passed, 1)
                        pool.wait_ge(scattered.sem, scattered.now(it, m - W_))
                        pool.sem_inc(stack.passed, 1)
                    nc.gpsimd.tensor_copy(own[j][:, :], row_ids[:, bass.ds(it * W_ + m, 1)]).then_inc(owned.sem, 1)
                    pool.wait_ge(owned.sem, owned.now(it, m))
                    pool.sem_inc(stack.passed, 1)
                    nc.gpsimd.indirect_dma_start(X[j][:, :], None, io["rows2"],
                                                 bass.IndirectOffsetOnAxis(own[j][:, :], 0), bounds_check=ROWS - 1,
                                                 oob_is_err=False).then_inc(gathered[j].sem, 16)
                m = u - 3
                if there(m):
                    pool.wait_ge(summed.sem, summed.now(it, m))
                    pool.sem_inc(stack.passed, 1)
                    if not (isinstance(it, int) and it * W_ + m < 1):
                        pool.wait_ge(scattered.sem, scattered.now(it, m - 1))
                        pool.sem_inc(stack.passed, 1)
                    nc.gpsimd.indirect_dma_start(io["out"], bass.IndirectOffsetOnAxis(own[m % W_][:, :], 0),
                                                 y[m % 2][:, :], None, bounds_check=ROWS - 1,
                                                 oob_is_err=False).then_inc(scattered.sem, 16)

            pool.wait_ge(setup, W_)
            passes(pool, step, -2, 3)
            pool.wait_ge(scattered.sem, 16 * blocks)

        @block.scalar
        def _(act):
            act.wait_ge(consts, 16)
            act.wait_ge(setup, W_ + 1)
            nc.scalar.copy(BR[0:1, :, :], stage[:, :, :]).then_inc(split, 1)

            def step(it, u, there):
                if there(u):
                    act.wait_ge(up.sem, up.now(it, u))
                    if not (isinstance(it, int) and it * W_ + u < 2):
                        act.wait_ge(h_t.sem, h_t.now(it, u - 2))
                    for c in range(2):
                        nc.scalar.activation(h[u % 2][:, c * HH:(c + 1) * HH], ps[:, 1 + c, 0:HH],
                                             ACT.Gelu).then_inc(gelu.sem, 1)
                m = u + 1
                if there(m):
                    act.wait_ge(x_t.sem, x_t.now(it, m))
                    if not (isinstance(it, int) and it * W_ + m < 2):
                        act.wait_ge(up.sem, up.now(it, m - 2))
                    nc.scalar.copy(pk[m % 2][:, 0, :], ps[:, 0, 0:P]).then_inc(x_h.sem, 1)
                    nc.scalar.copy(pk[m % 2][0:D2, 2, :], ps[0:D2, 6, 0:P]).then_inc(x_h.sem, 1)
                m = u - 1
                if there(m):
                    act.wait_ge(h_t.sem, h_t.now(it, m))
                    if not (isinstance(it, int) and it * W_ + m < 2):
                        act.wait_ge(down.sem, down.now(it, m - 2))
                    nc.scalar.copy(hh[m % 2][:, :].rearrange("p (b n) -> p b n", b=2), ps[:, 3:5, 0:HH]).then_inc(h_h.sem, 1)

            passes(act, step, -1, 1)

        @block.vector
        def _(dve):
            for j in range(W_):
                nc.vector.memset(X[j][:, :], 0.0).then_inc(setup, 1)
            nc.vector.memset(pick[:, :].bitcast(F32), 0.0)
            nc.vector.memset(BR[:, :, :].bitcast(F32), 0.0).then_inc(setup, 1)
            dve.wait_ge(setup, W_ + 1)
            for r in (0, 32):
                nc.vector.memset(pick[r:r + 1, :].bitcast(F32), 1.0).then_inc(setup, 1)
            dve.wait_ge(split, 1)
            nc.vector.tensor_tensor(BR[32:33, :, :], stage[:, :, :], BR[0:1, :, :].bitcast(F32), ALU.subtract
                                    ).then_inc(split, 1)

            def step(it, u, there):
                m = u + 1
                if there(m):
                    dve.wait_ge(x_h.sem, x_h.now(it, m, 1))
                    nc.vector.tensor_tensor(pk[m % 2][:, 1, :], ps[:, 0, 0:P], pk[m % 2][:, 0, :].bitcast(F32),
                                            ALU.subtract).then_inc(x_l.sem, 1)
                    dve.wait_ge(x_h.sem, x_h.now(it, m, 2))
                    nc.vector.tensor_tensor(pk[m % 2][D2:P, 2, :], ps[0:D2, 6, 0:P], pk[m % 2][0:D2, 2, :].bitcast(F32),
                                            ALU.subtract).then_inc(x_l.sem, 1)
                m = u - 1
                if there(m):
                    dve.wait_ge(h_h.sem, h_h.now(it, m))
                    nc.vector.tensor_tensor(hl[m % 2][:, :].rearrange("p (b n) -> p b n", b=2), ps[:, 3:5, 0:HH],
                                            hh[m % 2][:, :].rearrange("p (b n) -> p b n", b=2).bitcast(F32),
                                            ALU.subtract).then_inc(h_l.sem, 1)
                m = u - 2
                if there(m):
                    dve.wait_ge(down.sem, down.now(it, m))
                    dve.wait_ge(gathered[m % W_].sem, gathered[m % W_].now(it, m // W_))
                    if not (isinstance(it, int) and it * W_ + m < 2):
                        dve.wait_ge(scattered.sem, scattered.now(it, m - 2))
                    nc.vector.tensor_tensor(y[m % 2][:, :], ps[:, 5, 0:D], X[m % W_][:, D:2 * D], ALU.add
                                            ).then_inc(summed.sem, 1)

            passes(dve, step, -1, 2)

        @block.tensor
        def _(pe):
            pe.wait_ge(identity, 2)
            pe.wait_ge(setup, W_ + 3)
            pe.wait_ge(split, 2)

            def expert(it, m):
                return pe.value_load(table[0:1, bass.ds(it * W_ + m, 1)], min_val=0, max_val=E - 1)

            def step(it, u, there):
                if there(u):
                    e = expert(it, u)
                    pe.wait_ge(x_h.sem, x_h.now(it, u))
                    pe.wait_ge(x_l.sem, x_l.now(it, u))
                    if not (isinstance(it, int) and it * W_ + u < 1):
                        pe.wait_ge(gelu.sem, gelu.now(it, u - 1))
                    for n, (a, hlw, part) in enumerate(((0, 0, 0), (0, 1, 0), (1, 0, 0), (2, 0, 1), (2, 1, 1))):
                        for c in range(2):
                            nc.tensor.matmul(ps[:, 1 + c, 0:HH], pk[u % 2][:, a, :],
                                             W1[:, hlw, part, bass.ds(e, 1), c * HH:(c + 1) * HH].rearrange("p a n -> p (a n)"),
                                             start=n == 0, stop=False, skip_group_check=True)
                    for c in range(2):
                        last = nc.tensor.matmul(ps[:, 1 + c, 0:HH], pick[:, :],
                                                BR[:, bass.ds(e, 1), c * HH:(c + 1) * HH].rearrange("p a n -> p (a n)"),
                                                start=False, stop=True, skip_group_check=True)
                    last.then_inc(up.sem, 1)
                m = u + 1
                if there(m):
                    pe.wait_ge(gathered[m % W_].sem, gathered[m % W_].now(it, m // W_))
                    if not (isinstance(it, int) and it * W_ + m < 1):
                        pe.wait_ge(x_l.sem, x_l.now(it, m - 1))
                    nc.tensor.transpose(ps[:, 0, 0:P], X[m % W_][:, 0:P], ident[:, :])
                    nc.tensor.transpose(ps[0:D2, 6, 0:P], X[m % W_][:, P:D], ident[:, :]).then_inc(x_t.sem, 1)
                m = u - 1
                if there(m):
                    pe.wait_ge(gelu.sem, gelu.now(it, m))
                    if not (isinstance(it, int) and it * W_ + m < 1):
                        pe.wait_ge(h_l.sem, h_l.now(it, m - 1))
                    for c in range(HC):
                        last = nc.tensor.transpose(ps[:, 3 + c // 3, (c % 3) * P:(c % 3 + 1) * P],
                                                   h[m % 2][:, c * P:(c + 1) * P], ident[:, :])
                    last.then_inc(h_t.sem, 1)
                m = u - 2
                if there(m):
                    e = expert(it, m)
                    pe.wait_ge(h_h.sem, h_h.now(it, m))
                    pe.wait_ge(h_l.sem, h_l.now(it, m))
                    if not (isinstance(it, int) and it * W_ + m < 1):
                        pe.wait_ge(summed.sem, summed.now(it, m - 1))
                    for c in range(HC):
                        for n, (a, hlw) in enumerate(((hh, 0), (hh, 1), (hl, 0))):
                            nc.tensor.matmul(ps[:, 5, 0:D], a[m % 2][:, c * P:(c + 1) * P],
                                             W2[:, hlw, bass.ds(e, 1), c, :].rearrange("p a n -> p (a n)"),
                                             start=c == 0 and n == 0, stop=False, skip_group_check=True)
                    nc.tensor.matmul(ps[:, 5, 0:D], pick[:, :], BR[:, bass.ds(e, 1), HE:HE + D].rearrange("p a n -> p (a n)"),
                                     start=False, stop=True, skip_group_check=True).then_inc(down.sem, 1)

            passes(pe, step, -1, 2)


def build(nc, io):
    phases = (
        lambda stack: phase_a(nc, stack, io),
        lambda stack: moe_phase(nc, stack, io, "b", True, io["tp"], io["fw"], io["base"], io["h2"]),
        lambda stack: phase_c(nc, stack, io),
        lambda stack: last_experts(nc, stack, io),
    )
    for n, phase in enumerate(phases):
        stack = Semaphores(nc, n)
        phase(stack)
        stack.end()



SPECTRUM = list(range(KC)) + [D - j for j in range(1, KC - 1)]


def _parts(w):
    w = np.asarray(w)
    return np.stack([w[:P], np.concatenate([w[P:], w[P:]])], axis=1)


def _outs(w):
    return np.concatenate([w, w[:, P:]], axis=1)


def _twice(v):
    return np.concatenate([v[P:], v[P:]])


def _shape_constants():
    d, k = np.arange(D)[:, None], np.arange(KC)[None]
    ang = 2 * np.pi * ((d * k) % D) / D
    fft = np.zeros((D, 2 * KP))
    fft[:, :KC], fft[:, KP:KP + KC] = np.cos(ang), np.sin(ang)
    fft[:, KP], fft[:, KP + KC - 1] = 0, 0
    t = np.arange(T)
    ang = 2 * np.pi * ((t[:, None] * t[None]) % T) / T
    dft_t = np.zeros((2, TP, 2, 2, TP))
    for b in range(2):
        dft_t[b, :T, 0, b, :T] = np.cos(ang)
        dft_t[b, :T, 1, b, :T] = np.sin(ang)
    keys, queries = np.arange(TP)[None], np.arange(TP)[:, None]
    seen = np.where((keys <= queries) & (keys < T), 0.0, MASKED)
    return fft.astype(np.float32), dft_t.reshape(P, 2 * P).astype(np.float32), np.tile(seen, (2, 2)).astype(np.float32)


def _layout_a(i):
    fft, dft_t, mask = _shape_constants()
    f = np.float32
    x = np.zeros((D, B, CONV_T + 2 * HALO), f)
    x[:, :, HALO:HALO + S] = i["x"].transpose(2, 0, 1)
    x = x.reshape(D, NT, NB, -1)
    h = NB // 2
    tail = np.concatenate([x[P:, :, :h], x[P:, :, h:]], axis=0)
    xt = np.ascontiguousarray(np.concatenate([x[:P], tail], axis=2).transpose(1, 0, 2, 3))
    wa, ba = i["L0_attn_w_attn"][SPECTRUM], i["L0_attn_b_attn"]
    wq, wk, wv = wa[:, :D], wa[:, D:2 * D], wa[:, 2 * D:]
    w = np.concatenate([_outs(np.ascontiguousarray(i["L0_tok_w_pw"][:, :, 0].T)), fft, _outs(wq), _outs(wk), wv,
                        i["L0_attn_w_proj"][:, SPECTRUM], i["L0_ffn_gate_w"].T[SPECTRUM]], axis=1)
    cols = np.zeros((P, len(A_COL)), f)
    dw = i["L0_tok_w_dw"][:, 0, :]
    put = lambda n, v: cols.__setitem__((slice(None), A_COL[n]), v)
    for j in range(TAPS):
        put(f"tap{j}a", dw[:P, j])
        put(f"tap{j}b", _twice(dw[:, j]))
    for n, v in (("bdw", i["L0_tok_b_dw"]), ("bpw", i["L0_tok_b_pw"]), ("bq", ba[:D])):
        put(n + "a", v[:P])
        put(n + "b", _twice(v))
    par = (np.arange(P) // HD) % 2
    bk = ba[D:2 * D]
    for n, p in (("e", 0), ("o", 1)):
        own = par == p
        cols[own, A_COL[f"bk{n}a"]] = bk[:P][own]
        cols[own, A_COL[f"bk{n}b"]] = _twice(bk)[own]
    cols[par == 0, A_COL["even"]] = 1
    cols[par == 1, A_COL["odd"]] = 1
    rows = np.zeros((P, len(A_ROW), D), f)
    sp = lambda n: i[n][SPECTRUM]
    for n, v in (("gamma", sp("L0_tok_gamma")), ("beta", sp("L0_tok_beta")), ("bv", ba[2 * D:]),
                 ("bproj", sp("L0_attn_b_proj")), ("scale", sp("L0_ffn_scale")), ("gateb", i["L0_ffn_gate_b"])):
        rows[:, A_ROW[n], :len(v)] = v
    return {"x": xt, "a_w": _parts(w), "dft_t": dft_t, "a_cols": cols, "a_rows": rows, "a_mask": mask}


def _sel(experts):
    sel = np.zeros((64, HID), np.float32)
    for e in range(experts):
        n = HID // experts
        sel[e, e * n:(e + 1) * n] = sel[32 + e, e * n:(e + 1) * n] = 1
    return sel


def _bias_rows(b2, experts):
    out = np.zeros((64, D), np.float32)
    out[:experts] = out[32:32 + experts] = b2[:, SPECTRUM]
    return out


def _layout_b(i):
    w1, b1, w2 = i["L0_ffn_w1"][:, SPECTRUM], i["L0_ffn_b1"], i["L0_ffn_w2"][:, :, SPECTRUM]
    e, i2 = w1.shape[0], w1.shape[2] // 2
    parts = [w1[:, :, h * i2:(h + 1) * i2].transpose(1, 0, 2).reshape(D, CHUNKS, 1, P) for h in range(2)]
    w = np.concatenate(parts, axis=2).reshape(D, 2 * HID)
    b = np.stack([b1[:, h * i2:(h + 1) * i2].reshape(CHUNKS, P).T for h in range(2)], axis=1)
    return {"b_w1": _parts(w), "b_w2": w2.reshape(CHUNKS, P, D).transpose(1, 0, 2), "b_b1": b,
            "b_b2": _bias_rows(i["L0_ffn_b2"], e), "b_sel": _sel(e)}


def _layout_d(i):
    w1, b1, w2 = i["L1_ffn_W1"][:, SPECTRUM], i["L1_ffn_b1"], i["L1_ffn_W2"][:, :, SPECTRUM]
    e = w1.shape[0]
    bias = np.concatenate([b1, i["L1_ffn_b2"][:, SPECTRUM]], axis=1)
    return {"d_w1": _parts(w1.transpose(1, 0, 2).reshape(D, HID)),
            "d_w2": w2.reshape(CHUNKS, P, D).transpose(1, 0, 2), "d_bias": bias[None]}


def _layout_routing(i):
    p = np.arange(P)
    token = (p % TP < T).astype(np.float32)
    tri = np.stack([(p[:, None] < p[None]), np.ones((P, P))], axis=1).astype(np.float32)
    per_row = lambda v: np.tile(np.asarray(v, np.float32), (P, 1))
    return {"rt_tri": tri, "rt_pad": np.stack([token, (1 - token) * np.float32(NOWHERE)], axis=1),
            "rt_steps": per_row(np.arange(GROUPS) * P), "rt_order": per_row(np.arange(512)),
            "rt_ids": (1 + np.arange(GROUPS)[None] * P + p[:, None]).astype(np.float32)}


def _layout_c(i):
    f = np.float32
    t = lambda n: i[n].T
    gate = np.zeros((D, 16), f)
    gate[:, :4] = i["L1_ffn_Wg"][SPECTRUM]
    w = np.concatenate([_outs(t("L1_attn_Wk_a")[SPECTRUM]), _outs(t("L1_attn_Wv_a")[SPECTRUM]), _outs(t("L1_attn_Wr_a")[SPECTRUM]),
                        t("L1_attn_Wo_a")[:, SPECTRUM], t("L1_attn_Wr_f")[SPECTRUM][:, SPECTRUM],
                        t("L1_attn_Wk_f")[SPECTRUM], gate], axis=1)
    wv = t("L1_attn_Wv_f")[:, SPECTRUM].reshape(KFC, P, D).transpose(1, 0, 2)
    rows = np.zeros((P, len(C_ROW), D), f)
    for n, v in (("ln1w", i["L1_attn_ln1_w"][SPECTRUM]), ("ln1b", i["L1_attn_ln1_b"][SPECTRUM]),
                 ("ln2w", i["L1_attn_ln2_w"][SPECTRUM]), ("ln2b", i["L1_attn_ln2_b"][SPECTRUM]), ("gateb", i["L1_ffn_bg"])):
        rows[:, C_ROW[n], :len(v)] = v

    def table(v, pad):
        out = np.full((P, KEYS // TP, TP), pad, f)
        out[:, :NB, :T] = v[:P, None, None]
        out[:, NB:, :T] = _twice(v)[:, None, None]
        return out.reshape(P, KEYS)

    return {"c_w": _parts(w), "c_wv": wv, "c_rows": rows, "c_decay": table(i["L1_attn_decay"], NEG),
            "c_bonus": table(i["L1_attn_first"], 0.0)}


_SCRATCH = {"tp": (NT, P, 3, N), "fw": (NT, 64, N), "base": (NT, P, NG, D), "h2": (NT, P, NG, D),
            "rows2": (ROWS, 2 * D), "mask2": (P, GROUPS, E_D)}


def kernel(**inputs):
    import concourse.bacc as _bacc
    from concourse.bass_utils import run_bass_kernel_spmd as _run

    i = {n: np.asarray(a) for n, a in inputs.items()}
    arrays = {}
    for layout in (_layout_a, _layout_b, _layout_c, _layout_d, _layout_routing):
        arrays.update({n: np.ascontiguousarray(a) for n, a in layout(i).items()})
    nc = _bacc.Bacc("TRN2", target_bir_lowering=False, num_devices=1)
    io = {n: nc.dram_tensor(n, a.shape, F32, kind="ExternalInput").ap() for n, a in arrays.items()}
    io.update({n: nc.dram_tensor(n, shape, F32, kind="Internal").ap() for n, shape in _SCRATCH.items()})
    io["lists2"] = [nc.dram_tensor(f"lists2_{q}", (P * BLK_D, 1), F32, kind="Internal").ap() for q in range(LISTS)]
    io["out"] = nc.dram_tensor("out", (ROWS, D), F32, kind="ExternalOutput").ap()
    build(nc, io)
    r = _run(nc, [arrays], core_ids=[0]).results[0]["out"]
    y = r.reshape(B, TP, D)[:, :T]
    out = np.empty((B, T, D), np.float32)
    out[:, :, SPECTRUM] = y
    return out
```

```python
from contextlib import ExitStack

import numpy as np

import concourse.bass as bass
from concourse import mybir

F32 = mybir.dt.float32
F32R = mybir.dt.float32r
I32 = mybir.dt.int32
ALU = mybir.AluOpType
ACT = mybir.ActivationFunctionType
AXX = mybir.AxisListType.X

P = 128
B, S, D = 128, 125, 192
T = S // 2
TP = 64
TAPS = 7
HALO = TAPS // 2
NB = 8
NT = B // NB
NG = NB // 2
N = NB * TP
D2 = D - P
HEADS, HD = 12, 16
PAIRS = HEADS // 2
CONV_T = 2 * T
KC = D // 2 + 1
KP = KC + 1
EPS = 1e-5
NEG = -1.0e38
MASKED = -1.0e30
FREE = 3.0e38

A_COLS = {"pw": 256, "fft": 2 * KP, "q": 256, "k": 256, "v": 192, "proj": 192, "gate": 16}
C_COLS = {"wk": 256, "wv": 256, "wr": 256, "wo": 192, "rf": 192, "kf": 768, "gate": 16}


def offsets(cols):
    at, out = 0, {}
    for name, n in cols.items():
        out[name] = (at, n)
        at += n
    return out, at


A_AT, A_TOT = offsets(A_COLS)
C_AT, C_TOT = offsets(C_COLS)

A_COL = {n: k for k, n in enumerate(
    [f"tap{j}a" for j in range(TAPS)] + [f"tap{j}b" for j in range(TAPS)]
    + ["bdwa", "bdwb", "bpwa", "bpwb", "bqa", "bqb", "bkea", "bkoa", "bkeb", "bkob", "even", "odd"])}
A_ROW = {n: k for k, n in enumerate(["gamma", "beta", "bv", "bproj", "scale", "gateb"])}
C_ROW = {n: k for k, n in enumerate(["ln1w", "ln1b", "ln2w", "ln2b", "gateb"])}


class Semaphores:

    def __init__(self, nc, phase):
        self.nc, self.all = nc, []
        self.passed = self.new(f"passed{phase}")

    def new(self, name):
        self.all.append(self.nc.alloc_semaphore(name=name))
        return self.all[-1]

    def end(self):
        self.nc.all_engine_barrier()
        self.nc.clear_and_free_semaphores(self.all)
        self.nc.all_engine_barrier()


class Signal:

    def __init__(self, nc, stack, name, per=1, ways=2, step=1, credit=False):
        self.sem = stack.new(name)
        self.per, self.ways, self.step = per, ways, step
        self.primed = per * ways * step if credit else 0

    def credit(self, eng):
        eng.sem_inc(self.sem, self.primed)

    def now(self, it, u, n=None):
        n = self.per if n is None else n
        return it * (self.per * self.ways * self.step) + (u * self.per + n) * self.step + self.primed

    def last(self, it, u, n=None):
        n = self.per if n is None else n
        return it * (self.per * self.ways * self.step) + (u * self.per + n) * self.step

    def back(self, it, k):
        return self.now(it, k) if k >= 0 else self.last(it, self.ways + k)


class Count:

    def __init__(self, sem):
        self.sem, self.value = sem, 0

    def of(self, instruction):
        self.value += 1
        return instruction.then_inc(self.sem, 1)


def product5(nc, out, act, act_cols, w, w_cols, act_moves, start, stop):
    passes = ((0, 0, 0), (0, 1, 0), (1, 0, 0), (2, 0, 1), (2, 1, 1))
    last = None
    for k, (a, hl, part) in enumerate(passes):
        x = act[:, a, act_cols]
        y = w[:, hl, part, w_cols]
        lhs, rhs = (y, x) if act_moves else (x, y)
        last = nc.tensor.matmul(out, lhs, rhs, start=start and k == 0, stop=stop and k == 4,
                                skip_group_check=True)
    return last


class SplitWeights:
    CH, SLOTS = 512, 4

    def __init__(self, nc, stack, ctx, prefix, jobs):
        self.nc, self.pieces = nc, []
        for src, hi, lo in jobs:
            p, n = src.shape
            for c in range(0, n, self.CH):
                m = min(self.CH, n - c)
                self.pieces.append((src[:, c:c + m], hi[:, c:c + m], lo[:, c:c + m], p, m))
        self.stage = ctx.enter_context(nc.sbuf_tensor(f"{prefix}_stage", [P, self.SLOTS, self.CH], F32))
        self.loaded = [stack.new(f"{prefix}_loaded{j}") for j in range(self.SLOTS)]
        self.high = stack.new(f"{prefix}_high")
        self.low = stack.new(f"{prefix}_low")

    def load(self, sp):
        for k, (src, hi, lo, p, m) in enumerate(self.pieces):
            j = k % self.SLOTS
            if k >= self.SLOTS:
                sp.wait_ge(self.low, k - self.SLOTS + 1)
            sp.dma_start(self.stage[0:p, j, 0:m], src).then_inc(self.loaded[j], 16)

    def round(self, act):
        for k, (src, hi, lo, p, m) in enumerate(self.pieces):
            j = k % self.SLOTS
            act.wait_ge(self.loaded[j], 16 * (k // self.SLOTS + 1))
            self.nc.scalar.copy(hi, self.stage[0:p, j, 0:m]).then_inc(self.high, 1)

    def subtract(self, eng):
        for k, (src, hi, lo, p, m) in enumerate(self.pieces):
            eng.wait_ge(self.high, k + 1)
            eng.tensor_tensor(lo, self.stage[0:p, k % self.SLOTS, 0:m], hi.bitcast(F32),
                              ALU.subtract).then_inc(self.low, 1)


def split_weights(nc, stack, prefix, jobs):
    with ExitStack() as ctx:
        split = SplitWeights(nc, stack, ctx, prefix, jobs)
        block = ctx.enter_context(nc.Block())

        @block.sync
        def _(sp):
            split.load(sp)

        @block.scalar
        def _(act):
            split.round(act)

        @block.vector
        def _(dve):
            split.subtract(dve)


def fill_identity(nc, pool, ident, sem):
    pool.memset(ident[:, :], 0.0).then_inc(sem, 1)
    pool.wait_ge(sem, 1)
    pool.affine_select(out=ident[:, :], in_=ident[:, :], compare_op=ALU.not_equal, fill=1.0,
                       base=0, pattern=[[-1, P]], channel_multiplier=1).then_inc(sem, 1)


def norm_stats(nc, stack, dve, src, st, mv, stats_ready, moments_ready, it, u):
    for g in range(NG):
        nc.vector.bn_stats(st[:, g, :], src[:, g, :]).then_inc(stats_ready.sem, 1)
    dve.wait_ge(stats_ready.sem, stats_ready.now(it, u))
    dve.sem_inc(stack.passed, 1)
    for g in range(NG):
        nc.vector.bn_aggr(mv[:, g, :], st[:, g, :]).then_inc(moments_ready.sem, 1)


def norm_apply(nc, out, src, mv, rs, sig):
    for g in range(NG):
        nc.vector.tensor_scalar(out[:, g, :], src[:, g, :], mv[:, g, 0:1], rs[:, g:g + 1],
                                ALU.subtract, ALU.mult).then_inc(sig.sem, 1)


def norm_center(nc, dve, stack, out, src, mv, scale, moments, sig, it, u):
    dve.wait_ge(moments.sem, moments.now(it, u))
    for g in range(NG):
        nc.vector.scalar_tensor_tensor(out[:, g, :], src[:, g, :], mv[:, g, 0:1], scale, ALU.subtract, ALU.mult
                                       ).then_inc(sig.sem, 1)


def norm_finish(nc, out, src, rs, shift, sig):
    for g in range(NG):
        nc.vector.scalar_tensor_tensor(out[:, g, :], src[:, g, :], rs[:, g:g + 1], shift, ALU.mult, ALU.add
                                       ).then_inc(sig.sem, 1)


def transpose_tile(nc, ps, b0, src, ident, sig):
    for g in range(NG):
        nc.tensor.transpose(ps[:, b0, g * P:(g + 1) * P], src[:, g, 0:P], ident[:, :])
    for g in range(NG):
        last = nc.tensor.transpose(ps[0:D2, b0 + 1, g * P:(g + 1) * P], src[:, g, P:D], ident[:, :])
    last.then_inc(sig.sem, 1)


def pack_high(nc, ps, b0, pk, sig):
    nc.scalar.copy(pk[:, 0, :], ps[:, b0, :]).then_inc(sig.sem, 1)
    nc.scalar.copy(pk[0:D2, 2, :], ps[0:D2, b0 + 1, :]).then_inc(sig.sem, 1)


def pack_low(nc, dve, ps, b0, pk, high, sig, it, u):
    dve.wait_ge(high.sem, high.now(it, u, 1))
    nc.vector.tensor_tensor(pk[:, 1, :], ps[:, b0, :], pk[:, 0, :].bitcast(F32),
                            ALU.subtract).then_inc(sig.sem, 1)
    dve.wait_ge(high.sem, high.now(it, u, 2))
    nc.vector.tensor_tensor(pk[D2:P, 2, :], ps[0:D2, b0 + 1, :], pk[0:D2, 2, :].bitcast(F32),
                            ALU.subtract).then_inc(sig.sem, 1)


def row_highs(nc, src, parts, sig):
    for g, rows in parts:
        of = src[:, g:g + rows.shape[1], :]
        nc.scalar.copy(rows[:, :, 0:P], of[:, :, 0:P]).then_inc(sig.sem, 1)
        nc.scalar.copy(rows[:, :, 2 * P:2 * P + D2], of[:, :, P:D]).then_inc(sig.sem, 1)


def row_lows(nc, src, parts, sig):
    for g, rows in parts:
        of = src[:, g:g + rows.shape[1], :]
        for a, b, n in ((P, 0, P), (2 * P + D2, P, D2)):
            nc.gpsimd.tensor_tensor(rows[:, :, a:a + n], of[:, :, b:b + n], rows[:, :, a - n:a].bitcast(F32), ALU.subtract
                                    ).then_inc(sig.sem, 1)


def bcast_groups(row, n=D):
    return row[:, 0:n].unsqueeze(1).to_broadcast([P, NG, n])


class Router:

    def __init__(self, nc, stack, ctx, prefix, experts, k):
        self.nc, self.e, self.k, self.stack = nc, experts, k, stack
        sb = lambda n, shape: ctx.enter_context(nc.sbuf_tensor(f"{prefix}_{n}", shape, F32))
        self.gb = [sb(f"gb{u}", [P, NG, 24]) for u in range(2)]
        self.rep = [sb(f"rep{u}", [P, NG, 24]) for u in range(2)]
        self.m8 = [sb(f"m8{u}", [P, NG, 8]) for u in range(2)]
        self.sh = [sb(f"sh{u}", [P, NG, 16]) for u in range(2)]
        self.ex = [sb(f"ex{u}", [P, NG, 16]) for u in range(2)]
        self.mask = [sb(f"mask{u}", [P, NG, 16]) for u in range(2)]
        self.wm = [sb(f"wm{u}", [P, NG, 16]) for u in range(2)]
        self.den = [sb(f"den{u}", [P, NG]) for u in range(2)]
        self.fw = [sb(f"fw{u}", [P, NG, 16]) for u in range(2)]
        sig = lambda n, per=1, credit=False: Signal(nc, stack, f"{prefix}_{n}", per, credit=credit)
        self.biased, self.found, self.cut = sig("biased", credit=True), sig("found", NG), sig("cut")
        self.replaced, self.masked = sig("replaced", NG), sig("masked")
        self.shifted, self.exped = sig("shifted"), sig("exped")
        self.weighed, self.summed, self.inverse = sig("weighed"), sig("summed"), sig("inverse")
        self.gates = sig("gates")
        self.init = stack.new(f"{prefix}_init")

    def start(self, dve):
        nc = self.nc
        for u in range(2):
            nc.vector.memset(self.gb[u][:, :, 0:16], -FREE)
            nc.vector.memset(self.gb[u][:, :, 16:24], FREE)
            nc.vector.memset(self.wm[u][:, :, :], 0.0)
            nc.vector.memset(self.fw[u][:, :, :], 0.0).then_inc(self.init, 1)
        self.biased.credit(dve)
        dve.wait_ge(self.init, 2)

    def choose(self, dve, logits, bias_row, it, u):
        nc, e, k = self.nc, self.e, self.k
        gb, rep, m8 = self.gb[u], self.rep[u], self.m8[u]
        nc.vector.tensor_tensor(gb[:, :, 0:e], logits, bcast_groups(bias_row, e),
                                ALU.add).then_inc(self.biased.sem, 1)
        dve.wait_ge(self.biased.sem, self.biased.now(it, u))
        dve.sem_inc(self.stack.passed, 1)
        for g in range(NG):
            nc.vector.max(m8[:, g, :], gb[:, g, 0:16]).then_inc(self.found.sem, 1)
        dve.wait_ge(self.found.sem, self.found.now(it, u))
        nc.vector.memset(m8[:, :, k:8], FREE).then_inc(self.cut.sem, 1)
        if k > 1:
            nc.vector.tensor_tensor(self.sh[u][:, :, :], gb[:, :, 0:16],
                                    m8[:, :, 0:1].to_broadcast([P, NG, 16]),
                                    ALU.subtract).then_inc(self.shifted.sem, 1)
        dve.wait_ge(self.cut.sem, self.cut.now(it, u))
        dve.sem_inc(self.stack.passed, 1)
        for g in range(NG):
            nc.vector.match_replace(rep[:, g, :], m8[:, g, :], gb[:, g, :], -FREE / 2
                                    ).then_inc(self.replaced.sem, 1)
        dve.wait_ge(self.replaced.sem, self.replaced.now(it, u))
        if k == 1:
            nc.vector.tensor_tensor(self.fw[u][:, :, 0:e], rep[:, :, 0:e], gb[:, :, 0:e],
                                    ALU.not_equal).then_inc(self.gates.sem, 1)
            return
        nc.vector.tensor_tensor(self.mask[u][:, :, :], rep[:, :, 0:16], gb[:, :, 0:16],
                                ALU.not_equal).then_inc(self.masked.sem, 1)
        dve.wait_ge(self.masked.sem, self.masked.now(it, u))
        dve.wait_ge(self.exped.sem, self.exped.now(it, u))
        nc.vector.tensor_tensor(self.wm[u][:, :, :], self.mask[u][:, :, :], self.ex[u][:, :, :],
                                ALU.mult).then_inc(self.weighed.sem, 1)
        dve.wait_ge(self.weighed.sem, self.weighed.now(it, u))
        nc.vector.tensor_reduce(self.den[u][:, :], self.wm[u][:, :, :], AXX, ALU.add
                                ).then_inc(self.summed.sem, 1)
        dve.wait_ge(self.summed.sem, self.summed.now(it, u))
        nc.vector.reciprocal(self.den[u][:, :], self.den[u][:, :]).then_inc(self.inverse.sem, 1)
        dve.wait_ge(self.inverse.sem, self.inverse.now(it, u))
        nc.vector.tensor_tensor(self.fw[u][:, :, :], self.wm[u][:, :, :],
                                self.den[u][:, :].unsqueeze(2).to_broadcast([P, NG, 16]),
                                ALU.mult).then_inc(self.gates.sem, 1)

    def exponentials(self, act, it, u):
        act.wait_ge(self.shifted.sem, self.shifted.now(it, u))
        self.nc.scalar.activation(self.ex[u][:, :, :], self.sh[u][:, :, :], ACT.Exp
                                  ).then_inc(self.exped.sem, 1)


def phase_a(nc, stack, io):
    with ExitStack() as ctx:
        sb = lambda n, shape, dt=F32: ctx.enter_context(nc.sbuf_tensor(f"a_sb_{n}", shape, dt))
        two = lambda n, shape, dt=F32: [sb(f"{n}{u}", shape, dt) for u in range(2)]
        sig = lambda n, per=1, step=1, ways=2, credit=False: Signal(nc, stack, f"a_{n}", per, ways, step, credit)
        sig4 = lambda n, per=1: sig(n, per, ways=4)
        ps = ctx.enter_context(nc.psum_tensor("a_ps", [P, 8, 512], F32))

        W = sb("W", [P, 2, 2, A_TOT], F32R)
        CS = sb("CS", [P, 2, 2, P], F32R)
        cols = sb("cols", [P, len(A_COL)])
        rows = sb("rows", [P, len(A_ROW), D])
        mask = sb("mask", [P, P])
        ident = sb("ident", [P, P])
        split_weights(nc, stack, "aw", [
            (io["a_w"].rearrange("p a n -> p (a n)"),
             W[:, 0].rearrange("p a n -> p (a n)"), W[:, 1].rearrange("p a n -> p (a n)")),
            (io["dft_t"], CS[:, 0].rearrange("p a n -> p (a n)"), CS[:, 1].rearrange("p a n -> p (a n)"))])

        xin = two("xin", [P, NB + NB // 2, CONV_T + 2 * HALO])
        acc = two("acc", [P, (NB + NB // 2) * CONV_T])
        cv = two("cv", [P, 2 * (NB + NB // 2) * CONV_T], F32R)
        mx = two("mx", [P, 2, NB, TP])
        pk = two("pk", [P, 3, N], F32R)
        bs = two("bs", [P, NG, KP])
        xs = two("xs", [P, NG, 2 * D], F32R)
        yb, hb, nb = two("yb", [P, NG, D]), two("hb", [P, NG, D]), two("nb", [P, NG, D])
        q = two("q", [P, 2, N])
        kx = two("kx", [P, 2, 2, N])
        vblk = two("vblk", [P, NG, 2, PAIRS, 2, HD + 1])
        pt = two("pt", [P, 2 * PAIRS, P])
        sm_mx = two("smmx", [P, 2 * HEADS])
        rden = two("rden", [P, 2 * HEADS])
        st, mv = two("st", [P, NG, 6]), two("mv", [P, NG, 2])
        rs = two("rs", [P, NG])
        ra, rb, rc = two("ra", [P, NG]), two("rb", [P, NG]), two("rc", [P, NG])
        half = sb("half", [P, NG])
        router = Router(nc, stack, ctx, "ar", 16, 4)

        dma = lambda n, credit=False: [sig(f"{n}{u}", 1, 16, 1, credit) for u in range(2)]
        loaded, consts = dma("loaded"), stack.new("a_consts")
        setup = stack.new("a_setup")
        identity = stack.new("a_identity")
        conv0, conv, conv_h, conv_l = sig("conv0", 2), sig("conv", 2 * (TAPS - 1)), sig("convh", 2), sig("convl", 2)
        pw_done, pooled, act_r = sig("pwdone"), sig("pooled", 2), sig("relu", 2)
        hp_h, hp_l = sig("hph", 2), sig("hpl", 2)
        ftd, pq_h, pq_l = sig("ftd"), sig("pqh"), sig("pql")
        fts, bs_up, y_ready = sig("fts"), sig("bsup"), sig("y", 2)
        s1, m1, v1, r1, a1, h0 = sig("s1", 4), sig("m1", 4), sig("v1"), sig("r1"), sig("a1", 4), sig("h0", 4)
        s2, m2, v2, r2, n1 = sig("s2", 4), sig("m2", 4), sig("v2"), sig("r2"), sig("n1", 4)
        t1, p1h, p1l = sig("t1"), sig("p1h", 2), sig("p1l", 2)
        q_ps, q_up, k_ps, v_ps, v_up = sig("qps"), sig("qup", 2), sig("kps"), sig("vps"), sig("vup")
        ka_up, kv_up, vd_up, vo_up = sig("kaup", 2), sig("kvup", 2), sig("vdup", 2), sig("voup", 2)
        sc, sadd, smax, ssub, sexp = sig4("sc"), sig4("sadd", 4), sig4("smax"), sig4("ssub"), sig4("sexp")
        ptt, pta, ptv, pv, rd, at = sig4("ptt"), sig4("pta", 2), sig4("ptv"), sig4("pv"), sig4("rd"), sig4("at")
        t2, p2h, p2l = sig("t2"), sig("p2h", 2), sig("p2l", 2)
        hbias, pr, h1 = sig("hbias"), sig("pr"), sig("h1")
        s3, m3, pl3, n2, base, tt = sig("s3", 4), sig("m3", 4), sig("pl3", 6), sig("n2", 4), sig("base"), sig("tt", 4)
        t3, p3h, p3l = sig("t3"), sig("p3h", 2), sig("p3l", 2)
        gt, xh, xl = sig("gt"), sig("xh", 2), sig("xl", 2, credit=True)
        st_x, st_mask, st_fw, st_base = (dma(n, True) for n in ("stx", "stmask", "stfw", "stbase"))
        block = ctx.enter_context(nc.Block())
        col = lambda n, p0=0, p1=P: cols[p0:p1, A_COL[n]:A_COL[n] + 1]
        row = lambda n: rows[:, A_ROW[n], :]
        w_at = lambda n, a=0, m=None: slice(A_AT[n][0] + a, A_AT[n][0] + a + (m or A_AT[n][1]))
        NC = NB * CONV_T
        acc0 = [a[:, 0:NC].rearrange("p (b s) -> p b s", b=NB) for a in acc]
        acc1 = [a[:, NC:NC + NC // 2].rearrange("p (b s) -> p b s", b=NB // 2) for a in acc]
        sm = [a[:, 0:2 * PAIRS * P].rearrange("p (g j c) -> p g j c", g=2, j=PAIRS) for a in [
            sb(f"sm{u}", [P, 2 * PAIRS * P]) for u in range(2)]]
        pqn = NG * 2 * KP
        pq = [[c[:, hl * pqn:(hl + 1) * pqn].rearrange("p (g n) -> p g n", g=NG) for hl in range(2)] for c in cv]

        def dft_out(u, b0):
            return ps[:, 4 * u + b0:4 * u + b0 + 2, :].rearrange("p b (h n) -> p b h n", h=2)[:, :, :, 0:2 * KP]

        def two_banks(u, b0, n):
            return ps[:, 4 * u + b0:4 * u + b0 + 2, :].rearrange("p b (h n) -> p b h n", h=2)[:, :, :, 0:n]

        def split4(ap):
            return ap.rearrange("p (b h) n -> p b h n", b=2)

        @block.sync
        def _(sp):
            sp.dma_start(cols[:, :], io["a_cols"]).then_inc(consts, 16)
            sp.dma_start(rows[:, :, :], io["a_rows"]).then_inc(consts, 16)
            sp.dma_start(mask[:, :], io["a_mask"]).then_inc(consts, 16)
            for s in (*st_base, *st_x, *st_mask, *st_fw):
                s.credit(sp)
            for u in range(2):
                sp.dma_start(xin[u][:, :, :], io["x"][u]).then_inc(loaded[u].sem, 16)
            with sp.Fori(0, NT // 2) as it:
                for u in range(2):
                    sp.wait_ge(conv.sem, conv.now(it, u))
                    sp.sem_inc(stack.passed, 1)
                    sp.dma_start(xin[u][:, :, :], io["x"][it * 2 + u + 2]).then_inc(loaded[u].sem, 16)
                for u in range(2):
                    sp.wait_ge(base.sem, base.now(it, u))
                    sp.sem_inc(stack.passed, 1)
                    sp.dma_start(io["base"][it * 2 + u], hb[u][:, :, :]).then_inc(st_base[u].sem, 16)
                for u in range(2):
                    sp.wait_ge(xl.sem, xl.now(it, u))
                    sp.sem_inc(stack.passed, 1)
                    sp.dma_start(io["rows_b"].rearrange("(t g p) d -> t p g d", g=NG, p=P)[it * 2 + u],
                                 xs[u][:, :, :].bitcast(F32)).then_inc(st_x[u].sem, 16)
                for u in range(2):
                    of_tile = lambda x: x.rearrange("p (t g) e -> t p g e", g=NG)[it * 2 + u]
                    sp.wait_ge(router.gates.sem, router.gates.now(it, u))
                    sp.sem_inc(stack.passed, 1)
                    sp.dma_start(of_tile(io["mask_b"]), router.mask[u][:, :, :]).then_inc(st_mask[u].sem, 16)
                    sp.dma_start(of_tile(io["gate_b"]), router.fw[u][:, :, :]).then_inc(st_fw[u].sem, 16)
            for u in range(2):
                for s in (st_base, st_x, st_mask, st_fw):
                    sp.wait_ge(s[u].sem, s[u].now(NT // 2 - 1, 0))
                    sp.sem_inc(stack.passed, 1)

        @block.gpsimd
        def _(pool):
            fill_identity(nc, pool, ident, identity)
            nc.gpsimd.memset(half[:, :], -0.5).then_inc(setup, 1)
            xl.credit(pool)
            for u in range(2):
                nc.gpsimd.memset(vblk[u][:, :, :, :, :, :], 0.0).then_inc(setup, 1)
                nc.gpsimd.memset(mx[u][:, :, :, :], 0.0).then_inc(setup, 1)
            pool.wait_ge(setup, 5)
            for u in range(2):
                for par in range(2):
                    nc.gpsimd.memset(vblk[u][64 * par:64 * par + 64, :, :, :, par, HD:HD + 1], 1.0).then_inc(setup, 1)
            pool.wait_ge(setup, 9)
            with pool.Fori(0, NT // 2) as it:
                for (m, v, r) in ((m1, v1, r1), (m2, v2, r2)):
                    for u in range(2):
                        pool.wait_ge(m.sem, m.now(it, u))
                        pool.sem_inc(stack.passed, 1)
                        nc.gpsimd.tensor_scalar(ra[u][:, :], mv[u][:, :, 1], EPS, None, ALU.add).then_inc(v.sem, 1)
                        pool.wait_ge(v.sem, v.now(it, u))
                        nc.gpsimd.tensor_tensor(rs[u][:, :], ra[u][:, :], half[:, :], ALU.pow).then_inc(r.sem, 1)
                for u in range(2):
                    pool.wait_ge(v_up.sem, v_up.now(it, u))
                    pool.sem_inc(stack.passed, 1)
                    for b in range(2):
                        for par in range(2):
                            if b != par:
                                continue
                            nc.gpsimd.tensor_copy(
                                vblk[u][64 * par:64 * par + 64, :, b, :, par, 0:HD],
                                yb[u][64 * b:64 * b + 64, :, :].rearrange("p g (j a c) -> p g j a c", j=PAIRS, a=2)[:, :, :, par, :]
                            ).then_inc(vd_up.sem, 1)
                pool.wait_ge(vd_up.sem, vd_up.now(it, 1))
                for pg in range(2):
                    for u in range(2):
                        pool.wait_ge(smax.sem, smax.now(it, 2 * pg + u))
                        nc.gpsimd.tensor_tensor(
                            sm[u].rearrange("p g j (a c) -> p (g j a) c", a=2),
                            sm[u].rearrange("p g j (a c) -> p (g j a) c", a=2),
                            sm_mx[u][:, :].unsqueeze(2).to_broadcast([P, 2 * HEADS, TP]),
                            ALU.subtract).then_inc(ssub.sem, 1)
                for u in range(2):
                    pool.wait_ge(p1l.sem, p1l.now(it, u))
                    pool.wait_ge(h0.sem, h0.now(it, u))
                    nc.gpsimd.tensor_tensor(hb[u][:, :, :], hb[u][:, :, :], bcast_groups(row("bproj")), ALU.add).then_inc(hbias.sem, 1)
                for u in range(2):
                    pool.wait_ge(m3.sem, m3.now(it, u))
                    pool.sem_inc(stack.passed, 1)
                    nc.gpsimd.tensor_scalar(ra[u][:, :], mv[u][:, :, 1], EPS, None, ALU.add).then_inc(pl3.sem, 1)
                    pool.wait_ge(pl3.sem, pl3.now(it, u, 1))
                    nc.gpsimd.tensor_tensor(rs[u][:, :], ra[u][:, :], half[:, :], ALU.pow).then_inc(pl3.sem, 1)
                    pool.wait_ge(pl3.sem, pl3.now(it, u, 2))
                    nc.gpsimd.tensor_tensor(rb[u][:, :], rs[u][:, :], rs[u][:, :], ALU.mult).then_inc(pl3.sem, 1)
                    pool.wait_ge(pl3.sem, pl3.now(it, u, 3))
                    nc.gpsimd.tensor_tensor(rb[u][:, :], rb[u][:, :], mv[u][:, :, 1], ALU.mult).then_inc(pl3.sem, 1)
                    pool.wait_ge(pl3.sem, pl3.now(it, u, 4))
                    pool.sem_inc(stack.passed, 1)
                    nc.gpsimd.tensor_scalar(rb[u][:, :], rb[u][:, :], EPS, None, ALU.add).then_inc(pl3.sem, 1)
                    pool.wait_ge(pl3.sem, pl3.now(it, u, 5))
                    nc.gpsimd.tensor_tensor(rc[u][:, :], rb[u][:, :], half[:, :], ALU.pow).then_inc(pl3.sem, 1)
                for u in range(2):
                    pool.wait_ge(xh.sem, xh.now(it, u))
                    row_lows(nc, nb[u], [(0, xs[u][:, :, :])], xl)

        @block.vector
        def _(dve):
            dve.wait_ge(consts, 48)
            router.start(dve)
            dve.wait_ge(setup, 9)

            def tap(it, u, j):
                dve.wait_ge(conv0.sem, conv0.now(it, u))
                for c, (x, a) in enumerate(((xin[u][:, 0:NB, :], acc0[u]), (xin[u][:, NB:NB + NB // 2, :], acc1[u]))):
                    if j > 1:
                        dve.wait_ge(conv.sem, conv.now(it, u, 2 * (j - 2) + c + 1))
                    nc.vector.scalar_tensor_tensor(a, x[:, :, j:j + CONV_T], col(f"tap{j}{'ab'[c]}"), a,
                                                   ALU.mult, ALU.add).then_inc(conv.sem, 1)

            def conv_lows(it, u):
                for c, (c0, c1) in enumerate(((0, NC), (NC, NC + NC // 2))):
                    dve.wait_ge(conv_h.sem, conv_h.now(it, u, c + 1))
                    nc.vector.tensor_tensor(cv[u][:, NC * 3 // 2 + c0:NC * 3 // 2 + c1], acc[u][:, c0:c1],
                                            cv[u][:, c0:c1].bitcast(F32), ALU.subtract).then_inc(conv_l.sem, 1)

            for u in range(2):
                for j in range(1, TAPS):
                    tap(0, u, j)
            for u in range(2):
                conv_lows(0, u)
            with dve.Fori(0, NT // 2) as it:
                next_taps = iter([(j, u) for u in range(2) for j in range(1, TAPS)])

                def fill(n):
                    for _ in range(n):
                        j, u = next(next_taps)
                        tap(it + 1, u, j)

                for u in range(2):
                    dve.wait_ge(pw_done.sem, pw_done.now(it, u))
                    for c in range(2):
                        src = ps[:, 4 * u + 2 * c:4 * u + 2 * c + 2, 0:NC // 2].rearrange(
                            "p h (b s t) -> p h b s t", b=NB // 2, t=2)
                        nc.vector.tensor_reduce(
                            mx[u][:, c, :, 0:T].rearrange("p (h b) s -> p h b s", h=2), src, AXX, ALU.max
                        ).then_inc(pooled.sem, 1)
                for u in range(2):
                    dve.wait_ge(hp_h.sem, hp_h.now(it, u, 1))
                    nc.vector.tensor_tensor(pk[u][:, 1, :], mx[u][:, 0].rearrange("p b s -> p (b s)"),
                                            pk[u][:, 0, :].bitcast(F32), ALU.subtract).then_inc(hp_l.sem, 1)
                    dve.wait_ge(hp_h.sem, hp_h.now(it, u, 2))
                    nc.vector.tensor_tensor(pk[u][D2:P, 2, :], mx[u][0:D2, 1].rearrange("p b s -> p (b s)"),
                                            pk[u][0:D2, 2, :].bitcast(F32), ALU.subtract).then_inc(hp_l.sem, 1)
                fill(1)
                for u in range(2):
                    dve.wait_ge(pq_h.sem, pq_h.now(it, u))
                    nc.vector.tensor_tensor(split4(pq[u][1]), dft_out(u, 0), split4(pq[u][0].bitcast(F32)),
                                            ALU.subtract).then_inc(pq_l.sem, 1)
                fill(1)
                for u in range(2):
                    dve.wait_ge(bs_up.sem, bs_up.now(it, u))
                    a = two_banks(u, 2, KP)
                    nc.vector.tensor_tensor(split4(yb[u][:, :, 0:KC]), a[:, :, :, 0:KC], split4(bs[u][:, :, 0:KC]),
                                            ALU.subtract).then_inc(y_ready.sem, 1)
                    nc.vector.tensor_tensor(split4(yb[u][:, :, KC:D]), a[:, :, :, 1:KC - 1],
                                            split4(bs[u][:, :, 1:KC - 1]), ALU.add).then_inc(y_ready.sem, 1)
                for u in range(2):
                    dve.wait_ge(y_ready.sem, y_ready.now(it, u))
                    norm_stats(nc, stack, dve, yb[u], st[u], mv[u], s1, m1, it, u)
                for u in range(2):
                    dve.wait_ge(xl.sem, xl.last(it, u))
                    norm_center(nc, dve, stack, nb[u], yb[u], mv[u], row("gamma"), m1, a1, it, u)
                for u in range(2):
                    dve.wait_ge(a1.sem, a1.now(it, u))
                    dve.wait_ge(r1.sem, r1.now(it, u))
                    dve.wait_ge(st_base[u].sem, st_base[u].last(it, 0))
                    norm_finish(nc, hb[u], nb[u], rs[u], row("beta"), h0)
                for u in range(2):
                    dve.wait_ge(h0.sem, h0.now(it, u))
                    norm_stats(nc, stack, dve, hb[u], st[u], mv[u], s2, m2, it, u)
                fill(1)
                for u in range(2):
                    dve.wait_ge(r2.sem, r2.now(it, u))
                    norm_apply(nc, nb[u], hb[u], mv[u], rs[u], n1)
                fill(1)
                for u in range(2):
                    dve.wait_ge(t1.sem, t1.now(it, u))
                    pack_low(nc, dve, ps, 4 * u, pk[u], p1h, p1l, it, u)
                fill(1)
                for u in range(2):
                    dve.wait_ge(k_ps.sem, k_ps.now(it, u))
                    nc.vector.tensor_scalar(kx[u][0:D2, 1, 0, :], ps[0:D2, 4 * u + 1, :], col("even", 0, D2), col("bkeb", 0, D2),
                                            ALU.mult, ALU.add).then_inc(kv_up.sem, 1)
                    nc.vector.tensor_scalar(kx[u][0:D2, 1, 1, :], ps[0:D2, 4 * u + 1, :], col("odd", 0, D2), col("bkob", 0, D2),
                                            ALU.mult, ALU.add).then_inc(kv_up.sem, 1)
                for u in range(2):
                    dve.wait_ge(v_ps.sem, v_ps.now(it, u))
                    nc.vector.tensor_tensor(split4(yb[u][:, :, :]), two_banks(u, 2, D),
                                            row("bv").unsqueeze(1).unsqueeze(1).to_broadcast([P, 2, 2, D]), ALU.add).then_inc(v_up.sem, 1)
                fill(1)
                for pg in range(2):
                    for u in range(2):
                        dve.wait_ge(sc.sem, sc.now(it, 2 * pg + u))
                        if pg == 1:
                            dve.wait_ge(ptt.sem, ptt.now(it, u))
                        s = ps[:, 4 * u:4 * u + 4, :].rearrange("p r (g s c) -> p g s r c", g=2, s=2)
                        for g in range(2):
                            nc.vector.tensor_tensor(sm[u][:, g, 0:4, :], s[:, g, 0, :, :],
                                                    mask[:, :].unsqueeze(1).to_broadcast([P, 4, P]), ALU.add).then_inc(sadd.sem, 1)
                            nc.vector.tensor_tensor(sm[u][:, g, 4:6, :], s[:, g, 1, 0:2, :],
                                                    mask[:, :].unsqueeze(1).to_broadcast([P, 2, P]), ALU.add).then_inc(sadd.sem, 1)
                        dve.wait_ge(sadd.sem, sadd.now(it, 2 * pg + u))
                        nc.vector.tensor_reduce(sm_mx[u][:, :], sm[u].rearrange("p g j (a c) -> p (g j a) c", a=2),
                                                AXX, ALU.max).then_inc(smax.sem, 1)
                    fill(1)
                    for u in range(2):
                        dve.wait_ge(ptt.sem, ptt.now(it, 2 * pg + u))
                        nc.vector.tensor_copy(pt[u][:, 0:4, :], ps[:, 4 * u, :].rearrange("p (j c) -> p j c", j=4)).then_inc(ptv.sem, 1)
                    fill(1)
                    for u in range(2):
                        dve.wait_ge(pv.sem, pv.now(it, 2 * pg + u))
                        o = ps[:, 4 * u + 3, 0:2 * HEADS * (HD + 1)].rearrange("p (h c) -> p h c", c=HD + 1)
                        nc.vector.reciprocal(rden[u][:, :], o[:, :, HD]).then_inc(rd.sem, 1)
                        dve.wait_ge(rd.sem, rd.now(it, 2 * pg + u))
                        nc.vector.tensor_tensor(
                            nb[u][:, 2 * pg:2 * pg + 2, :].rearrange("p g (h c) -> p (g h) c", c=HD), o[:, :, 0:HD],
                            rden[u][:, :].unsqueeze(2).to_broadcast([P, 2 * HEADS, HD]), ALU.mult).then_inc(at.sem, 1)
                for u in range(2):
                    dve.wait_ge(t2.sem, t2.now(it, u))
                    pack_low(nc, dve, ps, 4 * u, pk[u], p2h, p2l, it, u)
                fill(1)
                for u in range(2):
                    dve.wait_ge(pr.sem, pr.now(it, u))
                    dve.wait_ge(hbias.sem, hbias.now(it, u))
                    nc.vector.tensor_tensor(split4(hb[u][:, :, :]), two_banks(u, 2, D), split4(hb[u][:, :, :]), ALU.add).then_inc(h1.sem, 1)
                for u in range(2):
                    dve.wait_ge(h1.sem, h1.now(it, u))
                    norm_stats(nc, stack, dve, hb[u], st[u], mv[u], s3, m3, it, u)
                fill(1)
                for u in range(2):
                    dve.wait_ge(pl3.sem, pl3.now(it, u))
                    norm_apply(nc, yb[u], hb[u], mv[u], rs[u], n2)
                for u in range(2):
                    dve.wait_ge(n2.sem, n2.now(it, u))
                    nc.vector.tensor_tensor(hb[u][:, :, :], hb[u][:, :, :], yb[u][:, :, :], ALU.add).then_inc(base.sem, 1)
                    for g in range(NG):
                        nc.vector.scalar_tensor_tensor(nb[u][:, g, :], yb[u][:, g, :], rc[u][:, g:g + 1],
                                                       row("scale"), ALU.mult, ALU.mult).then_inc(tt.sem, 1)
                for u in range(2):
                    dve.wait_ge(t3.sem, t3.now(it, u))
                    pack_low(nc, dve, ps, 4 * u, pk[u], p3h, p3l, it, u)
                for u in range(2):
                    conv_lows(it + 1, u)
                for u in range(2):
                    dve.wait_ge(gt.sem, gt.now(it, u))
                    dve.wait_ge(st_mask[u].sem, st_mask[u].last(it, 0))
                    dve.wait_ge(st_fw[u].sem, st_fw[u].last(it, 0))
                    router.choose(dve, ps[:, 4 * u + 2, 0:NG * 16].rearrange("p (g e) -> p g e", g=NG), row("gateb"), it, u)

        @block.scalar
        def _(act):
            act.wait_ge(consts, 48)
            act.wait_ge(setup, 9)

            def tap0(it, u):
                act.wait_ge(loaded[u].sem, loaded[u].now(it, 0))
                nc.scalar.activation(acc0[u], xin[u][:, 0:NB, 0:CONV_T], ACT.Identity,
                                     bias=col("bdwa"), scale=col("tap0a")).then_inc(conv0.sem, 1)
                nc.scalar.activation(acc1[u], xin[u][:, NB:NB + NB // 2, 0:CONV_T], ACT.Identity,
                                     bias=col("bdwb"), scale=col("tap0b")).then_inc(conv0.sem, 1)

            def conv_highs(it, u):
                for c, (c0, c1) in enumerate(((0, NC), (NC, NC + NC // 2))):
                    act.wait_ge(conv.sem, conv.now(it, u, 2 * (TAPS - 2) + c + 1))
                    nc.scalar.copy(cv[u][:, c0:c1], acc[u][:, c0:c1]).then_inc(conv_h.sem, 1)

            for u in range(2):
                tap0(0, u)
            for u in range(2):
                conv_highs(0, u)
            with act.Fori(0, NT // 2) as it:
                for u in range(2):
                    for c in range(2):
                        act.wait_ge(pooled.sem, pooled.now(it, u, c + 1))
                        nc.scalar.activation(mx[u][:, c, :, 0:T], mx[u][:, c, :, 0:T], ACT.Relu,
                                             bias=col(f"bpw{'ab'[c]}")).then_inc(act_r.sem, 1)
                    act.wait_ge(act_r.sem, act_r.now(it, u, 1))
                    nc.scalar.copy(pk[u][:, 0, :], mx[u][:, 0].rearrange("p b s -> p (b s)")).then_inc(hp_h.sem, 1)
                    act.wait_ge(act_r.sem, act_r.now(it, u, 2))
                    nc.scalar.copy(pk[u][0:D2, 2, :], mx[u][0:D2, 1].rearrange("p b s -> p (b s)")).then_inc(hp_h.sem, 1)
                for u in range(2):
                    act.wait_ge(conv_l.sem, conv_l.now(it, u))
                    tap0(it + 1, u)
                for u in range(2):
                    act.wait_ge(ftd.sem, ftd.now(it, u))
                    nc.scalar.copy(split4(pq[u][0]), dft_out(u, 0)).then_inc(pq_h.sem, 1)
                for u in range(2):
                    act.wait_ge(fts.sem, fts.now(it, u))
                    nc.scalar.copy(split4(bs[u][:, :, :]), two_banks(u, 2, 2 * KP)[:, :, :, KP:2 * KP]).then_inc(bs_up.sem, 1)
                for u in range(2):
                    act.wait_ge(t1.sem, t1.now(it, u))
                    pack_high(nc, ps, 4 * u, pk[u], p1h)
                for u in range(2):
                    act.wait_ge(q_ps.sem, q_ps.now(it, u))
                    nc.scalar.activation(q[u][:, 0, :], ps[:, 4 * u + 2, :], ACT.Identity, bias=col("bqa")).then_inc(q_up.sem, 1)
                    nc.scalar.activation(q[u][0:D2, 1, :], ps[0:D2, 4 * u + 3, :], ACT.Identity, bias=col("bqb", 0, D2)).then_inc(q_up.sem, 1)
                for u in range(2):
                    act.wait_ge(k_ps.sem, k_ps.now(it, u))
                    nc.scalar.activation(kx[u][:, 0, 0, :], ps[:, 4 * u, :], ACT.Identity, bias=col("bkea"), scale=col("even")).then_inc(ka_up.sem, 1)
                    nc.scalar.activation(kx[u][:, 0, 1, :], ps[:, 4 * u, :], ACT.Identity, bias=col("bkoa"), scale=col("odd")).then_inc(ka_up.sem, 1)
                for u in range(2):
                    act.wait_ge(v_up.sem, v_up.now(it, u))
                    for b in range(2):
                        par = 1 - b
                        nc.scalar.copy(
                            vblk[u][64 * par:64 * par + 64, :, b, :, par, 0:HD],
                            yb[u][64 * b:64 * b + 64, :, :].rearrange("p g (j a c) -> p g j a c", j=PAIRS, a=2)[:, :, :, par, :]
                        ).then_inc(vo_up.sem, 1)
                for pg in range(2):
                    for u in range(2):
                        act.wait_ge(ssub.sem, ssub.now(it, 2 * pg + u))
                        nc.scalar.activation(sm[u], sm[u], ACT.Exp).then_inc(sexp.sem, 1)
                    for u in range(2):
                        act.wait_ge(ptt.sem, ptt.now(it, 2 * pg + u))
                        for j in range(1, 3):
                            nc.scalar.copy(pt[u][:, 4 * j:4 * j + 4, :],
                                           ps[:, 4 * u + j, :].rearrange("p (j c) -> p j c", j=4)).then_inc(pta.sem, 1)
                for u in range(2):
                    act.wait_ge(t2.sem, t2.now(it, u))
                    pack_high(nc, ps, 4 * u, pk[u], p2h)
                for u in range(2):
                    conv_highs(it + 1, u)
                for u in range(2):
                    act.wait_ge(t3.sem, t3.now(it, u))
                    pack_high(nc, ps, 4 * u, pk[u], p3h)
                for u in range(2):
                    act.wait_ge(st_x[u].sem, st_x[u].last(it, 0))
                    row_highs(nc, nb[u], [(0, xs[u][:, :, :])], xh)
                for u in range(2):
                    router.exponentials(act, it, u)

        @block.tensor
        def _(pe):
            pe.wait_ge(identity, 2)
            pe.wait_ge(setup, 9)
            with pe.Fori(0, NT // 2) as it:
                for u in range(2):
                    pe.wait_ge(conv_h.sem, conv_h.now(it, u))
                    pe.wait_ge(conv_l.sem, conv_l.now(it, u))
                    pe.wait_ge(router.biased.sem, router.biased.last(it, u))
                    hi, lo, m = 0, NC * 3 // 2, NC // 2
                    for c in range(2):
                        for h in range(2):
                            out = ps[:, 4 * u + 2 * c + h, 0:m]
                            w = w_at("pw", c * P, P)
                            xh, xl = cv[u][:, hi + h * m:hi + (h + 1) * m], cv[u][:, lo + h * m:lo + (h + 1) * m]
                            nc.tensor.matmul(out, W[:, 0, 0, w], xh, start=True, stop=False)
                            nc.tensor.matmul(out, W[:, 1, 0, w], xh, start=False, stop=False)
                            nc.tensor.matmul(out, W[:, 0, 0, w], xl, start=False, stop=False)
                            r = slice(64 * h, 64 * h + 64)
                            xh, xl = cv[u][r, hi + NC:hi + NC + m], cv[u][r, lo + NC:lo + NC + m]
                            nc.tensor.matmul(out, W[r, 0, 1, w], xh, start=False, stop=False)
                            nc.tensor.matmul(out, W[r, 1, 1, w], xh, start=False, stop=False)
                            last = nc.tensor.matmul(out, W[r, 0, 1, w], xl, start=False, stop=True)
                    last.then_inc(pw_done.sem, 1)
                for u in range(2):
                    pe.wait_ge(hp_h.sem, hp_h.now(it, u))
                    pe.wait_ge(hp_l.sem, hp_l.now(it, u))
                    for g in range(NG):
                        last = product5(nc, ps[:, 4 * u + g // 2, (g % 2) * 256:(g % 2) * 256 + 2 * KP], pk[u],
                                        slice(g * P, (g + 1) * P), W, w_at("fft"), False, True, True)
                    last.then_inc(ftd.sem, 1)
                for u in range(2):
                    pe.wait_ge(pq_h.sem, pq_h.now(it, u))
                    pe.wait_ge(pq_l.sem, pq_l.now(it, u))
                    for g in range(NG):
                        for c in range(2):
                            out = ps[:, 4 * u + 2 + g // 2, (g % 2) * 256 + c * KP:(g % 2) * 256 + (c + 1) * KP]
                            cc = slice(c * KP, (c + 1) * KP)
                            nc.tensor.matmul(out, CS[:, 0, c, :], pq[u][0][:, g, cc], start=True, stop=False)
                            nc.tensor.matmul(out, CS[:, 1, c, :], pq[u][0][:, g, cc], start=False, stop=False)
                            last = nc.tensor.matmul(out, CS[:, 0, c, :], pq[u][1][:, g, cc], start=False, stop=True)
                    last.then_inc(fts.sem, 1)
                for u in range(2):
                    pe.wait_ge(n1.sem, n1.now(it, u))
                    transpose_tile(nc, ps, 4 * u, nb[u], ident, t1)
                for u in range(2):
                    pe.wait_ge(p1h.sem, p1h.now(it, u))
                    pe.wait_ge(p1l.sem, p1l.now(it, u))
                    for c in range(2):
                        last = product5(nc, ps[:, 4 * u + 2 + c, :], pk[u], slice(0, N), W, w_at("q", c * P, P), True, True, True)
                    last.then_inc(q_ps.sem, 1)
                    for c in range(2):
                        last = product5(nc, ps[:, 4 * u + c, :], pk[u], slice(0, N), W, w_at("k", c * P, P), True, True, True)
                    last.then_inc(k_ps.sem, 1)
                for u in range(2):
                    pe.wait_ge(q_up.sem, q_up.now(it, u))
                    for g in range(NG):
                        last = product5(nc, ps[:, 4 * u + 2 + g // 2, (g % 2) * 256:(g % 2) * 256 + D], pk[u],
                                        slice(g * P, (g + 1) * P), W, w_at("v"), False, True, True)
                    last.then_inc(v_ps.sem, 1)
                for pg in range(2):
                    for u in range(2):
                        if pg == 0:
                            pe.wait_ge(ka_up.sem, ka_up.now(it, u))
                            pe.wait_ge(kv_up.sem, kv_up.now(it, u))
                            pe.wait_ge(v_up.sem, v_up.now(it, u))
                        else:
                            pe.wait_ge(at.sem, at.now(it, u))
                        for g in range(2):
                            for b in range(2):
                                tok = slice(((2 * pg + g) * 2 + b) * TP, ((2 * pg + g) * 2 + b + 1) * TP)
                                for j in range(PAIRS):
                                    c, r = divmod(j, 4)
                                    f = slice(32 * r, 32 * r + 32)
                                    last = nc.tensor.matmul(
                                        ps[64 * b:64 * b + 64, 4 * u + r, g * 256 + c * P:g * 256 + (c + 1) * P],
                                        q[u][f, c, tok], kx[u][f, c, :, tok], start=True, stop=True)
                        last.then_inc(sc.sem, 1)
                    for u in range(2):
                        pe.wait_ge(sexp.sem, sexp.now(it, 2 * pg + u))
                        for g in range(2):
                            for j in range(PAIRS):
                                k = g * PAIRS + j
                                last = nc.tensor.transpose(ps[:, 4 * u + k // 4, (k % 4) * P:(k % 4 + 1) * P],
                                                           sm[u][:, g, j, :], ident[:, :])
                        last.then_inc(ptt.sem, 1)
                    for u in range(2):
                        pe.wait_ge(pta.sem, pta.now(it, 2 * pg + u))
                        pe.wait_ge(ptv.sem, ptv.now(it, 2 * pg + u))
                        if pg == 0:
                            pe.wait_ge(vd_up.sem, vd_up.now(it, u))
                            pe.wait_ge(vo_up.sem, vo_up.now(it, u))
                        for g in range(2):
                            for b in range(2):
                                for j in range(PAIRS):
                                    k = g * PAIRS + j
                                    last = nc.tensor.matmul(
                                        ps[64 * b:64 * b + 64, 4 * u + 3, k * 34:(k + 1) * 34],
                                        pt[u][:, k, 64 * b:64 * b + 64],
                                        vblk[u][:, 2 * pg + g, b, j, :, :], start=True, stop=True)
                        last.then_inc(pv.sem, 1)
                for u in range(2):
                    pe.wait_ge(at.sem, at.now(it, 2 + u))
                    transpose_tile(nc, ps, 4 * u, nb[u], ident, t2)
                for u in range(2):
                    pe.wait_ge(p2h.sem, p2h.now(it, u))
                    pe.wait_ge(p2l.sem, p2l.now(it, u))
                    for g in range(NG):
                        last = product5(nc, ps[:, 4 * u + 2 + g // 2, (g % 2) * 256:(g % 2) * 256 + D], pk[u],
                                        slice(g * P, (g + 1) * P), W, w_at("proj"), False, True, True)
                    last.then_inc(pr.sem, 1)
                for u in range(2):
                    pe.wait_ge(tt.sem, tt.now(it, u))
                    transpose_tile(nc, ps, 4 * u, nb[u], ident, t3)
                for u in range(2):
                    pe.wait_ge(p3h.sem, p3h.now(it, u))
                    pe.wait_ge(p3l.sem, p3l.now(it, u))
                    for g in range(NG):
                        last = product5(nc, ps[:, 4 * u + 2, g * 16:(g + 1) * 16], pk[u],
                                        slice(g * P, (g + 1) * P), W, w_at("gate"), False, True, True)
                    last.then_inc(gt.sem, 1)


HID = 3072
GROUPS = NT * NG
ROWS = GROUPS * P
WAYS_S = 6
NOWHERE = float(1 << 22)


def slot_blocks(k, experts):
    most = -(-B * T * k // P) + experts
    return -(-most // WAYS_S) * WAYS_S


E_B, K_B = 16, 4
BLK_B = slot_blocks(K_B, E_B)
E_D, K_D = 4, 1
BLK_D = slot_blocks(K_D, E_D)


def passes(eng, blocks, step, first, last):
    for n in range(first, WAYS_S):
        step(0, n, lambda m: m >= 0)
    with eng.Fori(1, blocks // WAYS_S - 1) as it:
        for u in range(WAYS_S):
            step(it, u, lambda m: True)
    for n in range(WAYS_S, 2 * WAYS_S + last):
        step(blocks // WAYS_S - 2, n, lambda m: m < 2 * WAYS_S)


class BlockExperts:
    LATE, ROW = 4, 12

    def __init__(self, pe, prefix, table, experts):
        self.pe, self.table, self.experts = pe, table, experts
        self.registers = [pe.alloc_register(f"{prefix}_expert{j}") for j in range(self.ROW)]

    def load(self, it, u):
        self.first = u
        self.pe.load(self.registers, self.table[0:1, bass.ds((it + u // WAYS_S) * self.ROW, self.ROW)])
        self.values = [self.pe.snap(r, min_val=0, max_val=self.experts - 1) for r in self.registers]

    def of(self, m):
        return self.values[m - self.first + self.LATE]


def among_first(it, m, n):
    return isinstance(it, int) and it * WAYS_S + m < n


def routing(nc, stack, io, pre, experts, k, blocks, row_ids, table, own_row, jobs, gates):
    E, GE, GK = experts, GROUPS * experts, GROUPS * k
    HALF = GK // 2
    with ExitStack() as ctx:
        sb = lambda n, shape, dt=F32: ctx.enter_context(nc.sbuf_tensor(f"{pre}_rt_{n}", shape, dt))
        ps = ctx.enter_context(nc.psum_tensor(f"{pre}_rt_ps", [P, 6, 512], F32))
        banks, width = -(-GE // 512), min(GE, 512)
        stage = sb("stage", [P, 2, P])
        tri = sb("tri", [P, 2, P], F32R)
        pad = sb("pad", [P, 3])
        steps = sb("steps", [P, GROUPS])
        order = sb("order", [P, max(blocks, P)])
        number = sb("number", [P, GROUPS])
        mask = sb("mask", [P, GROUPS, E])
        chosen = sb("chosen", [P, GROUPS, E], F32R)
        ones = sb("ones", [P, 1])
        tot, inc = sb("tot", [P, E, GROUPS]), sb("inc", [P, E, GROUPS])
        cum, cnt = sb("cum", [P, E + 1]), sb("cnt", [P, E])
        nbk, end, off = sb("nbk", [P, E]), sb("end", [P, E]), sb("off", [P, E])
        best = sb("best", [P, GROUPS, 8])
        slot, hi = sb("slot", [P, GROUPS, k]), sb("hi", [P, GROUPS, k])
        value = sb("value", [P, GROUPS, k])
        slot_i, block_i = sb("sloti", [P, GROUPS, k], I32), sb("blocki", [P, GROUPS, k], I32)
        lane = [sb(f"lane{j}", [P, P], F32R) for j in range(4)]
        where = [sb(f"where{j}", [P, blocks], F32R) for j in range(4)]
        of, more = sb("of", [P, blocks]), sb("more", [P, blocks])
        loaded = stack.new(f"{pre}_rt_loaded")
        tri_ready, mask_ready = stack.new(f"{pre}_rt_tri"), stack.new(f"{pre}_rt_mask")
        counted, zeroed = stack.new(f"{pre}_rt_counted"), stack.new(f"{pre}_rt_zeroed")
        planned = Count(stack.new(f"{pre}_rt_planned"))
        ids_ready, gates_ready = (stack.new(f"{pre}_rt_{n}") for n in ("ids", "gates"))
        placed = Signal(nc, stack, f"{pre}_rt_placed", 2, 4)
        taken = Signal(nc, stack, f"{pre}_rt_taken", 1, 4, credit=True)
        gates_loaded, stored = stack.new(f"{pre}_rt_gatesloaded"), stack.new(f"{pre}_rt_stored")
        split = SplitWeights(nc, stack, ctx, f"{pre}w", jobs)
        block = ctx.enter_context(nc.Block())
        if gates:
            gate = sb("gate", [P, GROUPS, E])
            slot_out = sb("slotout", [P, GROUPS, k], I32)
        flat = lambda x: x[:, :, :].rearrange("p a b -> p (a b)")

        @block.sync
        def _(sp):
            sp.dma_start(stage[:, :, :], io["rt_tri"]).then_inc(loaded, 16)
            sp.dma_start(pad[:, :], io["rt_pad"]).then_inc(loaded, 16)
            sp.dma_start(steps[:, :], io["rt_steps"]).then_inc(loaded, 16)
            sp.dma_start(order[:, :], io["rt_order"][:, 0:max(blocks, P)]).then_inc(loaded, 16)
            sp.dma_start(number[:, :], io["rt_number"]).then_inc(loaded, 16)
            sp.dma_start(mask[:, :, :], io[f"mask_{pre}"]).then_inc(loaded, 16)
            split.load(sp)
            if gates:
                sp.dma_start(gate[:, :, :], io[f"gate_{pre}"]).then_inc(gates_loaded, 16)
                sp.wait_ge(ids_ready, 1)
                sp.dma_start(io[f"slots_{pre}"], slot_out[:, :, :]).then_inc(stored, 16)
                sp.wait_ge(gates_ready, 1)
                sp.dma_start(io[f"gates_{pre}"], value[:, :, :]).then_inc(stored, 16)
                sp.wait_ge(stored, 32)

        @block.scalar
        def _(act):
            split.round(act)

        @block.gpsimd
        def _(pool):
            split.subtract(pool)

        @block.tensor
        def _(pe):
            taken.credit(pe)
            pe.wait_ge(tri_ready, 1)
            pe.wait_ge(mask_ready, 1)
            for h in range(banks):
                cols = slice(h * width, (h + 1) * width)
                nc.tensor.matmul(ps[:, h, 0:width], tri[:, 0, :], flat(chosen)[:, cols], start=True, stop=True)
                last = nc.tensor.matmul(ps[:, 2 + h, 0:width], tri[:, 1, :], flat(chosen)[:, cols], start=True, stop=True)
            last.then_inc(counted, 1)
            pe.wait_ge(zeroed, 4)
            for half in range(2):
                nc.tensor.matmul(ps[:, 4 + half, 0:blocks], tri[:, 1, :], where[0][:, :], start=True, stop=False,
                                 skip_group_check=True).then_inc(zeroed, 1)
            for half in range(2):
                with pe.Fori(half * HALF // 4, (half + 1) * HALF // 4) as it:
                    for u in range(4):
                        pe.wait_ge(placed.sem, placed.now(it, u))
                        nc.tensor.matmul(ps[:, 4 + half, 0:blocks], lane[u][:, :], where[u][:, :], start=False, stop=False,
                                         skip_group_check=True).then_inc(taken.sem, 1)

        @block.vector
        def _(dve):
            V = nc.vector
            for j in range(4):
                V.memset(where[j][:, :].bitcast(F32), 0.0).then_inc(zeroed, 1)
            planned.of(V.memset(ones[:, :], 1.0))
            planned.of(V.memset(table[:, :], 0))
            planned.of(V.memset(cum[:, 0:1], 0.0))
            dve.wait_ge(loaded, 96)
            V.tensor_copy(tri[:, :, :], stage[:, :, :]).then_inc(tri_ready, 1)
            V.tensor_scalar(chosen[:, :, :], mask[:, :, :], pad[:, 0:1], None, ALU.mult).then_inc(mask_ready, 1)
            dve.wait_ge(counted, 1)
            banked = lambda b0: ps[:, b0:b0 + banks, 0:width].rearrange("p b n -> p (b n)").rearrange("p (g e) -> p g e", e=E)
            planned.of(V.tensor_copy(tot[:, :, :], banked(2).rearrange("p g e -> p e g")))
            dve.wait_ge(planned.sem, planned.value)
            planned.of(V.tensor_tensor_scan(flat(inc), ones[:, :].to_broadcast([P, GE]), flat(tot), 0.0,
                                            op0=ALU.mult, op1=ALU.add))
            dve.wait_ge(planned.sem, planned.value)
            planned.of(V.tensor_tensor(tot[:, :, :], inc[:, :, :], tot[:, :, :], ALU.subtract))
            planned.of(V.tensor_copy(cum[:, 1:E + 1], inc[:, :, GROUPS - 1]))
            dve.wait_ge(planned.sem, planned.value)
            planned.of(V.tensor_tensor(cnt[:, :], cum[:, 1:E + 1], cum[:, 0:E], ALU.subtract))
            dve.wait_ge(planned.sem, planned.value)
            planned.of(V.tensor_tensor(inc[:, :, :], cnt[:, :].unsqueeze(2).to_broadcast([P, E, GROUPS]),
                                       steps[:, :].unsqueeze(1).to_broadcast([P, E, GROUPS]), ALU.is_gt))
            dve.wait_ge(planned.sem, planned.value)
            planned.of(V.tensor_reduce(nbk[:, :], inc[:, :, :], AXX, ALU.add))
            dve.wait_ge(planned.sem, planned.value)
            planned.of(V.tensor_tensor_scan(end[:, :], ones[:, :].to_broadcast([P, E]), nbk[:, :], 0.0,
                                            op0=ALU.mult, op1=ALU.add))
            dve.wait_ge(planned.sem, planned.value)
            planned.of(V.tensor_tensor(off[:, :], end[:, :], nbk[:, :], ALU.subtract))
            dve.wait_ge(planned.sem, planned.value)
            planned.of(V.scalar_tensor_tensor(off[:, :], off[:, :], float(P), cum[:, 0:E], ALU.mult, ALU.subtract))
            dve.wait_ge(planned.sem, planned.value)
            planned.of(V.tensor_scalar(off[:, :], off[:, :], 1.0, None, ALU.add))
            dve.wait_ge(planned.sem, planned.value)
            planned.of(V.tensor_tensor(tot[:, :, :], tot[:, :, :], off[:, :].unsqueeze(2).to_broadcast([P, E, GROUPS]), ALU.add))
            dve.wait_ge(planned.sem, planned.value)
            pos = inc[:, :, :].rearrange("p e g -> p (e g)").rearrange("p (g e) -> p g e", e=E)
            planned.of(V.tensor_tensor(pos, banked(0), tot[:, :, :].rearrange("p e g -> p g e"), ALU.add))
            dve.wait_ge(planned.sem, planned.value)
            planned.of(V.tensor_tensor(pos, pos, chosen[:, :, :].bitcast(F32), ALU.mult))
            dve.wait_ge(planned.sem, planned.value)
            if k == 1:
                planned.of(V.tensor_reduce(best[:, :, 0], pos, AXX, ALU.add))
            else:
                for g in range(GROUPS):
                    planned.of(V.max(best[:, g, :], pos[:, g, :]))
            dve.wait_ge(planned.sem, planned.value)
            planned.of(V.tensor_scalar(slot[:, :, :], best[:, :, 0:k], -1.0, pad[:, 1:2], ALU.add, ALU.add))
            dve.wait_ge(planned.sem, planned.value)
            planned.of(V.tensor_copy(slot_i[:, :, :], slot[:, :, :]))
            planned.of(V.tensor_copy(value[:, :, :], number[:, :].unsqueeze(2).to_broadcast([P, GROUPS, k])))
            dve.wait_ge(planned.sem, planned.value)
            if gates:
                V.tensor_scalar(slot_out[:, :, :], best[:, :, 0:k], -1.0, 0.0, ALU.add, ALU.max).then_inc(ids_ready, 1)
            planned.of(V.tensor_scalar(block_i[:, :, :], slot_i[:, :, :], 7, None, ALU.arith_shift_right))
            dve.wait_ge(planned.sem, planned.value)
            planned.of(V.tensor_copy(hi[:, :, :], block_i[:, :, :]))
            dve.wait_ge(planned.sem, planned.value)
            planned.of(V.scalar_tensor_tensor(slot[:, :, :], hi[:, :, :], -float(P), slot[:, :, :], ALU.mult, ALU.add))
            dve.wait_ge(planned.sem, planned.value)
            dve.wait_ge(zeroed, 6)
            for half in range(2):
                with dve.Fori(half * HALF // 4, (half + 1) * HALF // 4) as it:
                    for u in range(4):
                        at = bass.ds(it * 4 + u, 1)
                        dve.wait_ge(taken.sem, taken.last(it, u))
                        V.tensor_scalar(lane[u][:, :], order[:, 0:P], flat(slot)[:, at], None, ALU.is_equal
                                        ).then_inc(placed.sem, 1)
                        V.tensor_scalar(where[u][:, :], order[:, 0:blocks], flat(hi)[:, at], flat(value)[:, at],
                                        ALU.is_equal, ALU.mult).then_inc(placed.sem, 1)
            planned.of(V.tensor_scalar(of[:, :], order[:, 0:blocks], end[:, 0:1], None, ALU.is_ge))
            for e in range(1, E - 1):
                dve.wait_ge(planned.sem, planned.value)
                planned.of(V.scalar_tensor_tensor(of[:, :], order[:, 0:blocks], end[:, e:e + 1], of[:, :], ALU.is_ge, ALU.add))
            dve.wait_ge(planned.sem, planned.value)
            by_pass = table[:, :].rearrange("o (n r) -> o n r", r=BlockExperts.ROW)
            late = BlockExperts.LATE
            in_passes = of[0:1, :].rearrange("o (n w) -> o n w", w=WAYS_S)
            V.tensor_copy(by_pass[:, :, late:late + WAYS_S], in_passes)
            V.tensor_copy(by_pass[:, 1:, 0:late], in_passes[:, 0:-1, WAYS_S - late:])
            planned.of(V.tensor_scalar(own_row[:, :], of[0:64, :], pad[0:64, 2:3], None, ALU.is_equal))
            dve.wait_ge(taken.sem, taken.now(GK // 4 - 1, 3))
            planned.of(V.tensor_scalar(more[:, :], ps[:, 5, 0:blocks], 0.0, float(ROWS // 2), ALU.is_gt, ALU.mult))
            dve.wait_ge(planned.sem, planned.value)
            planned.of(V.tensor_tensor(more[:, :], ps[:, 5, 0:blocks], more[:, :], ALU.add))
            dve.wait_ge(planned.sem, planned.value)
            planned.of(V.tensor_tensor(more[:, :], ps[:, 4, 0:blocks], more[:, :], ALU.add))
            dve.wait_ge(planned.sem, planned.value)
            planned.of(V.tensor_scalar(of[:, :], more[:, :], 0.0, NOWHERE, ALU.is_equal, ALU.mult))
            dve.wait_ge(planned.sem, planned.value)
            planned.of(V.scalar_tensor_tensor(of[:, :], more[:, :], -1.0, of[:, :], ALU.add, ALU.add))
            dve.wait_ge(planned.sem, planned.value)
            V.tensor_copy(row_ids[:, :], of[:, :])
            if gates:
                dve.wait_ge(gates_loaded, 16)
                for j in range(k):
                    same = tot[:, :, :].rearrange("p e g -> p (e g)").rearrange("p (g e) -> p g e", e=E)
                    planned.of(V.tensor_tensor(same, pos, best[:, :, j:j + 1].to_broadcast([P, GROUPS, E]), ALU.is_equal))
                    dve.wait_ge(planned.sem, planned.value)
                    planned.of(V.tensor_tensor(same, same, gate[:, :, :], ALU.mult))
                    dve.wait_ge(planned.sem, planned.value)
                    planned.of(V.tensor_reduce(value[:, :, j], same, AXX, ALU.add))
                    dve.wait_ge(planned.sem, planned.value)
                dve.sem_inc(gates_ready, 1)


def first_experts(nc, stack, io):
    pre, E, blocks, W_ = "b", E_B, BLK_B, WAYS_S
    HE = D
    with ExitStack() as ctx:
        sb = lambda n, shape, dt=F32: ctx.enter_context(nc.sbuf_tensor(f"{pre}_sb_{n}", shape, dt))
        sig = lambda n, per=1, step=1: Signal(nc, stack, f"{pre}_{n}", per, W_, step)
        row_ids, table = sb("rowids", [P, blocks], I32), sb("table", [1, blocks // W_ * BlockExperts.ROW], I32)
        own_row = sb("ownrow", [64, blocks])
        W1 = sb("W1", [P, 2, 2, E, 2 * HE], F32R)
        W2 = sb("W2", [P, 2, 2, E, D], F32R)
        BR = sb("BR", [64, 2 * HE + D], F32R)
        stage = sb("stage", [E, 2 * HE + D])
        routing(nc, stack, io, pre, E, K_B, blocks, row_ids, table, own_row, [
            (io["b_w1"].rearrange("p a n -> p (a n)"), W1[:, 0].rearrange("p a e n -> p (a e n)"),
             W1[:, 1].rearrange("p a e n -> p (a e n)")),
            (io["b_w2"].rearrange("p a n -> p (a n)"), W2[:, 0].rearrange("p a e n -> p (a e n)"),
             W2[:, 1].rearrange("p a e n -> p (a e n)"))], True)
        ident, ident_r = sb("ident", [P, P]), sb("identr", [P, P], F32R)
        pick = [sb(f"pick{j}", [64, P], F32R) for j in range(W_)]
        X = [sb(f"X{j}", [P, 3, P], F32R) for j in range(W_)]
        own = [sb(f"own{j}", [P, 1], I32) for j in range(W_)]
        xk = [sb(f"xk{j}", [P, 3, P], F32R) for j in range(3)]
        hk = [sb(f"hk{j}", [P, 3, P], F32R) for j in range(3)]
        glu, lin, sg = ([sb(f"{n}{j}", [P, HE]) for j in range(3)] for n in ("glu", "lin", "sg"))
        h = [sb(f"h{j}", [P, 2 * P]) for j in range(3)]
        y = [sb(f"y{j}", [P, D]) for j in range(3)]
        ps = ctx.enter_context(nc.psum_tensor(f"{pre}_ps", [P, 8, 512], F32))
        consts, identity, setup = (stack.new(f"{pre}_{n}") for n in ("consts", "identity", "setup"))
        split = stack.new(f"{pre}_split")
        owned, picked = sig("owned"), sig("picked")
        gathered = [Signal(nc, stack, f"{pre}_gathered{j}", 1, 1, 16) for j in range(W_)]
        stored = [Signal(nc, stack, f"{pre}_stored{j}", 1, 2, 16) for j in range(3)]
        x_t, x_c, up, h_t, h_h, h_l = (sig(n, per) for n, per in (("xt", 1), ("xc", 1), ("up", 1), ("ht", 1), ("hh", 1), ("hl", 2)))
        cut_g, cut_l, gate, mixed, hidden = sig("cutg"), sig("cutl"), sig("gate"), sig("mixed"), sig("hidden")
        down, out = sig("down"), sig("out")
        block = ctx.enter_context(nc.Block())
        XB, HB, UP, OUT = 0, 2, 4, 6

        @block.sync
        def _(sp):
            sp.dma_start(stage[:, :], io["b_bias"]).then_inc(consts, 16)
            with sp.Fori(0, blocks // W_) as it:
                for u in range(W_):
                    sp.wait_ge(out.sem, out.now(it, u))
                    sp.sem_inc(stack.passed, 1)
                    sp.dma_start(io["slot_rows"].rearrange("(b p) d -> b p d", p=P)[it * W_ + u], y[u % 3][:, :]
                                 ).then_inc(stored[u % 3].sem, 16)
            for j in range(3):
                sp.wait_ge(stored[j].sem, 16 * blocks // 3)

        @block.gpsimd
        def _(pool):
            fill_identity(nc, pool, ident, identity)
            pool.wait_ge(identity, 2)
            nc.gpsimd.tensor_copy(ident_r[:, :], ident[:, :]).then_inc(identity, 1)

            def step(it, u, there):
                m = u + 4
                if there(m):
                    j = m % W_
                    if not among_first(it, m, W_):
                        pool.wait_ge(x_t.sem, x_t.now(it, m - W_))
                        pool.sem_inc(stack.passed, 1)
                    nc.gpsimd.tensor_copy(own[j][:, :], row_ids[:, bass.ds(it * W_ + m, 1)]).then_inc(owned.sem, 1)
                    pool.wait_ge(owned.sem, owned.now(it, m))
                    pool.sem_inc(stack.passed, 1)
                    nc.gpsimd.indirect_dma_start(X[j][:, :, :].rearrange("p a n -> p (a n)").bitcast(F32), None, io["rows_b"],
                                                 bass.IndirectOffsetOnAxis(own[j][:, :], 0), bounds_check=ROWS - 1,
                                                 oob_is_err=False).then_inc(gathered[j].sem, 16)

            pool.wait_ge(setup, W_)
            passes(pool, blocks, step, -4, 0)

        @block.scalar
        def _(act):
            act.wait_ge(consts, 16)
            act.wait_ge(setup, W_ + 5)
            nc.scalar.copy(BR[0:E, :], stage[:, :]).then_inc(split, 1)

            def step(it, u, there):
                m = u - 2
                if there(m):
                    act.wait_ge(h_t.sem, h_t.now(it, m))
                    if not among_first(it, m, 3):
                        act.wait_ge(down.sem, down.now(it, m - 3))
                    nc.scalar.copy(hk[m % 3][:, 0:3:2, :], ps[:, HB + m % 2, 0:2 * P].rearrange("p (a n) -> p a n", a=2)
                                   ).then_inc(h_h.sem, 1)
                if there(u):
                    act.wait_ge(cut_g.sem, cut_g.now(it, u))
                    if not among_first(it, u, 3):
                        act.wait_ge(hidden.sem, hidden.now(it, u - 3))
                    nc.scalar.activation(sg[u % 3][:, :], glu[u % 3][:, :], ACT.Sigmoid, scale=1.702).then_inc(gate.sem, 1)
                m = u + 2
                if there(m):
                    act.wait_ge(x_t.sem, x_t.now(it, m))
                    if not among_first(it, m, 3):
                        act.wait_ge(up.sem, up.now(it, m - 3))
                    nc.scalar.copy(xk[m % 3][:, :, :], ps[:, XB + m % 2, 0:3 * P].rearrange("p (a n) -> p a n", a=3)
                                   ).then_inc(x_c.sem, 1)
                m = u - 4
                if there(m):
                    act.wait_ge(down.sem, down.now(it, m))
                    if not among_first(it, m, 3):
                        j = m % 3
                        act.wait_ge(stored[j].sem, stored[j].now(it, m // 3 - 1))
                    nc.scalar.copy(y[m % 3][:, :], ps[:, OUT + m % 2, 0:D]).then_inc(out.sem, 1)

            passes(act, blocks, step, -2, 4)

        @block.vector
        def _(dve):
            for j in range(W_):
                nc.vector.memset(X[j][:, :, :].bitcast(F32), 0.0).then_inc(setup, 1)
            for j in range(3):
                nc.vector.memset(h[j][:, D:2 * P], 0.0).then_inc(setup, 1)
            nc.vector.memset(BR[:, :].bitcast(F32), 0.0).then_inc(setup, 1)
            dve.wait_ge(consts, 16)
            nc.vector.tensor_scalar(stage[:, HE:2 * HE], stage[:, HE:2 * HE], 1.0, None, ALU.add).then_inc(setup, 1)
            dve.wait_ge(split, 1)
            nc.vector.tensor_tensor(BR[32:32 + E, :], stage[:, :], BR[0:E, :].bitcast(F32), ALU.subtract
                                    ).then_inc(split, 1)

            def step(it, u, there):
                m = u - 1
                if there(m):
                    dve.wait_ge(mixed.sem, mixed.now(it, m))
                    dve.wait_ge(gate.sem, gate.now(it, m))
                    if not among_first(it, m, 3):
                        dve.wait_ge(h_t.sem, h_t.now(it, m - 3))
                    nc.vector.tensor_tensor(h[m % 3][:, 0:HE], lin[m % 3][:, :], sg[m % 3][:, :], ALU.mult).then_inc(hidden.sem, 1)
                if there(u):
                    dve.wait_ge(up.sem, up.now(it, u))
                    if not among_first(it, u, 3):
                        dve.wait_ge(hidden.sem, hidden.now(it, u - 3))
                        dve.wait_ge(gate.sem, gate.now(it, u - 3))
                    nc.vector.tensor_scalar(glu[u % 3][:, :], ps[:, UP + u % 2, 0:HE], 7.0, None, ALU.min).then_inc(cut_g.sem, 1)
                    nc.vector.tensor_scalar(lin[u % 3][:, :], ps[:, UP + u % 2, HE:2 * HE], 8.0, None, ALU.min
                                            ).then_inc(cut_l.sem, 1)
                m = u + 3
                if there(m):
                    if not among_first(it, m, W_):
                        dve.wait_ge(down.sem, down.now(it, m - W_))
                    nc.vector.tensor_copy(pick[m % W_][:, :], own_row[:, bass.ds(it * W_ + m, 1)].to_broadcast([64, P])
                                          ).then_inc(picked.sem, 1)
                if there(u):
                    dve.wait_ge(cut_l.sem, cut_l.now(it, u))
                    nc.vector.scalar_tensor_tensor(lin[u % 3][:, :], lin[u % 3][:, :], -6.0, glu[u % 3][:, :], ALU.max, ALU.mult
                                                   ).then_inc(mixed.sem, 1)
                m = u - 2
                if there(m):
                    c = hk[m % 3]
                    dve.wait_ge(h_h.sem, h_h.now(it, m))
                    nc.vector.tensor_tensor(c[:, 1, :], ps[:, HB + m % 2, 0:P], c[:, 0, :].bitcast(F32), ALU.subtract
                                            ).then_inc(h_l.sem, 1)
                    nc.vector.tensor_tensor(c[D2:P, 2, :], ps[0:D2, HB + m % 2, P:2 * P], c[0:D2, 2, :].bitcast(F32),
                                            ALU.subtract).then_inc(h_l.sem, 1)

            passes(dve, blocks, step, -3, 2)

        @block.tensor
        def _(pe):
            pe.wait_ge(identity, 3)
            pe.wait_ge(setup, W_ + 5)
            pe.wait_ge(split, 2)
            experts = BlockExperts(pe, pre, table, E)

            def product(bank, n, packed, W, e, j, columns, done):
                for i, (a, hlw, part) in enumerate(((0, 0, 0), (0, 1, 0), (1, 0, 0), (2, 0, 1), (2, 1, 1))):
                    nc.tensor.matmul(ps[:, bank, 0:n], packed[:, a, :],
                                     W[:, hlw, part, bass.ds(e, 1), :].rearrange("p a n -> p (a n)"),
                                     start=i == 0, stop=False, skip_group_check=True)
                nc.tensor.matmul(ps[:, bank, 0:n], pick[j][:, :], BR[:, columns],
                                 start=False, stop=True, skip_group_check=True).then_inc(done.sem, 1)

            def step(it, u, there):
                if there(u):
                    if u % W_ == 0:
                        experts.load(it, u)
                    e = experts.of(u)
                    pe.wait_ge(x_c.sem, x_c.now(it, u))
                    pe.wait_ge(picked.sem, picked.now(it, u))
                    if not among_first(it, u, 2):
                        pe.wait_ge(cut_l.sem, cut_l.now(it, u - 2))
                    product(UP + u % 2, 2 * HE, xk[u % 3], W1, e, u % W_, slice(0, 2 * HE), up)
                m = u + 2
                if there(m):
                    pe.wait_ge(gathered[m % W_].sem, gathered[m % W_].now(it, m // W_))
                    if not among_first(it, m, 2):
                        pe.wait_ge(x_c.sem, x_c.now(it, m - 2))
                    for a in range(3):
                        last = nc.tensor.transpose(ps[:, XB + m % 2, a * P:(a + 1) * P].bitcast(F32R), X[m % W_][:, a, :],
                                                   ident_r[:, :])
                    last.then_inc(x_t.sem, 1)
                m = u - 2
                if there(m):
                    pe.wait_ge(hidden.sem, hidden.now(it, m))
                    if not among_first(it, m, 2):
                        pe.wait_ge(h_l.sem, h_l.now(it, m - 2))
                    for a in range(2):
                        last = nc.tensor.transpose(ps[:, HB + m % 2, a * P:(a + 1) * P], h[m % 3][:, a * P:(a + 1) * P],
                                                   ident[:, :])
                    last.then_inc(h_t.sem, 1)
                m = u - 3
                if there(m):
                    pe.wait_ge(h_l.sem, h_l.now(it, m))
                    if not among_first(it, m, 2):
                        pe.wait_ge(out.sem, out.now(it, m - 2))
                    product(OUT + m % 2, D, hk[m % 3], W2, experts.of(m), m % W_, slice(2 * HE, 2 * HE + D), down)

            passes(pe, blocks, step, -2, 3)


def last_experts(nc, stack, io):
    pre, E, blocks, W_ = "d", E_D, BLK_D, WAYS_S
    HE = HID // E
    HC = HE // P
    HH = HE // 2
    with ExitStack() as ctx:
        sb = lambda n, shape, dt=F32: ctx.enter_context(nc.sbuf_tensor(f"{pre}_sb_{n}", shape, dt))
        sig = lambda n, per=1, step=1: Signal(nc, stack, f"{pre}_{n}", per, W_, step)
        row_ids, table = sb("rowids", [P, blocks], I32), sb("table", [1, blocks // W_ * BlockExperts.ROW], I32)
        own_row = sb("ownrow", [64, blocks])
        W1 = sb("W1", [P, 2, 2, E, HE], F32R)
        W2 = sb("W2", [P, 2, E, HC, D], F32R)
        BR = sb("BR", [64, HE + D], F32R)
        stage = sb("stage", [E, HE + D])
        routing(nc, stack, io, pre, E, 1, blocks, row_ids, table, own_row, [
            (io["d_w1"].rearrange("p a n -> p (a n)"), W1[:, 0].rearrange("p a e n -> p (a e n)"),
             W1[:, 1].rearrange("p a e n -> p (a e n)")),
            (io["d_w2"].rearrange("p a n -> p (a n)"), W2[:, 0].rearrange("p e c n -> p (e c n)"),
             W2[:, 1].rearrange("p e c n -> p (e c n)"))], False)
        ident, ident_r = sb("ident", [P, P]), sb("identr", [P, P], F32R)
        pick = [sb(f"pick{j}", [64, P], F32R) for j in range(W_)]
        X = [sb(f"X{j}", [P, 3 * D], F32R) for j in range(W_)]
        own = [sb(f"own{j}", [P, 1], I32) for j in range(W_)]
        pk = [sb(f"pk{j}", [P, 3, P], F32R) for j in range(2)]
        h = [sb(f"h{j}", [P, HE]) for j in range(2)]
        hh, hl = ([sb(f"{n}{j}", [P, HE], F32R) for j in range(2)] for n in ("hh", "hl"))
        y = [sb(f"y{j}", [P, D]) for j in range(2)]
        ps = ctx.enter_context(nc.psum_tensor(f"{pre}_ps", [P, 8, 512], F32))
        consts, identity, setup = (stack.new(f"{pre}_{n}") for n in ("consts", "identity", "setup"))
        split = stack.new(f"{pre}_split")
        owned, picked = sig("owned"), sig("picked")
        gathered = [Signal(nc, stack, f"{pre}_gathered{j}", 1, 1, 16) for j in range(W_)]
        scattered = sig("scattered", 1, 16)
        x_t, x_c, up, gelu, h_t, h_h, h_l = (
            sig(n, per) for n, per in (("xt", 1), ("xc", 1), ("up", 1), ("gelu", 2), ("ht", 1), ("hh", 1), ("hl", 1)))
        down, summed = sig("down"), sig("summed")
        block = ctx.enter_context(nc.Block())

        @block.sync
        def _(sp):
            sp.dma_start(stage[:, :], io["d_bias"]).then_inc(consts, 16)

        @block.gpsimd
        def _(pool):
            fill_identity(nc, pool, ident, identity)
            pool.wait_ge(identity, 2)
            nc.gpsimd.tensor_copy(ident_r[:, :], ident[:, :]).then_inc(identity, 1)

            def step(it, u, there):
                m = u + 2
                if there(m):
                    j = m % W_
                    if not among_first(it, m, W_):
                        pool.wait_ge(summed.sem, summed.now(it, m - W_))
                        pool.sem_inc(stack.passed, 1)
                        pool.wait_ge(scattered.sem, scattered.now(it, m - W_))
                        pool.sem_inc(stack.passed, 1)
                    nc.gpsimd.tensor_copy(own[j][:, :], row_ids[:, bass.ds(it * W_ + m, 1)]).then_inc(owned.sem, 1)
                    nc.gpsimd.tensor_copy(pick[j][:, :], own_row[:, bass.ds(it * W_ + m, 1)].to_broadcast([64, P])
                                          ).then_inc(picked.sem, 1)
                    pool.wait_ge(owned.sem, owned.now(it, m))
                    pool.sem_inc(stack.passed, 1)
                    nc.gpsimd.indirect_dma_start(X[j][:, :].bitcast(F32), None, io["rows_d"],
                                                 bass.IndirectOffsetOnAxis(own[j][:, :], 0), bounds_check=ROWS - 1,
                                                 oob_is_err=False).then_inc(gathered[j].sem, 16)
                m = u - 3
                if there(m):
                    pool.wait_ge(summed.sem, summed.now(it, m))
                    pool.sem_inc(stack.passed, 1)
                    if not among_first(it, m, 1):
                        pool.wait_ge(scattered.sem, scattered.now(it, m - 1))
                        pool.sem_inc(stack.passed, 1)
                    nc.gpsimd.indirect_dma_start(io["out"], bass.IndirectOffsetOnAxis(own[m % W_][:, :], 0),
                                                 y[m % 2][:, :], None, bounds_check=ROWS - 1,
                                                 oob_is_err=False).then_inc(scattered.sem, 16)

            pool.wait_ge(setup, W_)
            passes(pool, blocks, step, -2, 3)
            pool.wait_ge(scattered.sem, 16 * blocks)

        @block.scalar
        def _(act):
            act.wait_ge(consts, 16)
            act.wait_ge(setup, W_ + 1)
            nc.scalar.copy(BR[0:E, :], stage[:, :]).then_inc(split, 1)

            def step(it, u, there):
                if there(u):
                    act.wait_ge(up.sem, up.now(it, u))
                    if not among_first(it, u, 2):
                        act.wait_ge(h_t.sem, h_t.now(it, u - 2))
                    for c in range(2):
                        nc.scalar.activation(h[u % 2][:, c * HH:(c + 1) * HH], ps[:, 1 + c, 0:HH],
                                             ACT.Gelu).then_inc(gelu.sem, 1)
                m = u + 1
                if there(m):
                    act.wait_ge(x_t.sem, x_t.now(it, m))
                    if not among_first(it, m, 2):
                        act.wait_ge(up.sem, up.now(it, m - 2))
                    nc.scalar.copy(pk[m % 2][:, :, :], ps[:, 0, 0:3 * P].rearrange("p (a n) -> p a n", a=3)).then_inc(x_c.sem, 1)
                m = u - 1
                if there(m):
                    act.wait_ge(h_t.sem, h_t.now(it, m))
                    if not among_first(it, m, 2):
                        act.wait_ge(down.sem, down.now(it, m - 2))
                    nc.scalar.copy(hh[m % 2][:, :].rearrange("p (b n) -> p b n", b=2), ps[:, 3:5, 0:HH]).then_inc(h_h.sem, 1)

            passes(act, blocks, step, -1, 1)

        @block.vector
        def _(dve):
            for j in range(W_):
                nc.vector.memset(X[j][:, :].bitcast(F32), 0.0).then_inc(setup, 1)
            nc.vector.memset(BR[:, :].bitcast(F32), 0.0).then_inc(setup, 1)
            dve.wait_ge(split, 1)
            nc.vector.tensor_tensor(BR[32:32 + E, :], stage[:, :], BR[0:E, :].bitcast(F32), ALU.subtract
                                    ).then_inc(split, 1)

            def step(it, u, there):
                m = u - 1
                if there(m):
                    dve.wait_ge(h_h.sem, h_h.now(it, m))
                    nc.vector.tensor_tensor(hl[m % 2][:, :].rearrange("p (b n) -> p b n", b=2), ps[:, 3:5, 0:HH],
                                            hh[m % 2][:, :].rearrange("p (b n) -> p b n", b=2).bitcast(F32),
                                            ALU.subtract).then_inc(h_l.sem, 1)
                m = u - 2
                if there(m):
                    dve.wait_ge(down.sem, down.now(it, m))
                    dve.wait_ge(gathered[m % W_].sem, gathered[m % W_].now(it, m // W_))
                    if not among_first(it, m, 2):
                        dve.wait_ge(scattered.sem, scattered.now(it, m - 2))
                    nc.vector.tensor_tensor(y[m % 2][:, :], ps[:, 5, 0:D], X[m % W_][:, 2 * D:3 * D].bitcast(F32), ALU.add
                                            ).then_inc(summed.sem, 1)

            passes(dve, blocks, step, -1, 2)

        @block.tensor
        def _(pe):
            pe.wait_ge(identity, 3)
            pe.wait_ge(setup, W_ + 1)
            pe.wait_ge(split, 2)
            experts = BlockExperts(pe, pre, table, E)

            def step(it, u, there):
                if there(u):
                    if u % W_ == 0:
                        experts.load(it, u)
                    e = experts.of(u)
                    pe.wait_ge(x_c.sem, x_c.now(it, u))
                    if not among_first(it, u, 1):
                        pe.wait_ge(gelu.sem, gelu.now(it, u - 1))
                    for n, (a, hlw, part) in enumerate(((0, 0, 0), (0, 1, 0), (1, 0, 0), (2, 0, 1), (2, 1, 1))):
                        for c in range(2):
                            nc.tensor.matmul(ps[:, 1 + c, 0:HH], pk[u % 2][:, a, :],
                                             W1[:, hlw, part, bass.ds(e, 1), c * HH:(c + 1) * HH].rearrange("p a n -> p (a n)"),
                                             start=n == 0, stop=False, skip_group_check=True)
                    pe.wait_ge(picked.sem, picked.now(it, u))
                    for c in range(2):
                        last = nc.tensor.matmul(ps[:, 1 + c, 0:HH], pick[u % W_][:, :], BR[:, c * HH:(c + 1) * HH],
                                                start=False, stop=True, skip_group_check=True)
                    last.then_inc(up.sem, 1)
                m = u + 1
                if there(m):
                    pe.wait_ge(gathered[m % W_].sem, gathered[m % W_].now(it, m // W_))
                    if not among_first(it, m, 1):
                        pe.wait_ge(x_c.sem, x_c.now(it, m - 1))
                    for a in range(3):
                        last = nc.tensor.transpose(ps[:, 0, a * P:(a + 1) * P].bitcast(F32R),
                                                   X[m % W_][:, a * P:(a + 1) * P], ident_r[:, :])
                    last.then_inc(x_t.sem, 1)
                m = u - 1
                if there(m):
                    pe.wait_ge(gelu.sem, gelu.now(it, m))
                    if not among_first(it, m, 1):
                        pe.wait_ge(h_l.sem, h_l.now(it, m - 1))
                    for c in range(HC):
                        last = nc.tensor.transpose(ps[:, 3 + c // 3, (c % 3) * P:(c % 3 + 1) * P],
                                                   h[m % 2][:, c * P:(c + 1) * P], ident[:, :])
                    last.then_inc(h_t.sem, 1)
                m = u - 2
                if there(m):
                    pe.wait_ge(h_h.sem, h_h.now(it, m))
                    pe.wait_ge(h_l.sem, h_l.now(it, m))
                    if not among_first(it, m, 1):
                        pe.wait_ge(summed.sem, summed.now(it, m - 1))
                    e = experts.of(m)
                    for c in range(HC):
                        for n, (a, hlw) in enumerate(((hh, 0), (hh, 1), (hl, 0))):
                            nc.tensor.matmul(ps[:, 5, 0:D], a[m % 2][:, c * P:(c + 1) * P],
                                             W2[:, hlw, bass.ds(e, 1), c, :].rearrange("p a n -> p (a n)"),
                                             start=c == 0 and n == 0, stop=False, skip_group_check=True)
                    nc.tensor.matmul(ps[:, 5, 0:D], pick[m % W_][:, :], BR[:, HE:HE + D],
                                     start=False, stop=True, skip_group_check=True).then_inc(down.sem, 1)

            passes(pe, blocks, step, -1, 2)


KEYS = N + N // 2
KF = 4 * D
KFC = KF // P


def phase_c(nc, stack, io):
    with ExitStack() as ctx:
        sb = lambda n, shape, dt=F32: ctx.enter_context(nc.sbuf_tensor(f"c_sb_{n}", shape, dt))
        two = lambda n, shape, dt=F32: [sb(f"{n}{u}", shape, dt) for u in range(2)]
        sig = lambda n, per=1, step=1, ways=2, credit=False: Signal(nc, stack, f"c_{n}", per, ways, step, credit)
        dma = lambda n, credit=False: [sig(f"{n}{u}", 1, 16, 1, credit) for u in range(2)]
        ps = ctx.enter_context(nc.psum_tensor("c_ps", [P, 8, 512], F32))
        W = sb("W", [P, 2, 2, C_TOT], F32R)
        WV = sb("WV", [P, 2, KFC, D], F32R)
        rows = sb("rows", [P, len(C_ROW), D])
        decay, bonus = sb("decay", [P, KEYS]), sb("bonus", [P, KEYS])
        ident = sb("ident", [P, P])
        half = sb("half", [P, NG])
        flat = lambda ap: ap.rearrange("p a n -> p (a n)")
        split_weights(nc, stack, "cw", [
            (flat(io["c_w"]), flat(W[:, 0]), flat(W[:, 1])),
            (flat(io["c_wv"]), flat(WV[:, 0]), flat(WV[:, 1]))])
        slots = sb("slots", [P, (NT + 2) * NG * K_B], I32)
        gates = sb("gates", [P, (NT + 2) * NG * K_B])
        own_slots = [sb(f"ownslots{u}", [P, NG * K_B], I32) for u in range(2)]
        own_gates = two("owngates", [P, NG * K_B])
        pk = two("pk", [P, 3, N], F32R)
        hb, xb, nb = two("hb", [P, NG, D]), two("xb", [P, NG, D]), two("nb", [P, NG, D])
        kk, vv, er = two("kk", [P, KEYS]), two("vv", [P, KEYS]), two("er", [P, KEYS])
        ms, sa, sb_ = (two(n, [P, 2, KEYS + 1]) for n in ("ms", "sa", "sbb"))
        e1, e2 = two("e1", [P, 2, KEYS]), two("e2", [P, 2, KEYS])
        ye = [[e[u][:, d, r * D:(r + 1) * D] for e in (e1, e2) for d in range(2) for r in range(KEYS // D)] for u in range(2)]
        t1, t2 = two("t1", [P, KEYS]), two("t2", [P, KEYS])
        yh, yl = two("yh", [P, KEYS], F32R), two("yl", [P, KEYS], F32R)
        xs = [[(2 * c, (yh, yl)[c][u][:, :].rearrange("p (g n) -> p g n", g=2)) for c in range(2)] for u in range(2)]
        rl = [sb(f"rl{j}", [P, N]) for j in range(2)]
        fh = [sb(f"fh{j}", [P, N], F32R) for j in range(2)]
        fl = [sb(f"fl{j}", [P, N], F32R) for j in range(2)]
        st, mv = two("st", [P, NG, 6]), two("mv", [P, NG, 2])
        ra, rb, rs, rc = (two(n, [P, NG]) for n in ("ra", "rb", "rs", "rc"))
        router = Router(nc, stack, ctx, "cr", 4, 1)

        consts = stack.new("c_consts")
        identity = stack.new("c_identity")
        setup, cleared = (stack.new(n) for n in ("c_setup", "c_cleared"))
        loaded = dma("loaded")
        st_x = [sig(f"stx{u}", 2, 16, 1, True) for u in range(2)]
        st_mask, st_base = dma("stmask", True), dma("stbase", True)
        s1, m1, pl1, n3, l1, l1b = sig("s1", 4), sig("m1", 4), sig("pl1", 7), sig("n3", 4), sig("l1", 4), sig("l1b", 4)
        tr1, p1h, p1l = sig("tr1"), sig("p1h", 2), sig("p1l", 2)
        k_ps, v_ps, r_ps = sig("kps"), sig("vps"), sig("rps")
        k_up, v_up, r_up, kpad = sig("kup", 3), sig("vup", 3), sig("rup", 3), sig("kpad")
        mscan, x1a, x1b, x2, kb = sig("mscan", 2), sig("x1a", 2), sig("x1b", 2), sig("x2", 2), sig("kb")
        ex1, ex2, ev, ascan, bscan = sig("ex1", 2), sig("ex2", 2), sig("ev", 2), sig("ascan", 2), sig("bscan", 2)
        mm, df, exd, wa, wb, wv_ = sig("mm", 2), sig("df", 3), sig("exd", 3), sig("wa", 2), sig("wb", 2), sig("wv")
        nsum, dsum, den, dinv, yy, y_h, y_l = sig("nsum", 2), sig("dsum", 2), sig("den"), sig("dinv"), sig("yy"), sig("yh"), sig("yl")
        o_ps, x_up = sig("ops"), sig("xup")
        s2, m2, pl2, l2, l2b = sig("s2", 4), sig("m2", 4), sig("pl2", 2), sig("l2", 4), sig("l2b", 4)
        tr2, p2h, p2l = sig("tr2"), sig("p2h", 2), sig("p2l", 2)
        g_ps, g_ex, g_kv, x2_up, h_up = sig("gps"), sig("gex"), sig("gkv"), sig("x2up"), sig("hup")
        seq = lambda n: sig(n, ways=2 * KFC, credit=True)
        f_ps, f_relu, f_sq, f_h, f_l, f_used = (seq(n) for n in ("fps", "frelu", "fsq", "fh", "fl", "fused"))
        s3, m3, pl3, n4 = sig("s3", 4), sig("m3", 4), sig("pl3", 2), sig("n4", 4)
        tr3, p3h, p3l = sig("tr3"), sig("p3h", 2), sig("p3l", 2)
        gt, xh, xl = sig("gt"), sig("xh", 4), sig("xl", 4, credit=True)
        tabled, sliced = stack.new("c_tabled"), sig("sliced", 2)
        gathered = [sig(f"gathered{u}", 4 * NG, 16, 1) for u in range(2)]
        combined, added = sig("combined", K_B * NG), sig("added", 2)
        block = ctx.enter_context(nc.Block())
        row = lambda n: rows[:, C_ROW[n], :]
        w_at = lambda n, a=0, m=None: slice(C_AT[n][0] + a, C_AT[n][0] + a + (m or C_AT[n][1]))
        before = lambda x, d: x[:, d, 0:KEYS] if d == 0 else x[:, d, 1:KEYS + 1]
        after = lambda x, d: x[:, d, 1:KEYS + 1] if d == 0 else x[:, d, 0:KEYS]

        def scan(out, d0, d1, initial, op0, op1, d):
            if d == 1:
                out, d0, d1 = out[:, ::-1], d0[:, ::-1], d1[:, ::-1]
            return nc.vector.tensor_tensor_scan(out, d0, d1, initial, op0=op0, op1=op1)

        def two_banks(u, b0, n):
            return ps[:, 4 * u + b0:4 * u + b0 + 2, :].rearrange("p b (h n) -> p b h n", h=2)[:, :, :, 0:n]

        def split4(ap):
            return ap.rearrange("p (b h) n -> p b h n", b=2)

        def token_rows(tile):
            return io["rows_d"].rearrange("(t g p) d -> t p g d", g=NG, p=P)[tile]

        @block.sync
        def _(sp):
            sp.dma_start(slots[:, 0:GROUPS * K_B], io["slots_b"].rearrange("p g j -> p (g j)")).then_inc(tabled, 16)
            sp.dma_start(gates[:, 0:GROUPS * K_B], io["gates_b"].rearrange("p g j -> p (g j)")).then_inc(tabled, 16)
            sp.dma_start(rows[:, :, :], io["c_rows"]).then_inc(consts, 16)
            sp.dma_start(decay[:, :], io["c_decay"]).then_inc(consts, 16)
            sp.dma_start(bonus[:, :], io["c_bonus"]).then_inc(consts, 16)
            for s in (*st_base, *st_x, *st_mask):
                s.credit(sp)
            with sp.Fori(0, NT // 2) as it:
                for u in range(2):
                    sp.wait_ge(st_base[u].sem, st_base[u].last(it, 0))
                    sp.sem_inc(stack.passed, 1)
                    sp.dma_start(hb[u][:, :, :], io["base"][it * 2 + u]).then_inc(loaded[u].sem, 16)
                for u in range(2):
                    sp.wait_ge(h_up.sem, h_up.now(it, u))
                    sp.sem_inc(stack.passed, 1)
                    sp.dma_start(token_rows(it * 2 + u)[:, :, 2 * D:3 * D], hb[u][:, :, :]).then_inc(st_base[u].sem, 16)
                for u in range(2):
                    sp.wait_ge(xl.sem, xl.now(it, u))
                    sp.sem_inc(stack.passed, 1)
                    for g, part in xs[u]:
                        sp.dma_start(token_rows(it * 2 + u)[:, g:g + 2, 0:2 * D], part.bitcast(F32)).then_inc(st_x[u].sem, 16)
                for u in range(2):
                    sp.wait_ge(router.gates.sem, router.gates.now(it, u))
                    sp.sem_inc(stack.passed, 1)
                    sp.dma_start(io["mask_d"].rearrange("p (t g) e -> t p g e", g=NG)[it * 2 + u],
                                 router.fw[u][:, :, 0:4]).then_inc(st_mask[u].sem, 16)
            for u in range(2):
                for s in (st_base, st_x, st_mask):
                    sp.wait_ge(s[u].sem, s[u].now(NT // 2 - 1, 0))
                    sp.sem_inc(stack.passed, 1)

        @block.gpsimd
        def _(pool):
            fill_identity(nc, pool, ident, identity)
            nc.gpsimd.memset(half[:, :], -0.5).then_inc(setup, 1)
            pool.wait_ge(setup, 1)

            def power(out, x, s):
                nc.gpsimd.tensor_tensor(out[:, :], x[:, :], half[:, :], ALU.pow).then_inc(s.sem, 1)

            def gather(it, u):
                at = bass.ds((it * 2 + u) * (NG * K_B), NG * K_B)
                nc.gpsimd.tensor_copy(own_slots[u][:, :], slots[:, at]).then_inc(sliced.sem, 1)
                nc.gpsimd.tensor_copy(own_gates[u][:, :], gates[:, at]).then_inc(sliced.sem, 1)
                pool.wait_ge(sliced.sem, sliced.now(it, u))
                pool.sem_inc(stack.passed, 1)
                for r in range(NG * K_B):
                    nc.gpsimd.indirect_dma_start(ye[u][r], None, io["slot_rows"],
                                                 bass.IndirectOffsetOnAxis(own_slots[u][:, r:r + 1], 0),
                                                 bounds_check=P * BLK_B - 1, oob_is_err=False
                                                 ).then_inc(gathered[u].sem, 16)

            xl.credit(pool)
            nc.gpsimd.memset(slots[:, GROUPS * K_B:], 0).then_inc(setup, 1)
            nc.gpsimd.memset(gates[:, GROUPS * K_B:], 0.0).then_inc(setup, 1)
            pool.wait_ge(setup, 3)
            pool.wait_ge(tabled, 32)
            for u in range(2):
                gather(0, u)

            with pool.Fori(0, NT // 2) as it:
                for u in range(2):
                    var = mv[u][:, :, 1]
                    pool.wait_ge(m1.sem, m1.now(it, u))
                    pool.sem_inc(stack.passed, 1)
                    nc.gpsimd.tensor_scalar(ra[u][:, :], var, EPS, None, ALU.add).then_inc(pl1.sem, 1)
                    pool.wait_ge(pl1.sem, pl1.now(it, u, 1))
                    power(rs[u], ra[u], pl1)
                    pool.wait_ge(pl1.sem, pl1.now(it, u, 2))
                    nc.gpsimd.tensor_tensor(rb[u][:, :], rs[u][:, :], rs[u][:, :], ALU.mult).then_inc(pl1.sem, 1)
                    pool.wait_ge(pl1.sem, pl1.now(it, u, 3))
                    nc.gpsimd.tensor_tensor(rb[u][:, :], rb[u][:, :], var, ALU.mult).then_inc(pl1.sem, 1)
                    pool.wait_ge(pl1.sem, pl1.now(it, u, 4))
                    pool.sem_inc(stack.passed, 1)
                    nc.gpsimd.tensor_scalar(rb[u][:, :], rb[u][:, :], EPS, None, ALU.add).then_inc(pl1.sem, 1)
                    pool.wait_ge(pl1.sem, pl1.now(it, u, 5))
                    power(ra[u], rb[u], pl1)
                    pool.wait_ge(pl1.sem, pl1.now(it, u, 6))
                    nc.gpsimd.tensor_tensor(rc[u][:, :], rs[u][:, :], ra[u][:, :], ALU.mult).then_inc(pl1.sem, 1)
                for u in range(2):
                    pool.wait_ge(kpad.sem, kpad.now(it, u))
                    for d in range(2):
                        pool.wait_ge(mscan.sem, mscan.now(it, u, d + 1))
                        nc.gpsimd.tensor_tensor(e2[u][:, d, :], kk[u][:, :], after(ms[u], d), ALU.subtract).then_inc(x2.sem, 1)
                for u in range(2):
                    pool.wait_ge(ev.sem, ev.now(it, u, 2))
                    pool.wait_ge(ascan.sem, ascan.now(it, u, 2))
                    nc.gpsimd.tensor_tensor(t1[u][:, :], kk[u][:, :], bonus[:, :], ALU.add).then_inc(kb.sem, 1)

                def denominator(u):
                    for d in range(2):
                        pool.wait_ge(exd.sem, exd.now(it, u, d + 1))
                        pool.wait_ge(bscan.sem, bscan.now(it, u, d + 1))
                        x = before(sb_[u], d)
                        nc.gpsimd.tensor_tensor(x, x, e1[u][:, d, :], ALU.mult).then_inc(wb.sem, 1)
                    pool.wait_ge(wb.sem, wb.now(it, u, 2))
                    nc.gpsimd.tensor_tensor(e2[u][:, 0, :], before(sb_[u], 1), before(sb_[u], 0), ALU.add).then_inc(dsum.sem, 1)
                    pool.wait_ge(dsum.sem, dsum.now(it, u, 1))
                    pool.wait_ge(exd.sem, exd.now(it, u, 3))
                    nc.gpsimd.tensor_tensor(e2[u][:, 0, :], e2[u][:, 0, :], t1[u][:, :], ALU.add).then_inc(dsum.sem, 1)

                def rstd(u, m, pl):
                    pool.wait_ge(m.sem, m.now(it, u))
                    pool.sem_inc(stack.passed, 1)
                    nc.gpsimd.tensor_scalar(ra[u][:, :], mv[u][:, :, 1], EPS, None, ALU.add).then_inc(pl.sem, 1)
                    pool.wait_ge(pl.sem, pl.now(it, u, 1))
                    power(rs[u], ra[u], pl)

                denominator(0)
                rstd(0, m2, pl2)
                denominator(1)
                rstd(1, m2, pl2)
                for u in range(2):
                    pool.wait_ge(added.sem, added.now(it, u))
                    pool.sem_inc(stack.passed, 1)
                    gather(it + 1, u)
                for u in range(2):
                    rstd(u, m3, pl3)
                for u in range(2):
                    pool.wait_ge(xh.sem, xh.now(it, u))
                    row_lows(nc, nb[u], xs[u], xl)
            for u in range(2):
                pool.wait_ge(gathered[u].sem, gathered[u].now(NT // 2, 0))

        @block.vector
        def _(dve):
            dve.wait_ge(consts, 48)
            router.start(dve)
            live = lambda x: x[:, :].rearrange("p (b s) -> p b s", s=TP)[:, :, 0:T]
            nc.vector.tensor_scalar(live(decay), live(decay), 1.0 / T, None, ALU.mult).then_inc(cleared, 1)
            nc.vector.tensor_scalar(live(bonus), live(bonus), 1.0 / T, None, ALU.mult).then_inc(cleared, 1)
            for u in range(2):
                for x, v in ((ms, NEG), (sa, 0.0), (sb_, 0.0)):
                    nc.vector.memset(x[u][:, 0, 0:1], v).then_inc(cleared, 1)
                    nc.vector.memset(x[u][:, 1, KEYS:KEYS + 1], v).then_inc(cleared, 1)
            dve.wait_ge(setup, 1)
            dve.wait_ge(cleared, 14)
            for s in (f_sq, f_l):
                s.credit(dve)
            TT = nc.vector.tensor_tensor

            def combine(it, u, choices=range(K_B)):
                dve.wait_ge(gathered[u].sem, gathered[u].now(it, 0))
                dve.wait_ge(sliced.sem, sliced.now(it, u))
                for j in choices:
                    for g in range(NG):
                        first, r = g * K_B, g * K_B + j
                        gate_of = own_gates[u][:, r:r + 1]
                        if j == 0:
                            nc.vector.tensor_scalar(ye[u][first], ye[u][first], gate_of, None, ALU.mult).then_inc(combined.sem, 1)
                        else:
                            dve.wait_ge(combined.sem, combined.now(it, u, (j - 1) * NG + g + 1))
                            nc.vector.scalar_tensor_tensor(ye[u][first], ye[u][r], gate_of, ye[u][first],
                                                           ALU.mult, ALU.add).then_inc(combined.sem, 1)

            for u in range(2):
                combine(0, u)
            with dve.Fori(0, NT // 2) as it:
                for u in range(2):
                    dve.wait_ge(loaded[u].sem, loaded[u].now(it, 0))
                    dve.wait_ge(combined.sem, combined.now(it, u))
                    for c, e in enumerate((e1, e2)):
                        TT(hb[u][:, 2 * c:2 * c + 2, :], e[u][:, :, 0:D], hb[u][:, 2 * c:2 * c + 2, :], ALU.add
                           ).then_inc(added.sem, 1)
                for u in range(2):
                    dve.wait_ge(added.sem, added.now(it, u))
                    norm_stats(nc, stack, dve, hb[u], st[u], mv[u], s1, m1, it, u)
                for u in range(2):
                    dve.wait_ge(xl.sem, xl.last(it, u))
                    norm_center(nc, dve, stack, nb[u], hb[u], mv[u], row("ln1w"), m1, l1, it, u)
                for u in range(2):
                    dve.wait_ge(l1.sem, l1.now(it, u))
                    dve.wait_ge(pl1.sem, pl1.now(it, u))
                    norm_finish(nc, nb[u], nb[u], rc[u], row("ln1b"), l1b)
                for u in range(2):
                    norm_apply(nc, xb[u], hb[u], mv[u], rs[u], n3)
                for u in range(2):
                    dve.wait_ge(tr1.sem, tr1.now(it, u))
                    pack_low(nc, dve, ps, 4 * u, pk[u], p1h, p1l, it, u)
                for u in range(2):
                    dve.wait_ge(k_up.sem, k_up.now(it, u))
                    nc.vector.memset(kk[u][:, :].rearrange("p (b s) -> p b s", s=TP)[:, :, T:TP], NEG).then_inc(kpad.sem, 1)
                def maxima(u):
                    dve.wait_ge(kpad.sem, kpad.now(it, u))
                    for d in range(2):
                        scan(after(ms[u], d), decay[:, :], kk[u][:, :], NEG, ALU.add, ALU.max, d).then_inc(mscan.sem, 1)

                def decays(u):
                    for d in range(2):
                        dve.wait_ge(mscan.sem, mscan.now(it, u, d + 1))
                        TT(e1[u][:, d, :], before(ms[u], d), decay[:, :], ALU.add).then_inc(x1a.sem, 1)
                    for d in range(2):
                        dve.wait_ge(x1a.sem, x1a.now(it, u, d + 1))
                        TT(e1[u][:, d, :], e1[u][:, d, :], after(ms[u], d), ALU.subtract).then_inc(x1b.sem, 1)

                def states(u):
                    for d in range(2):
                        dve.wait_ge(ex1.sem, ex1.now(it, u, d + 1))
                        dve.wait_ge(ex2.sem, ex2.now(it, u, d + 1))
                        scan(after(sb_[u], d), e1[u][:, d, :], e2[u][:, d, :], 0.0, ALU.mult, ALU.add, d).then_inc(bscan.sem, 1)
                        dve.wait_ge(v_up.sem, v_up.now(it, u))
                        if d == 1:
                            dve.wait_ge(ascan.sem, ascan.now(it, u, 1))
                        TT(t1[u][:, :], e2[u][:, d, :], vv[u][:, :], ALU.mult).then_inc(ev.sem, 1)
                        dve.wait_ge(ev.sem, ev.now(it, u, d + 1))
                        scan(after(sa[u], d), e1[u][:, d, :], t1[u][:, :], 0.0, ALU.mult, ALU.add, d).then_inc(ascan.sem, 1)

                def shares(u):
                    TT(t2[u][:, :], before(ms[u], 0), before(ms[u], 1), ALU.max).then_inc(mm.sem, 1)
                    dve.wait_ge(kb.sem, kb.now(it, u))
                    dve.wait_ge(mm.sem, mm.now(it, u, 1))
                    TT(t2[u][:, :], t2[u][:, :], t1[u][:, :], ALU.max).then_inc(mm.sem, 1)
                    dve.wait_ge(mm.sem, mm.now(it, u, 2))
                    dve.wait_ge(ascan.sem, ascan.now(it, u))
                    dve.wait_ge(bscan.sem, bscan.now(it, u))
                    for d in range(2):
                        TT(e1[u][:, d, :], before(ms[u], d), t2[u][:, :], ALU.subtract).then_inc(df.sem, 1)
                    TT(t1[u][:, :], t1[u][:, :], t2[u][:, :], ALU.subtract).then_inc(df.sem, 1)

                def numerator(u):
                    for d in range(2):
                        dve.wait_ge(exd.sem, exd.now(it, u, d + 1))
                        TT(before(sa[u], d), before(sa[u], d), e1[u][:, d, :], ALU.mult).then_inc(wa.sem, 1)
                    dve.wait_ge(exd.sem, exd.now(it, u, 3))
                    TT(vv[u][:, :], vv[u][:, :], t1[u][:, :], ALU.mult).then_inc(wv_.sem, 1)
                    for d in range(2):
                        dve.wait_ge(wa.sem, wa.now(it, u, d + 1))
                        if d == 0:
                            dve.wait_ge(wv_.sem, wv_.now(it, u))
                        else:
                            dve.wait_ge(nsum.sem, nsum.now(it, u, 1))
                        TT(vv[u][:, :], vv[u][:, :], before(sa[u], d), ALU.add).then_inc(nsum.sem, 1)

                def output(u):
                    dve.wait_ge(dsum.sem, dsum.now(it, u))
                    dve.wait_ge(r_up.sem, r_up.now(it, u))
                    nc.vector.scalar_tensor_tensor(t2[u][:, :], er[u][:, :], 1.0, e2[u][:, 0, :], ALU.add, ALU.mult).then_inc(den.sem, 1)
                    dve.wait_ge(den.sem, den.now(it, u))
                    nc.vector.reciprocal(t2[u][:, :], t2[u][:, :]).then_inc(dinv.sem, 1)
                    dve.wait_ge(dinv.sem, dinv.now(it, u))
                    dve.wait_ge(nsum.sem, nsum.now(it, u))
                    TT(t1[u][:, :], vv[u][:, :], t2[u][:, :], ALU.mult).then_inc(yy.sem, 1)

                def output_low(u):
                    dve.wait_ge(y_h.sem, y_h.now(it, u))
                    TT(yl[u][:, :], t1[u][:, :], yh[u][:, :].bitcast(F32), ALU.subtract).then_inc(y_l.sem, 1)

                def residual(u):
                    dve.wait_ge(o_ps.sem, o_ps.now(it, u))
                    dve.wait_ge(n3.sem, n3.now(it, u))
                    TT(split4(xb[u][:, :, :]), two_banks(u, 0, D), split4(xb[u][:, :, :]), ALU.add).then_inc(x_up.sem, 1)

                def stats2(u):
                    dve.wait_ge(x_up.sem, x_up.now(it, u))
                    norm_stats(nc, stack, dve, xb[u], st[u], mv[u], s2, m2, it, u)

                def center2(u):
                    norm_center(nc, dve, stack, nb[u], xb[u], mv[u], row("ln2w"), m2, l2, it, u)

                def finish2(u):
                    dve.wait_ge(l2.sem, l2.now(it, u))
                    dve.wait_ge(pl2.sem, pl2.now(it, u))
                    norm_finish(nc, nb[u], nb[u], rs[u], row("ln2b"), l2b)

                def low2(u):
                    dve.wait_ge(tr2.sem, tr2.now(it, u))
                    pack_low(nc, dve, ps, 4 * u + 2, pk[u], p2h, p2l, it, u)

                for stage, u in ((maxima, 0), (decays, 0), (maxima, 1), (decays, 1), (states, 0),
                                 (states, 1), (shares, 0), (numerator, 0), (shares, 1), (output, 0),
                                 (output_low, 0), (numerator, 1), (residual, 0), (stats2, 0), (center2, 0),
                                 (finish2, 0), (low2, 0), (output, 1), (output_low, 1)):
                    stage(u)
                between = {2: (residual, stats2, center2), 3: (finish2,), 4: (low2,)}
                for k in range(2 * KFC + 1):
                    for stage in between.get(k, ()):
                        stage(1)
                    if k < 2 * KFC:
                        dve.wait_ge(f_relu.sem, f_relu.now(it, k))
                        TT(rl[k % 2][:, :], rl[k % 2][:, :], rl[k % 2][:, :], ALU.mult).then_inc(f_sq.sem, 1)
                    if k >= 1:
                        j = k - 1
                        dve.wait_ge(f_h.sem, f_h.now(it, j))
                        TT(fl[j % 2][:, :], rl[j % 2][:, :], fh[j % 2][:, :].bitcast(F32), ALU.subtract).then_inc(f_l.sem, 1)
                    if 8 <= k < 8 + K_B:
                        combine(it + 1, 0, (k - 8,))
                for u in range(2):
                    dve.wait_ge(f_used.sem, f_used.now(it, u * KFC + KFC - 1))
                    dve.wait_ge(g_ex.sem, g_ex.now(it, u))
                    TT(split4(nb[u][:, :, :]), two_banks(u, 0, D), split4(nb[u][:, :, :]), ALU.mult).then_inc(g_kv.sem, 1)
                    dve.wait_ge(g_kv.sem, g_kv.now(it, u))
                    TT(xb[u][:, :, :], xb[u][:, :, :], nb[u][:, :, :], ALU.add).then_inc(x2_up.sem, 1)
                    dve.wait_ge(x2_up.sem, x2_up.now(it, u))
                    TT(hb[u][:, :, :], hb[u][:, :, :], xb[u][:, :, :], ALU.add).then_inc(h_up.sem, 1)
                for u in range(2):
                    dve.wait_ge(h_up.sem, h_up.now(it, u))
                    norm_stats(nc, stack, dve, hb[u], st[u], mv[u], s3, m3, it, u)
                for u in range(2):
                    dve.wait_ge(pl3.sem, pl3.now(it, u))
                    norm_apply(nc, nb[u], hb[u], mv[u], rs[u], n4)
                for u in range(2):
                    dve.wait_ge(tr3.sem, tr3.now(it, u))
                    pack_low(nc, dve, ps, 4 * u + 2, pk[u], p3h, p3l, it, u)
                combine(it + 1, 1)
                for u in range(2):
                    dve.wait_ge(gt.sem, gt.now(it, u))
                    dve.wait_ge(st_mask[u].sem, st_mask[u].last(it, 0))
                    router.choose(dve, ps[:, 4 * u, 0:NG * 16].rearrange("p (g e) -> p g e", g=NG)[:, :, 0:4], row("gateb"), it, u)

        @block.scalar
        def _(act):
            act.wait_ge(consts, 48)
            act.wait_ge(cleared, 14)
            for s in (f_relu, f_h):
                s.credit(act)

            def unfold(u, bank, out, sg, func=ACT.Copy, scale=1.0):
                h = N // 2
                for o, i in ((out[:, 0:N], ps[:, bank, :]), (out[0:D2, N:KEYS], ps[0:D2, bank + 1, 0:h]),
                             (out[D2:P, N:KEYS], ps[D2:P, bank + 1, h:N])):
                    nc.scalar.activation(o, i, func, scale=scale).then_inc(sg.sem, 1)

            with act.Fori(0, NT // 2) as it:
                for u in range(2):
                    act.wait_ge(tr1.sem, tr1.now(it, u))
                    pack_high(nc, ps, 4 * u, pk[u], p1h)
                for u in range(2):
                    act.wait_ge(k_ps.sem, k_ps.now(it, u))
                    unfold(u, 4 * u + 2, kk[u], k_up)
                for u in range(2):
                    act.wait_ge(v_ps.sem, v_ps.now(it, u))
                    unfold(u, 4 * u, vv[u], v_up)
                for u in range(2):
                    act.wait_ge(r_ps.sem, r_ps.now(it, u))
                    unfold(u, 4 * u + 2, er[u], r_up, ACT.Exp, -1.0)
                for u in range(2):
                    for d in range(2):
                        act.wait_ge(x2.sem, x2.now(it, u, d + 1))
                        nc.scalar.activation(e2[u][:, d, :], e2[u][:, d, :], ACT.Exp).then_inc(ex2.sem, 1)
                        act.wait_ge(x1b.sem, x1b.now(it, u, d + 1))
                        nc.scalar.activation(e1[u][:, d, :], e1[u][:, d, :], ACT.Exp).then_inc(ex1.sem, 1)

                def shares(u):
                    for d in range(2):
                        act.wait_ge(df.sem, df.now(it, u, d + 1))
                        nc.scalar.activation(e1[u][:, d, :], e1[u][:, d, :], ACT.Exp).then_inc(exd.sem, 1)
                    act.wait_ge(df.sem, df.now(it, u, 3))
                    nc.scalar.activation(t1[u][:, :], t1[u][:, :], ACT.Exp).then_inc(exd.sem, 1)

                def output_high(u):
                    act.wait_ge(yy.sem, yy.now(it, u))
                    act.wait_ge(st_x[u].sem, st_x[u].last(it, 0))
                    nc.scalar.copy(yh[u][:, :], t1[u][:, :]).then_inc(y_h.sem, 1)

                def high2(u):
                    act.wait_ge(tr2.sem, tr2.now(it, u))
                    pack_high(nc, ps, 4 * u + 2, pk[u], p2h)

                def receptance(u):
                    act.wait_ge(g_ps.sem, g_ps.now(it, u))
                    nc.scalar.activation(split4(nb[u][:, :, :]), two_banks(u, 0, D), ACT.Sigmoid).then_inc(g_ex.sem, 1)

                for stage, u in ((shares, 0), (output_high, 0), (shares, 1), (high2, 0), (output_high, 1), (receptance, 0)):
                    stage(u)
                between = {4: high2, KFC: receptance}
                for k in range(2 * KFC + 1):
                    if k in between:
                        between[k](1)
                    if k < 2 * KFC:
                        act.wait_ge(f_ps.sem, f_ps.now(it, k))
                        act.wait_ge(f_l.sem, f_l.back(it, k - 2))
                        u = k // KFC
                        nc.scalar.activation(rl[k % 2][:, :], ps[:, 4 * u + 2 + k % 2, :], ACT.Relu).then_inc(f_relu.sem, 1)
                    if k >= 1:
                        j = k - 1
                        act.wait_ge(f_sq.sem, f_sq.now(it, j))
                        act.wait_ge(f_used.sem, f_used.back(it, j - 2))
                        nc.scalar.copy(fh[j % 2][:, :], rl[j % 2][:, :]).then_inc(f_h.sem, 1)
                for u in range(2):
                    act.wait_ge(tr3.sem, tr3.now(it, u))
                    pack_high(nc, ps, 4 * u + 2, pk[u], p3h)
                for u in range(2):
                    row_highs(nc, nb[u], xs[u], xh)

        @block.tensor
        def _(pe):
            pe.wait_ge(identity, 2)
            pe.wait_ge(cleared, 14)
            for s in (f_ps, f_used):
                s.credit(pe)

            def feature_major(u, b0, name, sg):
                for c in range(2):
                    last = product5(nc, ps[:, 4 * u + b0 + c, :], pk[u], slice(0, N), W, w_at(name, c * P, P), True, True, True)
                last.then_inc(sg.sem, 1)

            with pe.Fori(0, NT // 2) as it:
                for u in range(2):
                    pe.wait_ge(l1b.sem, l1b.now(it, u))
                    transpose_tile(nc, ps, 4 * u, nb[u], ident, tr1)
                for u in range(2):
                    pe.wait_ge(p1h.sem, p1h.now(it, u))
                    pe.wait_ge(p1l.sem, p1l.now(it, u))
                    feature_major(u, 2, "wk", k_ps)
                for u in range(2):
                    feature_major(u, 0, "wv", v_ps)
                for u in range(2):
                    pe.wait_ge(k_up.sem, k_up.now(it, u))
                    feature_major(u, 2, "wr", r_ps)
                def project(u):
                    pe.wait_ge(y_h.sem, y_h.now(it, u))
                    pe.wait_ge(y_l.sem, y_l.now(it, u))
                    for g in range(NG):
                        out = ps[:, 4 * u + g // 2, (g % 2) * 256:(g % 2) * 256 + D]
                        tok = slice(g * P, (g + 1) * P)
                        r = slice(D2 * (g // 2), D2 * (g // 2) + D2)
                        tail = slice(N + (g % 2) * P, N + (g % 2 + 1) * P)
                        w = w_at("wo")
                        steps = [(yh[u][:, tok], W[:, 0, 0, w]), (yh[u][:, tok], W[:, 1, 0, w]), (yl[u][:, tok], W[:, 0, 0, w]),
                                 (yh[u][r, tail], W[r, 0, 1, w]), (yh[u][r, tail], W[r, 1, 1, w]), (yl[u][r, tail], W[r, 0, 1, w])]
                        for n, (a, b) in enumerate(steps):
                            last = nc.tensor.matmul(out, a, b, start=n == 0, stop=n == 5)
                    last.then_inc(o_ps.sem, 1)

                def turn2(u):
                    pe.wait_ge(l2b.sem, l2b.now(it, u))
                    pe.wait_ge(r_up.sem, r_up.now(it, u))
                    transpose_tile(nc, ps, 4 * u + 2, nb[u], ident, tr2)

                def gate2(u):
                    pe.wait_ge(p2h.sem, p2h.now(it, u))
                    pe.wait_ge(p2l.sem, p2l.now(it, u))
                    for g in range(NG):
                        last = product5(nc, ps[:, 4 * u + g // 2, (g % 2) * 256:(g % 2) * 256 + D], pk[u],
                                        slice(g * P, (g + 1) * P), W, w_at("rf"), False, True, True)
                    last.then_inc(g_ps.sem, 1)

                project(0)
                turn2(0)
                gate2(0)
                between = {2: project, 4: turn2, 5: gate2}

                def hidden(k):
                    u, c = divmod(k, KFC)
                    pe.wait_ge(f_relu.sem, f_relu.back(it, k - 2))
                    product5(nc, ps[:, 4 * u + 2 + k % 2, :], pk[u], slice(0, N), W,
                             w_at("kf", c * P, P), True, True, True).then_inc(f_ps.sem, 1)

                def values(k):
                    u, c = divmod(k, KFC)
                    if c == 0:
                        pe.wait_ge(g_ex.sem, g_ex.now(it, u))
                    pe.wait_ge(f_h.sem, f_h.now(it, k))
                    pe.wait_ge(f_l.sem, f_l.now(it, k))
                    for g in range(NG):
                        tok = slice(g * P, (g + 1) * P)
                        out = ps[:, 4 * u + g // 2, (g % 2) * 256:(g % 2) * 256 + D]
                        for n, (a, hlw) in enumerate(((fh, 0), (fh, 1), (fl, 0))):
                            last = nc.tensor.matmul(out, a[k % 2][:, tok], WV[:, hlw, c, :],
                                                    start=c == 0 and n == 0 and g % 2 == 0, stop=c == KFC - 1 and n == 2,
                                                    skip_group_check=True)
                    last.then_inc(f_used.sem, 1)

                for k in range(2 * KFC + 2):
                    if k in between:
                        between[k](1)
                    if k < 2 * KFC:
                        hidden(k)
                    if k >= 2:
                        values(k - 2)
                for u in range(2):
                    pe.wait_ge(n4.sem, n4.now(it, u))
                    transpose_tile(nc, ps, 4 * u + 2, nb[u], ident, tr3)
                for u in range(2):
                    pe.wait_ge(p3h.sem, p3h.now(it, u))
                    pe.wait_ge(p3l.sem, p3l.now(it, u))
                    for g in range(NG):
                        last = product5(nc, ps[:, 4 * u, g * 16:(g + 1) * 16], pk[u],
                                        slice(g * P, (g + 1) * P), W, w_at("gate"), False, True, True)
                    last.then_inc(gt.sem, 1)


def build(nc, io):
    phases = (
        lambda stack: phase_a(nc, stack, io),
        lambda stack: first_experts(nc, stack, io),
        lambda stack: phase_c(nc, stack, io),
        lambda stack: last_experts(nc, stack, io),
    )
    for n, phase in enumerate(phases):
        stack = Semaphores(nc, n)
        phase(stack)
        stack.end()



SPECTRUM = list(range(KC)) + [D - j for j in range(1, KC - 1)]


def _parts(w):
    w = np.asarray(w)
    return np.stack([w[:P], np.concatenate([w[P:], w[P:]])], axis=1)


def _outs(w):
    return np.concatenate([w, w[:, P:]], axis=1)


def _twice(v):
    return np.concatenate([v[P:], v[P:]])


def _shape_constants():
    d, k = np.arange(D)[:, None], np.arange(KC)[None]
    ang = 2 * np.pi * ((d * k) % D) / D
    fft = np.zeros((D, 2 * KP))
    fft[:, :KC], fft[:, KP:KP + KC] = np.cos(ang), np.sin(ang)
    fft[:, KP], fft[:, KP + KC - 1] = 0, 0
    t = np.arange(T)
    ang = 2 * np.pi * ((t[:, None] * t[None]) % T) / T
    dft_t = np.zeros((2, TP, 2, 2, TP))
    for b in range(2):
        dft_t[b, :T, 0, b, :T] = np.cos(ang)
        dft_t[b, :T, 1, b, :T] = np.sin(ang)
    keys, queries = np.arange(TP)[None], np.arange(TP)[:, None]
    seen = np.where((keys <= queries) & (keys < T), 0.0, MASKED)
    return fft.astype(np.float32), dft_t.reshape(P, 2 * P).astype(np.float32), np.tile(seen, (2, 2)).astype(np.float32)


def _layout_a(i):
    fft, dft_t, mask = _shape_constants()
    f = np.float32
    x = np.zeros((D, B, CONV_T + 2 * HALO), f)
    x[:, :, HALO:HALO + S] = i["x"].transpose(2, 0, 1)
    x = x.reshape(D, NT, NB, -1)
    h = NB // 2
    tail = np.concatenate([x[P:, :, :h], x[P:, :, h:]], axis=0)
    xt = np.zeros((NT + 2, P, NB + NB // 2, CONV_T + 2 * HALO), f)
    xt[:NT] = np.concatenate([x[:P], tail], axis=2).transpose(1, 0, 2, 3)
    wa, ba = i["L0_attn_w_attn"][SPECTRUM], i["L0_attn_b_attn"]
    wq, wk, wv = wa[:, :D], wa[:, D:2 * D], wa[:, 2 * D:]
    w = np.concatenate([_outs(np.ascontiguousarray(i["L0_tok_w_pw"][:, :, 0].T)), fft, _outs(wq), _outs(wk), wv,
                        i["L0_attn_w_proj"][:, SPECTRUM], i["L0_ffn_gate_w"].T[SPECTRUM]], axis=1)
    cols = np.zeros((P, len(A_COL)), f)
    dw = i["L0_tok_w_dw"][:, 0, :]
    put = lambda n, v: cols.__setitem__((slice(None), A_COL[n]), v)
    for j in range(TAPS):
        put(f"tap{j}a", dw[:P, j])
        put(f"tap{j}b", _twice(dw[:, j]))
    for n, v in (("bdw", i["L0_tok_b_dw"]), ("bpw", i["L0_tok_b_pw"]), ("bq", ba[:D])):
        put(n + "a", v[:P])
        put(n + "b", _twice(v))
    par = (np.arange(P) // HD) % 2
    bk = ba[D:2 * D]
    for n, p in (("e", 0), ("o", 1)):
        own = par == p
        cols[own, A_COL[f"bk{n}a"]] = bk[:P][own]
        cols[own, A_COL[f"bk{n}b"]] = _twice(bk)[own]
    cols[par == 0, A_COL["even"]] = 1
    cols[par == 1, A_COL["odd"]] = 1
    rows = np.zeros((P, len(A_ROW), D), f)
    sp = lambda n: i[n][SPECTRUM]
    for n, v in (("gamma", sp("L0_tok_gamma")), ("beta", sp("L0_tok_beta")), ("bv", ba[2 * D:]),
                 ("bproj", sp("L0_attn_b_proj")), ("scale", sp("L0_ffn_scale")), ("gateb", i["L0_ffn_gate_b"])):
        rows[:, A_ROW[n], :len(v)] = v
    return {"x": xt, "a_w": _parts(w), "dft_t": dft_t, "a_cols": cols, "a_rows": rows, "a_mask": mask}


def _layout_b(i):
    w1, b1, w2, b2 = i["L0_ffn_w1"][:, SPECTRUM], i["L0_ffn_b1"], i["L0_ffn_w2"][:, :, SPECTRUM], i["L0_ffn_b2"][:, SPECTRUM]
    return {"b_w1": _parts(w1.transpose(1, 0, 2).reshape(D, -1)), "b_w2": _parts(w2.transpose(1, 0, 2).reshape(D, -1)),
            "b_bias": np.concatenate([b1, b2], axis=1)}


def _layout_d(i):
    w1, b1, w2 = i["L1_ffn_W1"][:, SPECTRUM], i["L1_ffn_b1"], i["L1_ffn_W2"][:, :, SPECTRUM]
    e = w1.shape[0]
    bias = np.concatenate([b1, i["L1_ffn_b2"][:, SPECTRUM]], axis=1)
    return {"d_w1": _parts(w1.transpose(1, 0, 2).reshape(D, HID)),
            "d_w2": w2.reshape(HID // P, P, D).transpose(1, 0, 2), "d_bias": bias}


def _layout_routing(i):
    p = np.arange(P)
    token = (p % TP < T).astype(np.float32)
    tri = np.stack([(p[:, None] < p[None]), np.ones((P, P))], axis=1).astype(np.float32)
    per_row = lambda v: np.tile(np.asarray(v, np.float32), (P, 1))
    return {"rt_tri": tri, "rt_pad": np.stack([token, (1 - token) * np.float32(NOWHERE), (p % 32).astype(np.float32)], axis=1),
            "rt_steps": per_row(np.arange(GROUPS) * P), "rt_order": per_row(np.arange(512)),
            "rt_number": (1 + np.arange(GROUPS)[None] % (GROUPS // 2) * P + p[:, None]).astype(np.float32)}


def _layout_c(i):
    f = np.float32
    t = lambda n: i[n].T
    gate = np.zeros((D, 16), f)
    gate[:, :4] = i["L1_ffn_Wg"][SPECTRUM]
    w = np.concatenate([_outs(t("L1_attn_Wk_a")[SPECTRUM]), _outs(t("L1_attn_Wv_a")[SPECTRUM]), _outs(t("L1_attn_Wr_a")[SPECTRUM]),
                        t("L1_attn_Wo_a")[:, SPECTRUM], t("L1_attn_Wr_f")[SPECTRUM][:, SPECTRUM],
                        t("L1_attn_Wk_f")[SPECTRUM], gate], axis=1)
    wv = t("L1_attn_Wv_f")[:, SPECTRUM].reshape(KFC, P, D).transpose(1, 0, 2)
    rows = np.zeros((P, len(C_ROW), D), f)
    for n, v in (("ln1w", i["L1_attn_ln1_w"][SPECTRUM]), ("ln1b", i["L1_attn_ln1_b"][SPECTRUM]),
                 ("ln2w", i["L1_attn_ln2_w"][SPECTRUM]), ("ln2b", i["L1_attn_ln2_b"][SPECTRUM]), ("gateb", i["L1_ffn_bg"])):
        rows[:, C_ROW[n], :len(v)] = v

    def table(v, pad):
        out = np.full((P, KEYS // TP, TP), pad, f)
        out[:, :NB, :T] = v[:P, None, None]
        out[:, NB:, :T] = _twice(v)[:, None, None]
        return out.reshape(P, KEYS)

    return {"c_w": _parts(w), "c_wv": wv, "c_rows": rows, "c_decay": table(i["L1_attn_decay"], NEG),
            "c_bonus": table(i["L1_attn_first"], 0.0)}


_SCRATCH = {"rows_b": (ROWS, 2 * D), "mask_b": (P, GROUPS, E_B), "gate_b": (P, GROUPS, E_B), "base": (NT, P, NG, D),
            "slot_rows": (P * BLK_B, D), "gates_b": (P, GROUPS, K_B), "rows_d": (ROWS, 3 * D), "mask_d": (P, GROUPS, E_D)}


def kernel(**inputs):
    import concourse.bacc as _bacc
    from concourse.bass_utils import run_bass_kernel_spmd as _run

    i = {n: np.asarray(a) for n, a in inputs.items()}
    arrays = {}
    for layout in (_layout_a, _layout_b, _layout_c, _layout_d, _layout_routing):
        arrays.update({n: np.ascontiguousarray(a) for n, a in layout(i).items()})
    nc = _bacc.Bacc("TRN2", target_bir_lowering=False, num_devices=1)
    io = {n: nc.dram_tensor(n, a.shape, F32, kind="ExternalInput").ap() for n, a in arrays.items()}
    io.update({n: nc.dram_tensor(n, shape, F32, kind="Internal").ap() for n, shape in _SCRATCH.items()})
    io["slots_b"] = nc.dram_tensor("slots_b", (P, GROUPS, K_B), I32, kind="Internal").ap()
    io["out"] = nc.dram_tensor("out", (ROWS, D), F32, kind="ExternalOutput").ap()
    build(nc, io)
    r = _run(nc, [arrays], core_ids=[0]).results[0]["out"]
    y = r.reshape(B, TP, D)[:, :T]
    out = np.empty((B, T, D), np.float32)
    out[:, :, SPECTRUM] = y
    return out
```
